# Optimizing a Trainium2 kernel written in Bass

```python
import numpy as np
import jax
import jax.numpy as jnp

def _softmax(x, axis=-1):
    return jax.nn.softmax(x, axis=axis)

def _gelu(x):
    return jax.nn.gelu(x, approximate=True)

def _silu(x):
    return jax.nn.silu(x)

def _sigmoid(x):
    return jax.nn.sigmoid(x)

def _layernorm(x, axis=-1, eps=1e-05):
    m = jnp.mean(x, axis=axis, keepdims=True)
    v = jnp.var(x, axis=axis, keepdims=True)
    return (x - m) / jnp.sqrt(v + eps)

def _scatter_add(tgt, idx, src, axis=0):
    return tgt.at[idx].add(src)

def _segment_sum(src, seg, n):
    return jax.ops.segment_sum(src, seg, n)
kernel_name = 'mk_seq_postln_d1_jaxref_r8_74288e'

def setup_inputs(seed: int=0):
    np.random.seed(seed)
    _w = jnp.asarray

    def _L0_attn_setup():
        import jax, jax.numpy as jnp
        import numpy as np
        B, S = (2, 256)
        HIDDEN, MLP = (128, 256)
        N_STATE, DT_RANK, CONV_K = (16, 64, 4)

        def _causal_depthwise_conv(u, conv_w, conv_b):
            u_pad = jnp.pad(u, ((0, 0), (CONV_K - 1, 0), (0, 0)))
            seq = u.shape[1]
            y = sum((u_pad[:, k:k + seq, :] * conv_w[:, k] for k in range(CONV_K)))
            return y + conv_b

        def _selective_scan(u, A_log, x_proj_w, dt_proj_w, dt_proj_b, D_skip):
            xp = u @ x_proj_w
            delta = jax.nn.softplus(xp[..., :DT_RANK] @ dt_proj_w + dt_proj_b)
            Bm = xp[..., DT_RANK:DT_RANK + N_STATE]
            Cm = xp[..., DT_RANK + N_STATE:]
            A = -jnp.exp(A_log)
            dA = jnp.exp(delta[..., None] * A)
            dBu = delta[..., None] * Bm[:, :, None, :] * u[..., None]

            def step(h, inp):
                dA_t, dBu_t, C_t = inp
                h = dA_t * h + dBu_t
                y = jnp.einsum('bdn,bn->bd', h, C_t)
                return (h, y)
            h0 = jnp.zeros((u.shape[0], u.shape[2], N_STATE), u.dtype)
            _, ys = jax.lax.scan(step, h0, (dA.transpose(1, 0, 2, 3), dBu.transpose(1, 0, 2, 3), Cm.transpose(1, 0, 2)))
            return ys.transpose(1, 0, 2) + u * D_skip
        key = jax.random.key(seed)
        ks = jax.random.split(key, 14)
        s = 0.02
        return {'x': jax.random.normal(ks[0], (B, S, HIDDEN), jnp.float32), 'W1': jax.random.normal(ks[1], (HIDDEN, MLP), jnp.float32) * s, 'b1': jnp.zeros((MLP,), jnp.float32), 'W2': jax.random.normal(ks[2], (HIDDEN, MLP), jnp.float32) * s, 'b2': jnp.zeros((MLP,), jnp.float32), 'conv_w': jax.random.normal(ks[3], (MLP, CONV_K), jnp.float32) * s, 'conv_b': jnp.zeros((MLP,), jnp.float32), 'A_log': jnp.log(jnp.broadcast_to(jnp.arange(1, N_STATE + 1, dtype=jnp.float32), (MLP, N_STATE))), 'x_proj_w': jax.random.normal(ks[4], (MLP, DT_RANK + 2 * N_STATE), jnp.float32) * s, 'dt_proj_w': jax.random.normal(ks[5], (DT_RANK, MLP), jnp.float32) * s, 'dt_proj_b': jnp.full((MLP,), -4.0, jnp.float32), 'D_skip': jnp.ones((MLP,), jnp.float32), 'Wo': jax.random.normal(ks[6], (MLP, HIDDEN), jnp.float32) * s, 'bo': jnp.zeros((HIDDEN,), jnp.float32)}
    _L0_attn_in = _L0_attn_setup()

    def _L0_ffn_setup():
        import jax, jax.numpy as jnp
        import numpy as np
        DIM = 128
        DEPTH = 2
        HEADS = 8
        DIM_HEAD = 64
        WINDOW = 64
        INNER = HEADS * DIM_HEAD
        HID = int(DIM * 4 * 2 / 3)
        B, N = (2, 1024)
        QK_SCALE = 8.0

        def shift_token(t):
            t1, t2 = jnp.split(t, 2, axis=-1)
            t2 = jnp.pad(t2, ((0, 0), (1, 0), (0, 0)))[:, :-1]
            return jnp.concatenate([t1, t2], axis=-1)

        def l2norm(t):
            return t / jnp.clip(jnp.linalg.norm(t, axis=-1, keepdims=True), 1e-12)

        def rotate_half(x):
            x1, x2 = jnp.split(x, 2, axis=-1)
            return jnp.concatenate([-x2, x1], axis=-1)

        def rotary_xpos(q, k):
            n = q.shape[-2]
            half_idx = jnp.arange(0, DIM_HEAD, 2, dtype=jnp.float32)
            inv_freq = 1.0 / 10000.0 ** (half_idx / DIM_HEAD)
            t = jnp.arange(n, dtype=jnp.float32)
            freqs = t[:, None] * inv_freq[None, :]
            freqs = jnp.concatenate([freqs, freqs], axis=-1)
            base = (half_idx + 0.4 * DIM_HEAD) / (1.4 * DIM_HEAD)
            power = (t - n // 2) / float(WINDOW // 2)
            scale = base[None, :] ** power[:, None]
            scale = jnp.concatenate([scale, scale], axis=-1)
            cos, sin = (jnp.cos(freqs), jnp.sin(freqs))
            q = q * cos * scale + rotate_half(q) * sin * scale
            k = k * cos / scale + rotate_half(k) * sin / scale
            return (q, k)

        def local_attention(q, k, v):
            b, h, n, d = q.shape
            w = n // WINDOW
            bq = q.reshape(b, h, w, WINDOW, d) * QK_SCALE
            bk = k.reshape(b, h, w, WINDOW, d)
            bv = v.reshape(b, h, w, WINDOW, d)

            def look_around(t):
                p = jnp.pad(t, ((0, 0), (0, 0), (1, 0), (0, 0), (0, 0)))
                return jnp.concatenate([p[:, :, :w], p[:, :, 1:]], axis=3)
            bk, bv = (look_around(bk), look_around(bv))
            bt = jnp.arange(n).reshape(w, WINDOW)
            btp = jnp.pad(bt, ((1, 0), (0, 0)), constant_values=-1)
            btk = jnp.concatenate([btp[:w], btp[1:]], axis=1)
            sim = jnp.einsum('bhwid,bhwjd->bhwij', bq, bk)
            i = bt[:, :, None]
            j = btk[:, None, :]
            mask = (i < j) | (i > j + WINDOW) | (j == -1)
            sim = jnp.where(mask, -jnp.finfo(sim.dtype).max, sim)
            attn = jax.nn.softmax(sim, axis=-1)
            out = jnp.einsum('bhwij,bhwjd->bhwid', attn, bv)
            return out.reshape(b, h, n, d)

        def _layer(x, wqkv, qs, ksc, wo, lg, lb, w1, b1, w2, b2):
            b, n, _ = x.shape
            h = shift_token(x)
            qkv = h @ wqkv
            q, k, v = jnp.split(qkv, 3, axis=-1)
            to_heads = lambda t: t.reshape(b, n, HEADS, DIM_HEAD).transpose(0, 2, 1, 3)
            q, k, v = (to_heads(q), to_heads(k), to_heads(v))
            q = l2norm(q) * qs
            k = l2norm(k) * ksc
            q, k = rotary_xpos(q, k)
            o = local_attention(q, k, v)
            o = o.transpose(0, 2, 1, 3).reshape(b, n, INNER)
            x = x + o @ wo
            h = shift_token(x)
            mu = h.mean(-1, keepdims=True)
            var = h.var(-1, keepdims=True)
            h = (h - mu) / jnp.sqrt(var + 1e-05) * lg + lb
            h = h @ w1 + b1
            a, g = jnp.split(h, 2, axis=-1)
            h = a * jax.nn.gelu(g, approximate=False)
            x = x + h @ w2 + b2
            return x
        key = jax.random.key(seed)
        ks = jax.random.split(key, 6)
        return {'x': jax.random.normal(ks[0], (B, N, DIM), jnp.float32), 'wqkv': jax.random.normal(ks[1], (DEPTH, DIM, 3 * INNER), jnp.float32) * 0.02, 'q_scale': jnp.ones((DEPTH, DIM_HEAD), jnp.float32), 'k_scale': jnp.ones((DEPTH, DIM_HEAD), jnp.float32), 'wo': jax.random.normal(ks[2], (DEPTH, INNER, DIM), jnp.float32) * 0.02, 'ln_g': jnp.ones((DEPTH, DIM), jnp.float32), 'ln_b': jnp.zeros((DEPTH, DIM), jnp.float32), 'w1': jax.random.normal(ks[3], (DEPTH, DIM, 2 * HID), jnp.float32) * 0.02, 'b1': jnp.zeros((DEPTH, 2 * HID), jnp.float32), 'w2': jax.random.normal(ks[4], (DEPTH, HID, DIM), jnp.float32) * 0.02, 'b2': jnp.zeros((DEPTH, DIM), jnp.float32)}
    _L0_ffn_in = _L0_ffn_setup()
    _d = {'L0_attn_x': _L0_attn_in['x'], 'L0_attn_W1': _L0_attn_in['W1'], 'L0_attn_b1': _L0_attn_in['b1'], 'L0_attn_W2': _L0_attn_in['W2'], 'L0_attn_b2': _L0_attn_in['b2'], 'L0_attn_conv_w': _L0_attn_in['conv_w'], 'L0_attn_conv_b': _L0_attn_in['conv_b'], 'L0_attn_A_log': _L0_attn_in['A_log'], 'L0_attn_x_proj_w': _L0_attn_in['x_proj_w'], 'L0_attn_dt_proj_w': _L0_attn_in['dt_proj_w'], 'L0_attn_dt_proj_b': _L0_attn_in['dt_proj_b'], 'L0_attn_D_skip': _L0_attn_in['D_skip'], 'L0_attn_Wo': _L0_attn_in['Wo'], 'L0_attn_bo': _L0_attn_in['bo'], 'L0_ffn_wqkv': _L0_ffn_in['wqkv'], 'L0_ffn_q_scale': _L0_ffn_in['q_scale'], 'L0_ffn_k_scale': _L0_ffn_in['k_scale'], 'L0_ffn_wo': _L0_ffn_in['wo'], 'L0_ffn_ln_g': _L0_ffn_in['ln_g'], 'L0_ffn_ln_b': _L0_ffn_in['ln_b'], 'L0_ffn_w1': _L0_ffn_in['w1'], 'L0_ffn_b1': _L0_ffn_in['b1'], 'L0_ffn_w2': _L0_ffn_in['w2'], 'L0_ffn_b2': _L0_ffn_in['b2']}
    _x0 = _d['L0_attn_x']
    _d['L0_attn_x'] = jax.random.normal(jax.random.fold_in(jax.random.key(seed), 1), (16, 256, 128), dtype=_x0.dtype)
    del _x0
    return _d

def reference(L0_attn_x, L0_attn_W1, L0_attn_b1, L0_attn_W2, L0_attn_b2, L0_attn_conv_w, L0_attn_conv_b, L0_attn_A_log, L0_attn_x_proj_w, L0_attn_dt_proj_w, L0_attn_dt_proj_b, L0_attn_D_skip, L0_attn_Wo, L0_attn_bo, L0_ffn_wqkv, L0_ffn_q_scale, L0_ffn_k_scale, L0_ffn_wo, L0_ffn_ln_g, L0_ffn_ln_b, L0_ffn_w1, L0_ffn_b1, L0_ffn_w2, L0_ffn_b2):

    def _L0_attn_ref(x, W1, b1, W2, b2, conv_w, conv_b, A_log, x_proj_w, dt_proj_w, dt_proj_b, D_skip, Wo, bo):
        import jax, jax.numpy as jnp
        import numpy as np
        B, S = (2, 256)
        HIDDEN, MLP = (128, 256)
        N_STATE, DT_RANK, CONV_K = (16, 64, 4)

        def _causal_depthwise_conv(u, conv_w, conv_b):
            u_pad = jnp.pad(u, ((0, 0), (CONV_K - 1, 0), (0, 0)))
            seq = u.shape[1]
            y = sum((u_pad[:, k:k + seq, :] * conv_w[:, k] for k in range(CONV_K)))
            return y + conv_b

        def _selective_scan(u, A_log, x_proj_w, dt_proj_w, dt_proj_b, D_skip):
            xp = u @ x_proj_w
            delta = jax.nn.softplus(xp[..., :DT_RANK] @ dt_proj_w + dt_proj_b)
            Bm = xp[..., DT_RANK:DT_RANK + N_STATE]
            Cm = xp[..., DT_RANK + N_STATE:]
            A = -jnp.exp(A_log)
            dA = jnp.exp(delta[..., None] * A)
            dBu = delta[..., None] * Bm[:, :, None, :] * u[..., None]

            def step(h, inp):
                dA_t, dBu_t, C_t = inp
                h = dA_t * h + dBu_t
                y = jnp.einsum('bdn,bn->bd', h, C_t)
                return (h, y)
            h0 = jnp.zeros((u.shape[0], u.shape[2], N_STATE), u.dtype)
            _, ys = jax.lax.scan(step, h0, (dA.transpose(1, 0, 2, 3), dBu.transpose(1, 0, 2, 3), Cm.transpose(1, 0, 2)))
            return ys.transpose(1, 0, 2) + u * D_skip
        gate = jax.nn.sigmoid(x @ W2 + b2)
        u = x @ W1 + b1
        u = jax.nn.sigmoid(_causal_depthwise_conv(u, conv_w, conv_b))
        y = _selective_scan(u, A_log, x_proj_w, dt_proj_w, dt_proj_b, D_skip)
        return y * gate @ Wo + bo

    def _L0_ffn_ref(x, wqkv, q_scale, k_scale, wo, ln_g, ln_b, w1, b1, w2, b2):
        import jax, jax.numpy as jnp
        import numpy as np
        DIM = 128
        DEPTH = 2
        HEADS = 8
        DIM_HEAD = 64
        WINDOW = 64
        INNER = HEADS * DIM_HEAD
        HID = int(DIM * 4 * 2 / 3)
        B, N = (2, 1024)
        QK_SCALE = 8.0

        def shift_token(t):
            t1, t2 = jnp.split(t, 2, axis=-1)
            t2 = jnp.pad(t2, ((0, 0), (1, 0), (0, 0)))[:, :-1]
            return jnp.concatenate([t1, t2], axis=-1)

        def l2norm(t):
            return t / jnp.clip(jnp.linalg.norm(t, axis=-1, keepdims=True), 1e-12)

        def rotate_half(x):
            x1, x2 = jnp.split(x, 2, axis=-1)
            return jnp.concatenate([-x2, x1], axis=-1)

        def rotary_xpos(q, k):
            n = q.shape[-2]
            half_idx = jnp.arange(0, DIM_HEAD, 2, dtype=jnp.float32)
            inv_freq = 1.0 / 10000.0 ** (half_idx / DIM_HEAD)
            t = jnp.arange(n, dtype=jnp.float32)
            freqs = t[:, None] * inv_freq[None, :]
            freqs = jnp.concatenate([freqs, freqs], axis=-1)
            base = (half_idx + 0.4 * DIM_HEAD) / (1.4 * DIM_HEAD)
            power = (t - n // 2) / float(WINDOW // 2)
            scale = base[None, :] ** power[:, None]
            scale = jnp.concatenate([scale, scale], axis=-1)
            cos, sin = (jnp.cos(freqs), jnp.sin(freqs))
            q = q * cos * scale + rotate_half(q) * sin * scale
            k = k * cos / scale + rotate_half(k) * sin / scale
            return (q, k)

        def local_attention(q, k, v):
            b, h, n, d = q.shape
            w = n // WINDOW
            bq = q.reshape(b, h, w, WINDOW, d) * QK_SCALE
            bk = k.reshape(b, h, w, WINDOW, d)
            bv = v.reshape(b, h, w, WINDOW, d)

            def look_around(t):
                p = jnp.pad(t, ((0, 0), (0, 0), (1, 0), (0, 0), (0, 0)))
                return jnp.concatenate([p[:, :, :w], p[:, :, 1:]], axis=3)
            bk, bv = (look_around(bk), look_around(bv))
            bt = jnp.arange(n).reshape(w, WINDOW)
            btp = jnp.pad(bt, ((1, 0), (0, 0)), constant_values=-1)
            btk = jnp.concatenate([btp[:w], btp[1:]], axis=1)
            sim = jnp.einsum('bhwid,bhwjd->bhwij', bq, bk)
            i = bt[:, :, None]
            j = btk[:, None, :]
            mask = (i < j) | (i > j + WINDOW) | (j == -1)
            sim = jnp.where(mask, -jnp.finfo(sim.dtype).max, sim)
            attn = jax.nn.softmax(sim, axis=-1)
            out = jnp.einsum('bhwij,bhwjd->bhwid', attn, bv)
            return out.reshape(b, h, n, d)

        def _layer(x, wqkv, qs, ksc, wo, lg, lb, w1, b1, w2, b2):
            b, n, _ = x.shape
            h = shift_token(x)
            qkv = h @ wqkv
            q, k, v = jnp.split(qkv, 3, axis=-1)
            to_heads = lambda t: t.reshape(b, n, HEADS, DIM_HEAD).transpose(0, 2, 1, 3)
            q, k, v = (to_heads(q), to_heads(k), to_heads(v))
            q = l2norm(q) * qs
            k = l2norm(k) * ksc
            q, k = rotary_xpos(q, k)
            o = local_attention(q, k, v)
            o = o.transpose(0, 2, 1, 3).reshape(b, n, INNER)
            x = x + o @ wo
            h = shift_token(x)
            mu = h.mean(-1, keepdims=True)
            var = h.var(-1, keepdims=True)
            h = (h - mu) / jnp.sqrt(var + 1e-05) * lg + lb
            h = h @ w1 + b1
            a, g = jnp.split(h, 2, axis=-1)
            h = a * jax.nn.gelu(g, approximate=False)
            x = x + h @ w2 + b2
            return x
        for l in range(DEPTH):
            x = _layer(x, wqkv[l], q_scale[l], k_scale[l], wo[l], ln_g[l], ln_b[l], w1[l], b1[l], w2[l], b2[l])
        return x
    x = L0_attn_x
    x = _layernorm(x + _L0_attn_ref(x, L0_attn_W1, L0_attn_b1, L0_attn_W2, L0_attn_b2, L0_attn_conv_w, L0_attn_conv_b, L0_attn_A_log, L0_attn_x_proj_w, L0_attn_dt_proj_w, L0_attn_dt_proj_b, L0_attn_D_skip, L0_attn_Wo, L0_attn_bo), axis=-1)
    x = _layernorm(x + _L0_ffn_ref(x, L0_ffn_wqkv, L0_ffn_q_scale, L0_ffn_k_scale, L0_ffn_wo, L0_ffn_ln_g, L0_ffn_ln_b, L0_ffn_w1, L0_ffn_b1, L0_ffn_w2, L0_ffn_b2), axis=-1)
    return x

_drawn_inputs = setup_inputs


def setup_inputs(seed=0):
    import zlib

    import numpy as np

    out = dict(_drawn_inputs(seed))
    spreads = {'L0_attn_b1': (0.0, 0.8),
     'L0_attn_b2': (0.0, 0.8),
     'L0_attn_conv_b': (0.0, 0.8),
     'L0_attn_dt_proj_b': (-4.0, 0.6),
     'L0_attn_D_skip': (1.0, 0.6),
     'L0_attn_bo': (0.0, 0.1),
     'L0_ffn_q_scale': (1.0, 0.6),
     'L0_ffn_k_scale': (1.0, 0.6),
     'L0_ffn_ln_g': (1.0, 0.6),
     'L0_ffn_ln_b': (0.0, 0.8),
     'L0_ffn_b1': (0.0, 0.8),
     'L0_ffn_b2': (0.0, 0.447)}
    factors = {'L0_attn_W1': 8.0,
     'L0_attn_W2': 5.746,
     'L0_attn_conv_w': 8.0,
     'L0_attn_A_log': 8.0,
     'L0_attn_x_proj_w': 8.0,
     'L0_attn_dt_proj_w': 8.0,
     'L0_ffn_wqkv': 3.08,
     'L0_ffn_wo': 3.025,
     'L0_ffn_w1': 6.215,
     'L0_ffn_w2': 6.145}
    for name, (base, spread) in spreads.items():
        noise = np.random.default_rng([zlib.crc32(name.encode()), seed]).standard_normal(out[name].shape)
        drawn = base * np.exp(spread * noise) if base else spread * noise
        out[name] = jnp.asarray(drawn.astype(out[name].dtype))
    for name, factor in factors.items():
        out[name] = (out[name] * factor).astype(out[name].dtype)
    return out
```

```python
import numpy as np
import concourse.bass as bass
from concourse import mybir
from contextlib import ExitStack

F32 = mybir.dt.float32
BF16 = mybir.dt.bfloat16
ALU = mybir.AluOpType
ACT = mybir.ActivationFunctionType
AX = mybir.AxisListType


def below(v, k):
    return isinstance(v, int) and v < k


def build(nc, a, out):
    NSEQ, S, D = a["L0_attn_x"].shape
    CH = a["L0_attn_W1"].shape[1]
    NH = CH // 128
    NST = a["L0_attn_A_log"].shape[1]
    RANK = a["L0_attn_dt_proj_w"].shape[0]
    PAIRS = NSEQ // 2
    T = 2 * S
    NG = NST // 2
    XB = T // 128
    BC = 2 * NST
    EPS = 1e-5
    DEPTH, _, HID = a["L0_ffn_w2"].shape[0], 0, a["L0_ffn_w2"].shape[1]
    HD = a["L0_ffn_q_scale"].shape[1]
    INNER = a["L0_ffn_wo"].shape[1]
    HEADS = INNER // HD
    HP = HEADS // 2
    NC = -(-HID // 128)
    CW = [min(128, HID - 128 * c) for c in range(NC)]
    TILES = PAIRS * XB

    ctx = ExitStack()
    with ctx:
        def sb(name, shape, dt=F32):
            return ctx.enter_context(nc.sbuf_tensor(name, shape, dt))

        def ps(name, shape, dt=F32):
            return ctx.enter_context(nc.psum_tensor(name, shape, dt))

        def sem(name):
            return ctx.enter_context(nc.semaphore(name))

        ident = sb("ident", [128, 128])
        ones_mean = sb("ones_mean", [128, 128])
        onehot_src = sb("onehot_src", [3 * BC, BC])
        onehot = sb("onehot", [3 * BC, BC, 128], BF16)
        w1 = sb("w1", [128, CH])
        w2 = sb("w2", [128, CH])
        wx = sb("wx", [128, NH, RANK + BC])
        wbc3 = sb("wbc3", [128, NH, 3, BC])
        wdt = sb("wdt", [RANK, CH])
        wo = sb("wo", [128, NH, D])
        b1 = sb("b1", [128, NH])
        nb2 = sb("nb2", [128, NH])
        bdt = sb("bdt", [128, NH])
        cw = sb("cw", [128, NH, 4])
        cb = sb("cb", [128, NH])
        nA = sb("nA", [128, NH, NST])
        dsk = sb("dsk", [128, NH])
        bo = sb("bo", [128, 1])
        diagD = sb("diagD", [128, NH, 128])

        xT = sb("xT", [128, NSEQ, S + 1])
        eps = sb("eps", [128, 1])
        one = sb("one", [128, 1])
        held = sb("held", [128, 1])

        identb = sb("identb", [128, 128], BF16)
        maskf = sb("maskf", [128, 2, 128])
        maskb = sb("maskb", [128, 2, 4, 128], BF16)
        rot_c = sb("rot_c", [128, 2, 2, HD])
        rot_s = sb("rot_s", [128, 2, 2, HD])
        mhalf = sb("mhalf", [128, 2 * HEADS])
        F = []
        for l in range(DEPTH):
            F.append(dict(
                wqkv=sb(f"wqkv{l}", [128, 3 * INNER]), wo=sb(f"wof{l}", [128, INNER // 128, D]),
                w1=sb(f"w1f{l}", [128, 2 * HID]), w2=sb(f"w2f{l}", [128, NC, D]),
                lg=sb(f"lg{l}", [128, 1]), lb=sb(f"lb{l}", [128, 1]), b1=sb(f"b1f{l}", [128, 2 * NC]),
                b2=sb(f"b2f{l}", [128, 1]), qk_scale=sb(f"qks{l}", [128, 2, HD]),
                tc=sb(f"tc{l}", [128, 2, 2, HD]), ts=sb(f"ts{l}", [128, 2, 2, HD])))

        mscope = ExitStack()

        def msb(name, shape, dt=F32):
            return mscope.enter_context(nc.sbuf_tensor(name, shape, dt))

        def mps(name, shape, dt=F32):
            return mscope.enter_context(nc.psum_tensor(name, shape, dt))

        xin = msb("xin", [128, XB, D])
        ub = msb("ub", [128, NH, 2, S + 3])
        uacc = msb("uacc", [128, NH, 2, S])
        u = msb("u", [128, NH, 2, S])
        xdt = msb("xdt", [RANK, T])
        bc_f = msb("bc_f", [3 * BC, T])
        bc_r = msb("bc_r", [3 * BC, T])
        bc_t = msb("bc_t", [3 * BC, T], BF16)
        third = msb("third", [3 * BC, 2])
        bc_s = msb("bc_s", [3 * BC, T], BF16)
        sp_m = msb("sp_m", [128, NH, T])
        sp_l = msb("sp_l", [128, NH, T])
        delta = msb("delta", [128, NH, 2, S])
        du = msb("du", [128, NH * T])
        gate = msb("gate", [128, NH, T])
        yg = msb("yg", [128, NH, T])
        NDA, NHB = 2, 4
        dA = [msb(f"dA{k}", [128, 2, NH, 2, S]) for k in range(NDA)]
        hb = [msb(f"hb{k}", [128, 2, NH, T]) for k in range(NHB)]
        hc = [msb(f"hc{k}", [128, 2, NH, T]) for k in range(2)]
        csb = msb("csb", [128, 2, 2, T])
        rb = msb("rb", [128, T])
        rc = msb("rc", [128, T])
        rsq = msb("rsq", [128, T])
        rstd = msb("rstd", [128, T])
        pB = mps("pB", [128, 2, T])
        pC = mps("pC", [128, 2, T])
        pY = mps("pY", [128, NH, T])
        pW = mps("pW", [128, 2, T])
        mscope.close()

        fscope = ExitStack()

        def fsb(name, shape, dt=F32):
            return fscope.enter_context(nc.sbuf_tensor(name, shape, dt))

        def fps(scope, name, shape, dt=F32):
            return scope.enter_context(nc.psum_tensor(name, shape, dt))

        x0T = fsb("x0T", [128, NSEQ, S])
        hT = fsb("hT", [128, XB, 128])
        t1 = fsb("t1", [128, 2, INNER])
        t2 = fsb("t2", [128, 2, INNER])
        qk_sq = fsb("qk_sq", [128, 2, INNER])
        ss = fsb("ss", [128, 2 * HEADS])
        ssc = fsb("ssc", [128, 2 * HEADS])
        rn = [fsb(f"rn{k}", [128, 2 * HEADS]) for k in range(2)]
        qk = fsb("qk", [128, 2, INNER])
        qkT = [fsb(f"qkT{k}", [128, 2, HP, 128]) for k in range(2)]
        V = [fsb(f"V{k}", [128, INNER]) for k in range(XB)]
        Vm = [fsb(f"Vm{k}", [128, INNER]) for k in range(XB)]
        mx = fsb("mx", [128, HEADS])
        sc8 = fsb("sc8", [128, HEADS])
        nb = fsb("nb", [128, HEADS])
        psums = fsb("psums", [128, HEADS])
        rs = fsb("rs", [128, HEADS])
        P = [fsb(f"P{k}", [128, HEADS, 128]) for k in range(2)]
        PT = fsb("PT", [128, HEADS, 128])
        oT = fsb("oT", [128, HP, T])
        hn = fsb("hn", [128, PAIRS, T])
        gl = fsb("gl", [128, NC, T])
        mm_ = fsb("mm_", [128, NC, T])
        lin_b = [fsb(f"lin_b{k}", [128, T]) for k in range(2)]
        lc_b = [fsb(f"lc_b{k}", [128, T]) for k in range(2)]
        lsq_b = [fsb(f"lsq_b{k}", [128, T]) for k in range(2)]
        lr_b = [fsb(f"lr_b{k}", [128, T]) for k in range(2)]
        foT = [fsb(f"foT{k}", [128, T]) for k in range(2)]
        fout = [fsb(f"fout{k}", [128, XB, D]) for k in range(2)]
        fscope.close()
        s1 = ExitStack()
        pA = fps(s1, "pA", [128, 2, INNER])
        pT = fps(s1, "pT", [128, 2, INNER])
        pS = fps(s1, "pS", [128, 2, HP, 128])
        pV = fps(s1, "pV", [128, INNER])
        pE = fps(s1, "pE", [128, T])
        s1.close()
        pG = fps(s1, "pG", [128, NC, T])
        pU = fps(s1, "pU", [128, NC, T])
        pO = fps(s1, "pO", [128, T])
        pb1 = fps(s1, "pb1", [128, T])
        s1.close()
        pLm = fps(s1, "pLm", [128, 2, T])
        pLv = fps(s1, "pLv", [128, 2, T])
        pLt = fps(s1, "pLt", [128, 2, T])
        s1.close()

        ffn_loaded = sem("ffn_loaded")
        tabs = sem("tabs")
        x0_saved = sem("x0_saved")
        ATT = [{n: sem(f"{n}{l}") for n in """ht qk_ps v_ps rot sqd ssr ssd rnd addd qkd tps qk_ev simd mxr mxs mxd expd rsd pnorm
            ptp pt_ev v_ev pvd o_ev wod xud""".split()} for l in range(DEPTH)]
        LNS = [{n: sem(f"{n}{l}") for n in "lin lmean lcent lsq lvar lrl lrstd lnorm ltp lev lst".split()} for l in range(DEPTH + 1)]
        FF = [{n: sem(f"f{n}{l}") for n in "b1p b1d g u ge m o x".split()} for l in range(DEPTH)]
        a_exp = sem("a_exp")
        b_ready = sem("b_ready")
        bc_f_done = sem("bc_f_done")
        bc_ps = sem("bc_ps")
        bc_split = sem("bc_split")
        tapped = sem("tapped")
        part = sem("part")
        c_ev = sem("c_ev")
        c_ready = sem("c_ready")
        cent = sem("cent")
        consts_p = sem("consts_p")
        consts_v = sem("consts_v")
        da_ready = sem("da_ready")
        dbu = sem("dbu")
        delta_done = sem("delta_done")
        dt_ps = sem("dt_ps")
        du_done = sem("du_done")
        gate_done = sem("gate_done")
        gate_e = sem("gate_e")
        gate_l = sem("gate_l")
        gate_ps = sem("gate_ps")
        hc_pool = sem("hc_pool")
        hc_dve = sem("hc_dve")
        mean_ps = sem("mean_ps")
        resid = sem("resid")
        rstd_done = sem("rstd_done")
        rstd_l = sem("rstd_l")
        scan = sem("scan")
        sig_e = sem("sig_e")
        sig_l = sem("sig_l")
        sp_a = sem("sp_a")
        sp_done = sem("sp_done")
        sp_e = sem("sp_e")
        sq = sem("sq")
        stored = [sem(f"stored{q}") for q in range(2)]
        u_b = sem("u_b")
        u_conv = sem("u_conv")
        u_ps = sem("u_ps")
        u_sig = sem("u_sig")
        var_ps = sem("var_ps")
        weights = sem("weights")
        wo_ps = sem("wo_ps")
        x_done = sem("x_done")
        x_in = sem("x_in")
        x_t = sem("x_t")
        xdt_done = sem("xdt_done")
        xdt_ps = sem("xdt_ps")
        xt_ps = sem("xt_ps")
        y_init = sem("y_init")
        yg_done = sem("yg_done")
        ysum = sem("ysum")
        load_list = [
            (ident[:], a["c_ident"]), (onehot_src[:], a["c_onehot"]), (third[:], a["c_third"]),
            (w1[:], a["L0_attn_W1"]), (w2[:], a["L0_attn_W2"]),
            (wx[:], a["L0_attn_x_proj_w"].rearrange("(c p) n -> p c n", p=128)),
            (wdt[:], a["L0_attn_dt_proj_w"]),
            (wo[:], a["L0_attn_Wo"].rearrange("(c p) n -> p c n", p=128)),
            (b1[:], a["L0_attn_b1"]),
            (nb2[:], a["L0_attn_b2"]),
            (bdt[:], a["L0_attn_dt_proj_b"]),
            (cb[:], a["L0_attn_conv_b"]),
            (cw[:], a["L0_attn_conv_w"].rearrange("(c p) k -> p c k", p=128)),
            (nA[:], a["L0_attn_A_log"].rearrange("(c p) k -> p c k", p=128)),
            (dsk[:], a["L0_attn_D_skip"]),
            (bo[:], a["L0_attn_bo"]),
        ]
        LOADED = 16 * len(load_list)
        ffn_list = [(maskf[:], a["c_mask"]), (rot_c[:], a["c_rot_c"]), (rot_s[:], a["c_rot_s"])]
        for l in range(DEPTH):
            f = F[l]
            ffn_list += [
                (f["wqkv"][:], a["L0_ffn_wqkv"][l]),
                (f["wo"][:], a["L0_ffn_wo"][l].rearrange("(c p) n -> p c n", p=128)),
                (f["w1"][:], a["L0_ffn_w1"][l]),
                (f["w2"][:, 0:NC - 1, :], a["L0_ffn_w2"][l, 0:128 * (NC - 1), :].rearrange("(c p) n -> p c n", p=128)),
                (f["w2"][0:CW[-1], NC - 1, :], a["L0_ffn_w2"][l, 128 * (NC - 1):HID, :]),
                (f["lg"][:], a["L0_ffn_ln_g"][l]), (f["lb"][:], a["L0_ffn_ln_b"][l]), (f["b2"][:], a["L0_ffn_b2"][l]),
                (f["b1"][:], a["L0_ffn_b1"][l]),
                (f["qk_scale"][:, 0, :], a["L0_ffn_q_scale"][l].partition_broadcast(128)),
                (f["qk_scale"][:, 1, :], a["L0_ffn_k_scale"][l].partition_broadcast(128)),
            ]
        FFN_LOADED = 16 * len(ffn_list)

        ON_DVE = ()
        ON_POOL = tuple(g for g in range(NG) if g not in ON_DVE)

        def wait_group(eng, on_pool, on_dve, i, g):
            if g < 0:
                i, g = i - 1, g + NG
            if below(i, 0):
                return
            mine, sem_ = (ON_DVE, on_dve) if g in ON_DVE else (ON_POOL, on_pool)
            eng.wait_ge(sem_, len(mine) * i + sum(x <= g for x in mine))

        def xs(i):
            return xT[:, bass.ds(2 * i, 2), 1:S + 1]

        def seqs(ap):
            return ap.rearrange("p (s t) -> p s t", s=2)

        block = ctx.enter_context(nc.Block())

        def pairs(eng, step):
            step(0, True, False)
            with eng.Fori(1, PAIRS - 1) as i:
                step(i, False, False)
            step(PAIRS - 1, False, True)

        def halves(eng, both):
            both(0, True)
            with eng.Fori(1, PAIRS // 2) as i:
                both(i, False)

        @block.sync
        def _(sp):
            for dst, src in load_list:
                sp.dma_start(dst, src).then_inc(weights, 16)
            x_pairs = a["L0_attn_x"].rearrange("(i s) (b p) d -> i p (s b) d", s=2, p=128)
            sp.dma_start(xin[:], x_pairs[0]).then_inc(x_in, 16)
            for dst, src in ffn_list:
                sp.dma_start(dst, src).then_inc(ffn_loaded, 16)
            with sp.Fori(1, PAIRS) as i:
                sp.wait_ge(xt_ps, i)
                sp.dma_start(xin[:], x_pairs[i]).then_inc(x_in, 16)
            L = LNS[DEPTH]
            o_pairs = out.rearrange("(i s) (b p) d -> i p (s b) d", s=2, p=128)

            def store(n, q):
                sp.wait_ge(L["lev"], n + 1)
                sp.dma_start(o_pairs[n], fout[q][:]).then_inc(stored[q], 16)

            with sp.Fori(0, PAIRS // 2) as i:
                store(2 * i, 0)
                store(2 * i + 1, 1)
            for q in range(2):
                sp.wait_ge(stored[q], 16 * (PAIRS // 2))

        @block.tensor
        def _(pe):
            pe.wait_ge(weights, LOADED)
            pe.wait_ge(consts_v, 1)
            pe.wait_ge(consts_p, 1)

            def transposes(n):
                pe.wait_ge(x_in, 16 * (n + 1))
                for b in range(XB):
                    mm = nc.tensor.transpose(pW[:, 0, 128 * b:128 * b + 128], xin[:, b, :], ident[:])
                mm.then_inc(xt_ps, 1)

            def u_rows(n):
                pe.wait_ge(x_t, n + 1)
                for h in range(NH):
                    mm = nc.tensor.matmul(pW[:, h, :], w1[:, 128 * h:128 * h + 128], xs(n), start=True, stop=True)
                mm.then_inc(u_ps, 1)

            def out_rows(n):
                pe.wait_ge(yg_done, n + 1)
                for h in range(NH):
                    mm = nc.tensor.matmul(pW[:, 0, :], wo[:, h, :], yg[:, h, :], start=(h == 0), stop=(h == NH - 1))
                mm.then_inc(wo_ps, 1)

            def bc_rows(n):
                pe.wait_ge(sp_a, n + 1)
                for h in range(NH):
                    mm = nc.tensor.matmul(pW[0:3 * BC, 0, :], wbc3[:, h, :, :].rearrange("p k n -> p (k n)"),
                                          u[:, h, :, :].rearrange("p s t -> p (s t)"), start=(h == 0), stop=(h == NH - 1))
                mm.then_inc(bc_ps, 1)

            def xdt_rows(n):
                pe.wait_ge(u_sig, n + 1)
                for h in range(NH):
                    mm = nc.tensor.matmul(pW[0:RANK, 1, :], wx[:, h, 0:RANK],
                                          u[:, h, :, :].rearrange("p s t -> p (s t)"), start=(h == 0), stop=(h == NH - 1))
                mm.then_inc(xdt_ps, 1)

            def dt_rows(n):
                pe.wait_ge(xdt_done, n + 1)
                for h in range(NH):
                    mm = nc.tensor.matmul(pW[:, h, :], wdt[:, 128 * h:128 * h + 128], xdt[:], start=True, stop=True)
                mm.then_inc(dt_ps, 1)

            def gate_rows(n):
                for h in range(NH):
                    mm = nc.tensor.matmul(pW[:, h, :], w2[:, 128 * h:128 * h + 128], xs(n), start=True, stop=True)
                mm.then_inc(gate_ps, 1)

            def b_rows(n, g, i0):
                if g == 0:
                    pe.wait_ge(bc_split, n + 1)
                if not below(i0 + g, 1):
                    pe.wait_ge(dbu, i0 + g)
                for k in range(2):
                    mm = nc.tensor.matmul(pB[:, k, :], onehot[:, 2 * g + k, :], bc_s[:], start=True, stop=True)
                mm.then_inc(b_ready, 1)
                wait_group(pe, c_ev, hc_dve, n, g - 1)
                for k in range(2):
                    mm = nc.tensor.matmul(pC[:, k, :], onehot[:, NST + 2 * g + k, :], bc_s[:], start=True, stop=True)
                mm.then_inc(c_ready, 1)

            def sum_states(i, g):
                wait_group(pe, hc_pool, hc_dve, i, g)
                for k in range(2):
                    for h in range(NH):
                        mm = nc.tensor.matmul(pY[:, h, :], ident[:], hc[g % 2][:, k, h, :], start=False,
                                              stop=(g == NG - 1 and k == 1), skip_group_check=True)
                mm.then_inc(ysum, 1)

            def variance_rows(n):
                pe.wait_ge(sq, n + 1)
                nc.tensor.matmul(pW[:, 1, :], ones_mean[:], rsq[:], start=True, stop=True).then_inc(var_ps, 1)

            def mean_rows(n):
                pe.wait_ge(resid, n + 1)
                nc.tensor.matmul(pW[:, 0, :], ones_mean[:], rb[:], start=True, stop=True).then_inc(mean_ps, 1)

            def step(i, first, last):
                for g in range(NG):
                    if g < NG - 1:
                        b_rows(i, g + 1, NG * i)
                    if g == 0 and not last:
                        if first:
                            pe.wait_ge(bc_f_done, 1)
                        else:
                            pe.wait_ge(gate_e, i)
                        transposes(i + 1)
                    if g == 1 and not last:
                        u_rows(i + 1)
                    if g == 2 and not first:
                        if not last:
                            pe.wait_ge(u_b, i + 2)
                        else:
                            pe.wait_ge(gate_e, i)
                        out_rows(i - 1)
                    if g == 3:
                        if not first:
                            mean_rows(i - 1)
                    if g == 4 and not last:
                        xdt_rows(i + 1)
                    if g == 5 and not last:
                        if not first:
                            pe.wait_ge(cent, i)
                        dt_rows(i + 1)
                    if g == 6:
                        if not last:
                            bc_rows(i + 1)
                        if not first:
                            variance_rows(i - 1)
                    if g == 7:
                        if not last:
                            pe.wait_ge(bc_f_done, i + 2)
                        if not first:
                            pe.wait_ge(rstd_done, i)
                        gate_rows(i)
                        if not last:
                            b_rows(i + 1, 0, NG * (i + 1))
                    if g == 0 and not first:
                        sum_states(i - 1, NG - 1)
                    if g == 1:
                        if not first:
                            pe.wait_ge(yg_done, i)
                        for h in range(NH):
                            mm = nc.tensor.matmul(pY[:, h, :], diagD[:, h, :], u[:, h, :, :].rearrange("p s t -> p (s t)"),
                                                  start=True, stop=False, skip_group_check=True)
                        mm.then_inc(y_init, 1)
                    if g > 0:
                        sum_states(i, g - 1)

            transposes(0)
            u_rows(0)
            pe.wait_ge(u_b, 1)
            xdt_rows(0)
            dt_rows(0)
            bc_rows(0)
            b_rows(0, 0, 0)
            pairs(pe, step)
            sum_states(PAIRS - 1, NG - 1)
            pe.wait_ge(gate_e, PAIRS)
            out_rows(PAIRS - 1)
            mean_rows(PAIRS - 1)
            variance_rows(PAIRS - 1)
            pe.wait_ge(x_done, PAIRS)
            pe.wait_ge(ffn_loaded, FFN_LOADED)
            pe.wait_ge(tabs, 1)

            def attention(l):
                A, f = ATT[l], F[l]

                def qkv(t, j):
                    pe.wait_ge(A["ht"], t + 1)
                    if not below(t, 1):
                        pe.wait_ge(A["rot"], t)
                        pe.wait_ge(A["sqd"], t)
                    for c in range(2):
                        mm = nc.tensor.matmul(pA[:, c, :], hT[:, j, :], f["wqkv"][:, INNER * c:INNER * (c + 1)],
                                              start=True, stop=True)
                    mm.then_inc(A["qk_ps"], 1)
                    if not below(t, 1):
                        pe.wait_ge(A["v_ev"], t)
                    nc.tensor.matmul(pV[:], hT[:, j, :], f["wqkv"][:, 2 * INNER:3 * INNER],
                                     start=True, stop=True).then_inc(A["v_ps"], 1)

                def turn_qk(t):
                    pe.wait_ge(A["qkd"], t + 1)
                    if not below(t, 2):
                        pe.wait_ge(A["pt_ev"], t - 1)
                    elif not below(t, 1):
                        pe.wait_ge(A["qk_ev"], t)
                    for c in range(2):
                        for hp in range(HP):
                            mm = nc.tensor.transpose(pT[:, c, 128 * hp:128 * hp + 128], qk[:, c, 128 * hp:128 * hp + 128],
                                                     ident[:])
                    mm.then_inc(A["tps"], 1)

                def sims(t, j):
                    pe.wait_ge(A["qk_ev"], t + 1)
                    if not below(t, 1):
                        pe.wait_ge(A["expd"], t)
                    pos = j % 2
                    for par in range(2):
                        nc.tensor.matmul(pS[:, par, :, :].rearrange("p h k -> p (h k)"), identb[:],
                                         maskb[:, pos, :, :].rearrange("p h k -> p (h k)"), start=True, stop=False,
                                         skip_group_check=True)
                    cur, prev = qkT[j % 2], qkT[(j + 1) % 2]
                    for hp in range(HP):
                        for par in range(2):
                            r = slice(64 * par, 64 * par + 64)
                            nc.tensor.matmul(pS[0:64, par, hp, 0:64], cur[r, 0, hp, 0:64], cur[r, 1, hp, 0:64],
                                             start=False, stop=True, skip_group_check=True)
                            if pos:
                                nc.tensor.matmul(pS[0:64, par, hp, 64:128], cur[r, 0, hp, 0:64], prev[r, 1, hp, 64:128],
                                                 start=False, stop=True, skip_group_check=True)
                            mm = nc.tensor.matmul(pS[64:128, par, hp, :], cur[r, 0, hp, 64:128], cur[r, 1, hp, :],
                                                  start=False, stop=True, skip_group_check=True)
                    mm.then_inc(A["simd"], 1)

                def turn_p(t, j):
                    pe.wait_ge(A["pnorm"], t + 1)
                    for par in range(2):
                        for hp in range(HP):
                            mm = nc.tensor.transpose(pT[:, par, 128 * hp:128 * hp + 128], P[j % 2][:, par * HP + hp, :], ident[:])
                    mm.then_inc(A["ptp"], 1)

                def mix(t, j):
                    pos = j % 2
                    pe.wait_ge(A["pt_ev"], t + 1)
                    pe.wait_ge(A["v_ev"], t + 1)
                    if not below(t, 1):
                        pe.wait_ge(A["o_ev"], t)
                    for hp in range(HP):
                        for par in range(2):
                            hc_ = slice(HD * (2 * hp + par), HD * (2 * hp + par + 1))
                            o = pE[64 * par:64 * par + 64, 128 * hp:128 * hp + 128]
                            nc.tensor.matmul(o[:, 64:128], V[j][:, hc_], PT[:, par * HP + hp, 64:128], start=True, stop=True)
                            if pos:
                                mm = nc.tensor.matmul(o[:, 0:64], Vm[j][:, hc_], PT[:, par * HP + hp, 0:64], start=True, stop=True)
                            else:
                                mm = nc.tensor.matmul(o[:, 0:64], V[j][0:64, hc_], PT[0:64, par * HP + hp, 0:64], start=True, stop=True)
                    mm.then_inc(A["pvd"], 1)

                def project(i):
                    pe.wait_ge(A["o_ev"], XB * (i + 1))
                    for c in range(HP):
                        mm = nc.tensor.matmul(pE[:], f["wo"][:, c, :], oT[:, c, :], start=(c == 0), stop=(c == HP - 1))
                    mm.then_inc(A["wod"], 1)

                def step(i, first, last):
                    for j in range(XB):
                        t = XB * i + j
                        if not (last and j == XB - 1):
                            turn_qk(t + 1)
                        if not (last and j >= XB - 2):
                            qkv(t + 2, (j + 2) % XB)
                        if not (last and j == XB - 1):
                            sims(t + 1, (j + 1) % XB)
                        if j == 0 and not first:
                            project(i - 1)
                        turn_p(t, j)
                        if j == 0 and not first:
                            pe.wait_ge(A["xud"], i)
                        mix(t, j)

                qkv(0, 0)
                qkv(1, 1)
                turn_qk(0)
                sims(0, 0)
                pairs(pe, step)
                project(PAIRS - 1)

            def norm_stats(k, final):
                L = LNS[k]

                def both(i, first):
                    for q in range(2):
                        n = 2 * i + q
                        pe.wait_ge(L["lin"], n + 1)
                        nc.tensor.matmul(pLm[:, q, :], ones_mean[:], lin_b[q][:], start=True, stop=True).then_inc(L["lmean"], 1)
                    for q in range(2):
                        n = 2 * i + q
                        pe.wait_ge(L["lsq"], n + 1)
                        if not first:
                            pe.wait_ge(L["lrstd"], n - 1)
                        nc.tensor.matmul(pLv[:, q, :], ones_mean[:], lsq_b[q][:], start=True, stop=True).then_inc(L["lvar"], 1)
                    if final:
                        for q in range(2):
                            n = 2 * i + q
                            pe.wait_ge(L["lnorm"], n + 1)
                            if not first:
                                pe.wait_ge(L["lev"], n - 1)
                            for b in range(XB):
                                mm = nc.tensor.transpose(pLt[:, q, 128 * b:128 * b + 128], foT[q][:, 128 * b:128 * b + 128], ident[:])
                            mm.then_inc(L["ltp"], 1)

                halves(pe, both)

            def feed(l):
                f, Q = F[l], FF[l]
                for c in range(2 * NC):
                    w = CW[c % NC]
                    c0 = 128 * (c % NC) + HID * (c // NC)
                    mm = nc.tensor.matmul(pb1[0:w, c:c + 1], f["w1"][:, c0:c0 + w], f["lb"][:], start=True, stop=True)
                mm.then_inc(Q["b1p"], 1)

                def up(i, c):
                    w = CW[c]
                    if not below(i, 1):
                        pe.wait_ge(Q["ge"], NC * i + c - NC + 1)
                    nc.tensor.matmul(pG[0:w, c, :], f["w1"][:, HID + 128 * c:HID + 128 * c + w], hn[:, bass.ds(i, 1), :].rearrange("p o t -> p (o t)"), start=True,
                                     stop=True).then_inc(Q["g"], 1)
                    if not below(i, 1):
                        pe.wait_ge(Q["m"], NC * i + c - NC + 1)
                    nc.tensor.matmul(pU[0:w, c, :], f["w1"][:, 128 * c:128 * c + w], hn[:, bass.ds(i, 1), :].rearrange("p o t -> p (o t)"), start=True,
                                     stop=True).then_inc(Q["u"], 1)

                def down(i, c):
                    w = CW[c]
                    pe.wait_ge(Q["m"], NC * i + c + 1)
                    if c == 0 and not below(i, 1):
                        pe.wait_ge(Q["x"], i)
                    nc.tensor.matmul(pO[:], f["w2"][0:w, c, :], mm_[0:w, c, :], start=(c == 0), stop=(c == NC - 1)).then_inc(Q["o"], 1)

                def step(i, first):
                    up(i, 0)
                    if not first:
                        down(i - 1, NC - 1)
                    up(i, 1)
                    down(i, 0)
                    up(i, 2)
                    down(i, 1)

                step(0, True)
                with pe.Fori(1, PAIRS) as i:
                    step(i, False)
                down(PAIRS - 1, NC - 1)

            for l in range(DEPTH):
                attention(l)
                pe.wait_ge(ATT[l]["xud"], PAIRS)
                norm_stats(l, False)
                pe.wait_ge(LNS[l]["lnorm"], PAIRS)
                feed(l)
                pe.wait_ge(FF[l]["x"], PAIRS)
            norm_stats(DEPTH, True)

        @block.scalar
        def _(act):
            nc.scalar.preload_act_table_set("natural_log_exp_and_others")
            act.wait_ge(consts_p, 1)
            act.wait_ge(weights, LOADED)
            nc.scalar.activation(nA[:], nA[:], ACT.Exp).then_inc(a_exp, 1)
            act.wait_ge(consts_v, 1)

            def x_copy(n):
                act.wait_ge(xt_ps, n + 1)
                nc.scalar.copy(xs(n), seqs(pW[:, 0, :])).then_inc(x_t, 1)

            def u_bias(n, first):
                act.wait_ge(u_ps, n + 1)
                if not first:
                    act.wait_ge(u_conv, n)
                for h in range(NH):
                    mm = nc.scalar.activation(ub[:, h, :, 3:S + 3], seqs(pW[:, h, :]), ACT.Identity, bias=b1[:, h:h + 1])
                mm.then_inc(u_b, 1)

            def u_sigmoid(n, first):
                act.wait_ge(u_conv, n + 1)
                nc.scalar.activation(uacc[:], uacc[:], ACT.Exp, scale=-1.0).then_inc(sig_e, 1)
                act.wait_ge(sig_e, n + 1)
                nc.scalar.activation(uacc[:], uacc[:], ACT.Ln, bias=one[:]).then_inc(sig_l, 1)
                if not first:
                    act.wait_ge(y_init, n)
                    act.wait_ge(du_done, n)
                act.wait_ge(sig_l, n + 1)
                nc.scalar.activation(u[:], uacc[:], ACT.Exp, scale=-1.0).then_inc(u_sig, 1)

            def bc_copy(n, first):
                act.wait_ge(bc_ps, n + 1)
                if not first:
                    act.wait_ge(bc_split, n)
                nc.scalar.copy(bc_f[:], pW[0:3 * BC, 0, :]).then_inc(bc_f_done, 1)

            def xdt_copy(n):
                act.wait_ge(xdt_ps, n + 1)
                nc.scalar.copy(xdt[:], pW[0:RANK, 1, :]).then_inc(xdt_done, 1)

            def softplus(n, first):
                act.wait_ge(dt_ps, n + 1)
                if not first:
                    act.wait_ge(delta_done, n)
                for h in range(NH):
                    nc.scalar.activation(sp_m[:, h, :], pW[:, h, :], ACT.Relu, bias=bdt[:, h:h + 1])
                for h in range(NH):
                    mm = nc.scalar.activation(sp_l[:, h, :], pW[:, h, :], ACT.Abs, bias=bdt[:, h:h + 1])
                mm.then_inc(sp_a, 1)
                act.wait_ge(sp_a, n + 1)
                nc.scalar.activation(sp_l[:], sp_l[:], ACT.Exp, scale=-1.0).then_inc(sp_e, 1)
                act.wait_ge(sp_e, n + 1)
                nc.scalar.activation(sp_l[:], sp_l[:], ACT.Ln, bias=one[:]).then_inc(sp_done, 1)

            def gates(n, first):
                act.wait_ge(gate_ps, n + 1)
                if not first:
                    act.wait_ge(yg_done, n)
                for h in range(NH):
                    mm = nc.scalar.activation(gate[:, h, :], pW[:, h, :], ACT.Exp, scale=-1.0, bias=nb2[:, h:h + 1])
                mm.then_inc(gate_e, 1)
                act.wait_ge(gate_e, n + 1)
                nc.scalar.activation(gate[:], gate[:], ACT.Ln, bias=one[:]).then_inc(gate_l, 1)
                act.wait_ge(gate_l, n + 1)
                nc.scalar.activation(gate[:], gate[:], ACT.Exp, scale=-1.0).then_inc(gate_done, 1)

            def decay(n, g, k0):
                if g == 0:
                    act.wait_ge(delta_done, n + 1)
                if not below(k0 + g, NDA):
                    act.wait_ge(scan, k0 + g - NDA + 1)
                for k in range(2):
                    for h in range(NH):
                        mm = nc.scalar.activation(dA[g % NDA][:, k, h, :, 1:S], delta[:, h, :, 1:S], ACT.Exp,
                                                  scale=nA[:, h, 2 * g + k:2 * g + k + 1])
                mm.then_inc(da_ready, 1)

            def c_copy(n, g):
                act.wait_ge(c_ready, NG * n + g + 1)
                if g - 2 in ON_POOL or g < 2 and g - 2 + NG in ON_POOL:
                    wait_group(act, hc_pool, hc_dve, n, g - 2)
                nc.scalar.copy(csb[:, g % 2, :, :], pC[:]).then_inc(c_ev, 1)

            def square(n):
                act.wait_ge(cent, n + 1)
                if not below(n, 1):
                    act.wait_ge(var_ps, n)
                nc.scalar.activation(rsq[:], rc[:], ACT.Square).then_inc(sq, 1)

            def rsqrt(n):
                act.wait_ge(var_ps, n + 1)
                if not below(n, 1):
                    act.wait_ge(x_done, n)
                nc.scalar.activation(rstd[:], pW[:, 1, :], ACT.Ln, bias=eps[:]).then_inc(rstd_l, 1)
                act.wait_ge(rstd_l, n + 1)
                nc.scalar.activation(rstd[:], rstd[:], ACT.Exp, scale=-0.5).then_inc(rstd_done, 1)

            def step(i, first, last):
                for g in range(NG):
                    if g + 1 < NG and g + 1 in ON_POOL:
                        c_copy(i, g + 1)
                    if g + 2 < NG:
                        decay(i, g + 2, NG * i)
                    if not last:
                        if g == 0:
                            x_copy(i + 1)
                        if g == 1:
                            u_bias(i + 1, False)
                        if g == 3:
                            u_sigmoid(i + 1, False)
                    if g == 4 and not first:
                        square(i - 1)
                    if not last:
                        if g == 4:
                            xdt_copy(i + 1)
                        if g == 5:
                            softplus(i + 1, False)
                        if g == 6:
                            bc_copy(i + 1, False)
                    if g == 6 and not first:
                        rsqrt(i - 1)
                    if g == 7:
                        if not last:
                            decay(i + 1, 0, NG * (i + 1))
                            if 0 in ON_POOL:
                                c_copy(i + 1, 0)
                        gates(i, first)
                        if not last:
                            decay(i + 1, 1, NG * (i + 1))

            x_copy(0)
            u_bias(0, True)
            u_sigmoid(0, True)
            xdt_copy(0)
            softplus(0, True)
            bc_copy(0, True)
            decay(0, 0, 0)
            if 0 in ON_POOL:
                c_copy(0, 0)
            decay(0, 1, 0)
            pairs(act, step)
            square(PAIRS - 1)
            rsqrt(PAIRS - 1)

            act.wait_ge(x_done, PAIRS)
            act.wait_ge(ffn_loaded, FFN_LOADED)
            nc.scalar.copy(x0T[:], xT[:, :, 1:S + 1]).then_inc(x0_saved, 1)

            def attention(l):
                A = ATT[l]

                def square(t):
                    act.wait_ge(A["rot"], t + 1)
                    if not below(t, 1):
                        act.wait_ge(A["ssr"], t)
                    nc.scalar.activation(qk_sq[:], pA[:], ACT.Square).then_inc(A["sqd"], 1)

                def v_copy(t, j):
                    act.wait_ge(A["v_ps"], t + 1)
                    nc.scalar.copy(V[j][:], pV[:])
                    if j % 2:
                        mm = nc.scalar.copy(Vm[j][0:64, :], pV[0:64, :])
                    else:
                        mm = nc.scalar.copy(Vm[j + 1][64:128, :], pV[64:128, :])
                    mm.then_inc(A["v_ev"], 1)

                def qk_copy(t, j):
                    act.wait_ge(A["tps"], t + 1)
                    nc.scalar.copy(qkT[j % 2][:].rearrange("p c h k -> p (c h k)"), pT[:].rearrange("p c n -> p (c n)")).then_inc(A["qk_ev"], 1)

                def p_copy(t):
                    act.wait_ge(A["ptp"], t + 1)
                    nc.scalar.copy(PT[:].rearrange("p h k -> p (h k)"), pT[:].rearrange("p c n -> p (c n)")).then_inc(A["pt_ev"], 1)

                def exps(t, j):
                    act.wait_ge(A["mxd"], t + 1)
                    if not below(t, 1):
                        act.wait_ge(A["rsd"], t)
                    for par in range(2):
                        for hp in range(HP):
                            h = par * HP + hp
                            mm = nc.scalar.activation(P[j % 2][:, h, :], pS[:, par, hp, :], ACT.Exp, scale=sc8[:, h:h + 1],
                                                      bias=nb[:, h:h + 1], accum_out=psums[:, h:h + 1])
                    mm.then_inc(A["expd"], 1)

                def o_copy(t, j):
                    act.wait_ge(A["pvd"], t + 1)
                    nc.scalar.copy(oT[:, :, 128 * j:128 * j + 128], pE[:].rearrange("p (h q) -> p h q", h=HP)).then_inc(A["o_ev"], 1)

                def step(i, first, last):
                    for j in range(XB):
                        t = XB * i + j
                        if not (last and j == XB - 1):
                            qk_copy(t + 1, j + 1)
                        if not (last and j >= XB - 2):
                            square(t + 2)
                            v_copy(t + 2, (j + 2) % XB)
                        p_copy(t)
                        if not (last and j == XB - 1):
                            exps(t + 1, j + 1)
                        o_copy(t, j)

                square(0)
                v_copy(0, 0)
                square(1)
                v_copy(1, 1)
                qk_copy(0, 0)
                exps(0, 0)
                pairs(act, step)

            def norm_stats(k, final):
                L = LNS[k]

                def both(i, first):
                    for q in range(2):
                        n = 2 * i + q
                        act.wait_ge(L["lcent"], n + 1)
                        if not first:
                            act.wait_ge(L["lvar"], n - 1)
                        nc.scalar.activation(lsq_b[q][:], lc_b[q][:], ACT.Square).then_inc(L["lsq"], 1)
                    for q in range(2):
                        n = 2 * i + q
                        act.wait_ge(L["lvar"], n + 1)
                        if not first:
                            act.wait_ge(L["lnorm"], n - 1)
                        nc.scalar.activation(lr_b[q][:], pLv[:, q, :], ACT.Ln, bias=eps[:]).then_inc(L["lrl"], 1)
                        act.wait_ge(L["lrl"], n + 1)
                        nc.scalar.activation(lr_b[q][:], lr_b[q][:], ACT.Exp, scale=-0.5).then_inc(L["lrstd"], 1)
                    if final:
                        for q in range(2):
                            n = 2 * i + q
                            act.wait_ge(L["ltp"], n + 1)
                            if not first:
                                act.wait_ge(stored[q], 16 * i)
                            nc.scalar.copy(fout[q][:].rearrange("p b d -> p (b d)"), pLt[:, q, :]).then_inc(L["lev"], 1)

                halves(act, both)

            def feed(l):
                f, Q = F[l], FF[l]
                act.wait_ge(Q["b1d"], 1)

                def step(i, first):
                    for c in range(NC):
                        w = CW[c]
                        act.wait_ge(Q["g"], NC * i + c + 1)
                        if not first:
                            act.wait_ge(Q["m"], NC * i + c - NC + 1)
                        nc.scalar.activation(gl[0:w, c, :], pG[0:w, c, :], ACT.Gelu,
                                             bias=f["b1"][0:w, NC + c:NC + c + 1]).then_inc(Q["ge"], 1)

                step(0, True)
                with act.Fori(1, PAIRS) as i:
                    step(i, False)

            for l in range(DEPTH):
                if l:
                    nc.scalar.preload_act_table_set("natural_log_exp_and_others")
                attention(l)
                act.wait_ge(ATT[l]["xud"], PAIRS)
                norm_stats(l, False)
                feed(l)
                act.wait_ge(FF[l]["x"], PAIRS)
            nc.scalar.preload_act_table_set("natural_log_exp_and_others")
            norm_stats(DEPTH, True)

        @block.vector
        def _(dve):
            dve.wait_ge(weights, LOADED)
            nc.vector.tensor_copy(onehot[:], onehot_src[:].unsqueeze(2).to_broadcast([3 * BC, BC, 128]))
            for k in range(3):
                nc.vector.tensor_copy(wbc3[:, :, k, :], wx[:, :, RANK:RANK + BC])
            for h in range(NH):
                nc.vector.tensor_scalar(diagD[:, h, :], ident[:], dsk[:, h:h + 1], None, ALU.mult)
            nc.vector.tensor_scalar(nb2[:], nb2[:], -1.0, None, ALU.mult)
            dve.wait_ge(a_exp, 1)
            nc.vector.tensor_scalar(nA[:], nA[:], -1.0, None, ALU.mult).then_inc(consts_v, 1)

            def conv(n, first):
                dve.wait_ge(u_b, n + 1)
                if not first:
                    dve.wait_ge(u_sig, n)
                for h in range(NH):
                    mm = nc.vector.tensor_scalar(uacc[:, h, :, :], ub[:, h, :, 3:S + 3], cw[:, h, 3:4], cb[:, h:h + 1],
                                                 ALU.mult, ALU.add)
                mm.then_inc(tapped, 1)
                for k in range(3):
                    dve.wait_ge(tapped, 3 * n + k + 1)
                    for h in range(NH):
                        mm = nc.vector.scalar_tensor_tensor(out=uacc[:, h, :, :], in0=ub[:, h, :, k:k + S],
                                                            scalar=cw[:, h, k:k + 1], in1=uacc[:, h, :, :],
                                                            op0=ALU.mult, op1=ALU.add)
                    mm.then_inc(tapped if k < 2 else u_conv, 1)

            def inject(n, g, k0):
                dve.wait_ge(b_ready, k0 + g + 1)
                if g == 0:
                    dve.wait_ge(du_done, n + 1)
                wait_group(dve, hc_pool, hc_dve, n, g - NHB)
                nc.vector.tensor_tensor(hb[g % NHB][:], du[:].rearrange("p (h t) -> p h t", h=NH).unsqueeze(1).to_broadcast([128, 2, NH, T]),
                                        pB[:].unsqueeze(2).to_broadcast([128, 2, NH, T]), ALU.mult).then_inc(dbu, 1)

            def recur(g, k0):
                dve.wait_ge(dbu, k0 + g + 1)
                dve.wait_ge(da_ready, k0 + g + 1)
                flat = hb[g % NHB][:].rearrange("p k h t -> p (k h t)")
                nc.vector.tensor_tensor_scan(flat, dA[g % NDA][:].rearrange("p k h s t -> p (k h s t)"), flat, 0.0,
                                             ALU.mult, ALU.add).then_inc(scan, 1)

            def product(n, g):
                dve.wait_ge(scan, NG * n + g + 1)
                dve.wait_ge(c_ready, NG * n + g + 1)
                if not below(NG * n + g, 2):
                    dve.wait_ge(ysum, NG * n + g - 1)
                nc.vector.tensor_tensor(hc[g % 2][:], hb[g % NHB][:], pC[:].unsqueeze(2).to_broadcast([128, 2, NH, T]),
                                        ALU.mult).then_inc(hc_dve, 1)

            def y_gate(n, k1):
                dve.wait_ge(ysum, k1)
                dve.wait_ge(gate_done, n + 1)
                if not below(n, 1):
                    dve.wait_ge(wo_ps, n)
                nc.vector.tensor_tensor(yg[:], pY[:], gate[:], ALU.mult).then_inc(yg_done, 1)

            def residual(n):
                dve.wait_ge(wo_ps, n + 1)
                nc.vector.scalar_tensor_tensor(out=seqs(rb[:]), in0=seqs(pW[:, 0, :]), scalar=bo[:, 0:1], in1=xs(n),
                                               op0=ALU.add, op1=ALU.add).then_inc(resid, 1)

            def center(n):
                dve.wait_ge(mean_ps, n + 1)
                nc.vector.tensor_tensor(rc[:], rb[:], pW[:, 0, :], ALU.subtract).then_inc(cent, 1)

            def normal(n):
                dve.wait_ge(rstd_done, n + 1)
                nc.vector.tensor_tensor(xs(n), seqs(rc[:]), seqs(rstd[:]), ALU.mult).then_inc(x_done, 1)

            def step(i, first, last):
                for g in range(NG):
                    inject(i, g, NG * i)
                    recur(g, NG * i)
                    if g in ON_DVE:
                        product(i, g)
                    if g == 2 and not last:
                        conv(i + 1, False)
                    if not first:
                        if g == 1:
                            y_gate(i - 1, NG * i)
                        if g == 2:
                            residual(i - 1)
                        if g == 3:
                            center(i - 1)
                        if g == 7:
                            normal(i - 1)

            conv(0, True)
            pairs(dve, step)
            y_gate(PAIRS - 1, NG * PAIRS)
            residual(PAIRS - 1)
            center(PAIRS - 1)
            normal(PAIRS - 1)
            dve.wait_ge(x_done, PAIRS)
            dve.wait_ge(ffn_loaded, FFN_LOADED)
            nc.vector.tensor_copy(identb[:], ident[:])
            nc.vector.tensor_copy(maskb[:], maskf[:].unsqueeze(2).to_broadcast([128, 2, 4, 128]))
            for l in range(DEPTH):
                f = F[l]
                for pos in range(2):
                    nc.vector.tensor_tensor(f["tc"][:, pos], rot_c[:, pos], f["qk_scale"][:], ALU.mult)
                    for r in range(2):
                        mm = nc.vector.tensor_tensor(f["ts"][:, pos, :, 32 * r:32 * r + 32], rot_s[:, pos, :, 32 * r:32 * r + 32],
                                                     f["qk_scale"][:, :, 32 - 32 * r:64 - 32 * r], ALU.mult)
            mm.then_inc(tabs, 1)
            dve.wait_ge(tabs, 1)

            def attention(l):
                A, f = ATT[l], F[l]

                def shift(n, j):
                    t, pos = XB * n + j, j % 2
                    if not below(t, XB):
                        dve.wait_ge(A["v_ps"], t - XB + 1)
                    sq_ = bass.ds(2 * n + j // 2, 1)
                    nc.vector.tensor_copy(hT[0:64, j, :], xT[0:64, sq_, 1 + 128 * pos:129 + 128 * pos].rearrange("p o t -> p (o t)"))
                    nc.vector.tensor_copy(hT[64:128, j, :], xT[64:128, sq_, 128 * pos:128 + 128 * pos].rearrange("p o t -> p (o t)")).then_inc(A["ht"], 1)

                def rotate(t, j):
                    pos = j % 2
                    dve.wait_ge(A["qk_ps"], t + 1)
                    if not below(t, 1):
                        dve.wait_ge(A["addd"], t)
                    v4 = lambda x: x[:].rearrange("p c (h d) -> p c h d", d=HD)
                    nc.vector.tensor_tensor(v4(t1), v4(pA), f["tc"][:, pos].unsqueeze(2).to_broadcast([128, 2, HEADS, HD]), ALU.mult)
                    for r in range(2):
                        o, n_ = 32 * r, 32 - 32 * r
                        mm = nc.vector.tensor_tensor(v4(t2)[:, :, :, o:o + 32], v4(pA)[:, :, :, n_:n_ + 32],
                                                     f["ts"][:, pos, :, o:o + 32].unsqueeze(2).to_broadcast([128, 2, HEADS, 32]), ALU.mult)
                    mm.then_inc(A["rot"], 1)

                def lengths(t):
                    dve.wait_ge(A["sqd"], t + 1)
                    nc.vector.tensor_reduce(ss[:], qk_sq[:].rearrange("p c (h d) -> p (c h) d", d=HD), AX.X, ALU.add).then_inc(A["ssr"], 1)
                    dve.wait_ge(A["ssr"], t + 1)
                    if not below(t, 1):
                        dve.wait_ge(A["rnd"], t)
                    nc.vector.tensor_scalar(ssc[:], ss[:], 1e-24, None, ALU.max).then_inc(A["ssd"], 1)

                def maxima(t, j):
                    dve.wait_ge(A["simd"], t + 1)
                    nc.vector.tensor_reduce(mx[:], pS[:].rearrange("p c h k -> p (c h) k"), AX.X, ALU.max).then_inc(A["mxr"], 1)
                    dve.wait_ge(A["rnd"], t + 1)
                    nc.vector.tensor_scalar(sc8[:].rearrange("p (c h) -> p c h", c=2),
                                            rn[j % 2][:, 0:HEADS].rearrange("p (h c) -> p c h", c=2), 8.0, None, ALU.mult).then_inc(A["mxs"], 1)
                    dve.wait_ge(A["mxr"], t + 1)
                    dve.wait_ge(A["mxs"], t + 1)
                    nc.vector.scalar_tensor_tensor(out=nb[:], in0=mx[:], scalar=-1.0, in1=sc8[:], op0=ALU.mult, op1=ALU.mult).then_inc(A["mxd"], 1)

                def inverse(t):
                    dve.wait_ge(A["expd"], t + 1)
                    if not below(t, 1):
                        dve.wait_ge(A["pnorm"], t)
                    nc.vector.reciprocal(rs[:], psums[:]).then_inc(A["rsd"], 1)

                def add_x(n):
                    dve.wait_ge(A["wod"], n + 1)
                    nc.vector.tensor_tensor(xs(n), seqs(pE[:]), xs(n), ALU.add).then_inc(A["xud"], 1)

                def step(i, first, last):
                    for j in range(XB):
                        t = XB * i + j
                        if j == 0:
                            shift(i, 3)
                        elif not last:
                            shift(i + 1, j - 1)
                        inverse(t)
                        if not (last and j >= XB - 2):
                            rotate(t + 2, j)
                            lengths(t + 2)
                        if not (last and j == XB - 1):
                            maxima(t + 1, j + 1)
                        if j == 0 and not first:
                            add_x(i - 1)

                for j in range(3):
                    shift(0, j)
                for j in range(2):
                    rotate(j, j)
                    lengths(j)
                maxima(0, 0)
                if l == 0:
                    dve.wait_ge(x0_saved, 1)
                pairs(dve, step)
                add_x(PAIRS - 1)

            def norm_stats(k, final):
                L = LNS[k]

                def both(i, first):
                    for q in range(2):
                        n = 2 * i + q
                        if not first:
                            dve.wait_ge(L["lcent"], n - 1)
                        if final:
                            mm = nc.vector.tensor_tensor(seqs(lin_b[q][:]), xs(n), x0T[:, bass.ds(2 * n, 2), :], ALU.add)
                        else:
                            nc.vector.tensor_copy(seqs(lin_b[q][:])[0:64], xs(n)[0:64])
                            mm = nc.vector.tensor_copy(seqs(lin_b[q][:])[64:128], xT[64:128, bass.ds(2 * n, 2), 0:S])
                        mm.then_inc(L["lin"], 1)
                    for q in range(2):
                        n = 2 * i + q
                        dve.wait_ge(L["lmean"], n + 1)
                        if not first:
                            dve.wait_ge(L["lnorm"], n - 1)
                        nc.vector.tensor_tensor(lc_b[q][:], lin_b[q][:], pLm[:, q, :], ALU.subtract).then_inc(L["lcent"], 1)
                    for q in range(2):
                        n = 2 * i + q
                        dve.wait_ge(L["lrstd"], n + 1)
                        if final:
                            if not first:
                                dve.wait_ge(L["ltp"], n - 1)
                            nc.vector.tensor_tensor(foT[q][:], lc_b[q][:], lr_b[q][:], ALU.mult).then_inc(L["lnorm"], 1)
                        else:
                            nc.vector.scalar_tensor_tensor(out=hn[:, bass.ds(n, 1), :].rearrange("p o t -> p (o t)"), in0=lc_b[q][:], scalar=F[k]["lg"][:, 0:1],
                                                           in1=lr_b[q][:], op0=ALU.mult, op1=ALU.mult).then_inc(L["lnorm"], 1)

                halves(dve, both)

            def feed(l):
                f, Q = F[l], FF[l]
                dve.wait_ge(Q["b1p"], 1)
                for c in (0, NC):
                    nc.vector.tensor_tensor(f["b1"][:, c:c + NC - 1], f["b1"][:, c:c + NC - 1], pb1[:, c:c + NC - 1], ALU.add)
                    e = slice(c + NC - 1, c + NC)
                    mm = nc.vector.tensor_tensor(f["b1"][0:CW[-1], e], f["b1"][0:CW[-1], e], pb1[0:CW[-1], e], ALU.add)
                mm.then_inc(Q["b1d"], 1)
                dve.wait_ge(Q["b1d"], 1)

                def gated(i, c):
                    w = CW[c]
                    dve.wait_ge(Q["ge"], NC * i + c + 1)
                    dve.wait_ge(Q["u"], NC * i + c + 1)
                    if not below(i, 1):
                        dve.wait_ge(Q["o"], NC * i + c - NC + 1)
                    nc.vector.scalar_tensor_tensor(out=mm_[0:w, c, :], in0=pU[0:w, c, :], scalar=f["b1"][0:w, c:c + 1],
                                                   in1=gl[0:w, c, :], op0=ALU.add, op1=ALU.mult).then_inc(Q["m"], 1)

                def add_x(n):
                    dve.wait_ge(Q["o"], NC * (n + 1))
                    nc.vector.scalar_tensor_tensor(out=xs(n), in0=seqs(pO[:]), scalar=f["b2"][:, 0:1], in1=xs(n),
                                                   op0=ALU.add, op1=ALU.add).then_inc(Q["x"], 1)

                def step(i, first):
                    gated(i, 0)
                    if not first:
                        add_x(i - 1)
                    gated(i, 1)
                    gated(i, 2)

                step(0, True)
                with dve.Fori(1, PAIRS) as i:
                    step(i, False)
                add_x(PAIRS - 1)

            for l in range(DEPTH):
                attention(l)
                dve.wait_ge(ATT[l]["xud"], PAIRS)
                norm_stats(l, False)
                dve.wait_ge(LNS[l]["lnorm"], PAIRS)
                feed(l)
                dve.wait_ge(FF[l]["x"], PAIRS)
            norm_stats(DEPTH, True)

        @block.gpsimd
        def _(pool):
            nc.gpsimd.memset(ones_mean[:], 1.0 / D)
            nc.gpsimd.memset(eps[:], EPS)
            nc.gpsimd.memset(mhalf[:], -0.5)
            nc.gpsimd.memset(one[:], 1.0)
            nc.gpsimd.memset(xT[:, :, 0:1], 0.0)
            nc.gpsimd.memset(ub[:, :, :, 0:3], 0.0)
            for k in range(NDA):
                mm = nc.gpsimd.memset(dA[k][:, :, :, :, 0:1].rearrange("p k h s t -> p (k h s) t"), 0.0)
            mm.then_inc(consts_p, 1)

            def hold():
                nc.gpsimd.tensor_tensor(held[:], one[:], one[:], ALU.mult)

            def split(n, k1):
                pool.wait_ge(bc_f_done, n + 1)
                hold()
                nc.gpsimd.tensor_scalar(bc_t[:], bc_f[:], third[:, 0:1], 0.0, ALU.mult, ALU.add).then_inc(part, 1)
                pool.wait_ge(part, 3 * n + 1)
                nc.gpsimd.tensor_tensor(bc_r[:], bc_f[:], bc_t[:], ALU.subtract).then_inc(part, 1)
                pool.wait_ge(part, 3 * n + 2)
                hold()
                nc.gpsimd.tensor_scalar(bc_t[:], bc_r[:], third[:, 1:2], 0.0, ALU.mult, ALU.add).then_inc(part, 1)
                pool.wait_ge(part, 3 * n + 3)
                if k1 is not None:
                    pool.wait_ge(c_ready, k1)
                nc.gpsimd.tensor_tensor(bc_s[:], bc_r[:], bc_t[:], ALU.subtract).then_inc(bc_split, 1)

            def delta_add(n, k1):
                pool.wait_ge(sp_done, n + 1)
                if k1 is not None:
                    pool.wait_ge(da_ready, k1)
                nc.gpsimd.tensor_tensor(delta[:].rearrange("p h s t -> p (h s t)"), sp_m[:].rearrange("p h t -> p (h t)"),
                                        sp_l[:].rearrange("p h t -> p (h t)"), ALU.add).then_inc(delta_done, 1)

            def du_mul(n, k1):
                pool.wait_ge(delta_done, n + 1)
                if k1 is not None:
                    pool.wait_ge(dbu, k1)
                nc.gpsimd.tensor_tensor(du[:], delta[:].rearrange("p h s t -> p (h s t)"),
                                        u[:].rearrange("p h s t -> p (h s t)"), ALU.mult).then_inc(du_done, 1)

            def readout(n, g):
                k0 = NG * n
                wait_group(pool, c_ev, c_ev, n, g)
                pool.wait_ge(scan, k0 + g + 1)
                if not below(k0 + g, 2):
                    pool.wait_ge(ysum, k0 + g - 1)
                nc.gpsimd.tensor_tensor(hc[g % 2][:], hb[g % NHB][:], csb[:, g % 2, :, :].unsqueeze(2).to_broadcast([128, 2, NH, T]),
                                        ALU.mult).then_inc(hc_pool, 1)

            def step(i, first, last):
                for g in range(NG):
                    if not last:
                        if g == 7:
                            delta_add(i + 1, NG * i + NG)
                            split(i + 1, NG * i + NG)
                            du_mul(i + 1, NG * i + NG)
                    if g in ON_POOL:
                        readout(i, g)

            pool.wait_ge(weights, LOADED)
            delta_add(0, None)
            du_mul(0, None)
            split(0, None)
            pairs(pool, step)
            pool.wait_ge(x_done, PAIRS)

            def attention(l):
                A = ATT[l]

                def rows(t, j):
                    pool.wait_ge(A["rot"], t + 1)
                    if not below(t, 1):
                        pool.wait_ge(A["tps"], t)
                    nc.gpsimd.tensor_tensor(qk[:], t1[:], t2[:], ALU.add).then_inc(A["addd"], 1)
                    pool.wait_ge(A["ssd"], t + 1)
                    if not below(t, 2):
                        pool.wait_ge(A["mxd"], t - 1)
                    nc.gpsimd.tensor_tensor(rn[j % 2][:], ssc[:], mhalf[:], ALU.pow).then_inc(A["rnd"], 1)
                    pool.wait_ge(A["rnd"], t + 1)
                    kk = qk[:, 1, :].rearrange("p (h d) -> p h d", d=HD)
                    nc.gpsimd.tensor_tensor(kk, kk, rn[j % 2][:, HEADS:2 * HEADS].unsqueeze(2).to_broadcast([128, HEADS, HD]),
                                            ALU.mult).then_inc(A["qkd"], 1)

                def normalise(t, j):
                    pool.wait_ge(A["rsd"], t + 1)
                    nc.gpsimd.tensor_tensor(P[j % 2][:], P[j % 2][:], rs[:].unsqueeze(2).to_broadcast([128, HEADS, 128]),
                                            ALU.mult).then_inc(A["pnorm"], 1)

                def step(i, first, last):
                    for j in range(XB):
                        t = XB * i + j
                        normalise(t, j)
                        if not (last and j >= XB - 2):
                            rows(t + 2, j)

                rows(0, 0)
                rows(1, 1)
                pairs(pool, step)

            for l in range(DEPTH):
                attention(l)


_INS = ['L0_attn_x', 'L0_attn_W1', 'L0_attn_b1', 'L0_attn_W2', 'L0_attn_b2', 'L0_attn_conv_w', 'L0_attn_conv_b',
        'L0_attn_A_log', 'L0_attn_x_proj_w', 'L0_attn_dt_proj_w', 'L0_attn_dt_proj_b', 'L0_attn_D_skip', 'L0_attn_Wo',
        'L0_attn_bo', 'L0_ffn_wqkv', 'L0_ffn_q_scale', 'L0_ffn_k_scale', 'L0_ffn_wo', 'L0_ffn_ln_g', 'L0_ffn_ln_b',
        'L0_ffn_w1', 'L0_ffn_b1', 'L0_ffn_w2', 'L0_ffn_b2']


_COLUMNS = {'L0_attn_b1', 'L0_attn_b2', 'L0_attn_dt_proj_b', 'L0_attn_conv_b', 'L0_attn_D_skip', 'L0_attn_bo'}

_LAYER_COLUMNS = {'L0_ffn_ln_g', 'L0_ffn_ln_b', 'L0_ffn_b2'}


def constants():
    bc, s, hd, window = 32, 256, 64, 64
    half = np.arange(0, hd, 2, dtype=np.float32)
    inv = (np.float32(1.0) / np.float32(10000.0) ** (half / np.float32(hd))).astype(np.float32)
    tok = np.arange(s, dtype=np.float32)
    freq = np.tile(tok[:, None] * inv[None, :], (1, 2))
    base = (half + np.float32(0.4 * hd)) / np.float32(1.4 * hd)
    power = (tok - s // 2) / np.float32(window // 2)
    scale = np.tile(base[None, :] ** power[:, None], (1, 2)).astype(np.float32)
    sign = np.where(np.arange(hd) < hd // 2, -1.0, 1.0).astype(np.float32)
    cos, sin = np.cos(freq), np.sin(freq) * sign
    rot_c = np.stack([cos * scale, cos / scale], 1).reshape(2, 128, 2, hd).transpose(1, 0, 2, 3)
    rot_s = np.stack([sin * scale, sin / scale], 1).reshape(2, 128, 2, hd).transpose(1, 0, 2, 3)
    r, c = np.arange(64)[:, None], np.arange(64)[None, :]
    own, before = np.where(c <= r, 0.0, -1e30), np.where(c >= r, 0.0, -1e30)
    none = np.full((64, 64), -1e30)
    mask = np.stack([np.block([[own, none], [before, own]]), np.block([[own, before], [before, own]])], 1)
    return {
        "c_ident": np.eye(128, dtype=np.float32),
        "c_third": np.repeat(np.array([[0, 0], [1, 0], [1, 1]], np.float32), bc, axis=0),
        "c_onehot": np.tile(np.eye(bc, dtype=np.float32), (3, 1)),
        "c_rot_c": np.ascontiguousarray(rot_c, np.float32), "c_rot_s": np.ascontiguousarray(rot_s, np.float32),
        "c_mask": np.ascontiguousarray(mask, np.float32),
    }


def kernel(**inputs):
    import concourse.bacc as bacc
    from concourse.bass_utils import run_bass_kernel_spmd

    nc = bacc.Bacc("TRN2", target_bir_lowering=False, num_devices=1)
    arrays, aps = {}, {}
    for name in _INS:
        value = np.asarray(inputs[name])
        if name in _COLUMNS:
            value = value.reshape(-1, 128).T
        if name in _LAYER_COLUMNS:
            value = value.reshape(value.shape[0], 128, 1)
        if name == 'L0_ffn_b1':
            hid = value.shape[1] // 2
            padded = np.zeros((value.shape[0], 2, 3 * 128), value.dtype)
            padded[:, :, :hid] = value.reshape(-1, 2, hid)
            value = padded.reshape(-1, 6, 128).transpose(0, 2, 1)
        arrays["in_" + name] = np.ascontiguousarray(value)
    for name, value in constants().items():
        arrays["in_" + name] = value
    for name, value in arrays.items():
        aps[name[3:]] = nc.dram_tensor(name, value.shape, mybir.dt.from_np(value.dtype), kind="ExternalInput").ap()
    shape = inputs["L0_attn_x"].shape
    out = nc.dram_tensor("out_0", shape, mybir.dt.float32, kind="ExternalOutput").ap()
    build(nc, aps, out)
    r = run_bass_kernel_spmd(nc, [arrays], core_ids=[0])
    return r.results[0]["out_0"]
```

```python
import math
import numpy as np
import concourse.bass as bass
from concourse import mybir
from contextlib import ExitStack

F32 = mybir.dt.float32
BF16 = mybir.dt.bfloat16
ALU = mybir.AluOpType
ACT = mybir.ActivationFunctionType
AX = mybir.AxisListType


def below(v, k):
    return isinstance(v, int) and v < k


def build(nc, a, out):
    NSEQ, S, D = a["L0_attn_x"].shape
    CH = a["L0_attn_W1"].shape[1]
    NH = CH // 128
    NST = a["L0_attn_A_log"].shape[1]
    RANK = a["L0_attn_dt_proj_w"].shape[0]
    PAIRS = NSEQ // 2
    T = 2 * S
    NG = NST // 2
    XB = T // 128
    BC = 2 * NST
    EPS = 1e-5
    LEN_MIN = 1e-24
    DEPTH, _, HID = a["L0_ffn_w2"].shape[0], 0, a["L0_ffn_w2"].shape[1]
    HD = a["L0_ffn_q_scale"].shape[1]
    INNER = a["L0_ffn_wo"].shape[1]
    HEADS = INNER // HD
    HP = HEADS // 2
    NC = -(-HID // 128)
    CW = [min(128, HID - 128 * c) for c in range(NC)]
    TILES = PAIRS * XB

    ctx = ExitStack()
    with ctx:
        def sb(name, shape, dt=F32):
            return ctx.enter_context(nc.sbuf_tensor(name, shape, dt))

        def ps(name, shape, dt=F32):
            return ctx.enter_context(nc.psum_tensor(name, shape, dt))

        def sem(name):
            return ctx.enter_context(nc.semaphore(name))

        ident = sb("ident", [128, 128])
        ones_mean = sb("ones_mean", [128, 128])
        onehot_src = sb("onehot_src", [3 * BC, BC])
        onehot = sb("onehot", [3 * BC, BC, 128], BF16)
        w1 = sb("w1", [128, CH])
        w2 = sb("w2", [128, CH])
        wx = sb("wx", [128, NH, RANK + BC])
        wbc3 = sb("wbc3", [128, NH, 3, BC])
        wdt = sb("wdt", [RANK, CH])
        wo = sb("wo", [128, NH, D])
        b1 = sb("b1", [128, NH])
        nb2 = sb("nb2", [128, NH])
        bdt = sb("bdt", [128, NH])
        cw = sb("cw", [128, NH, 4])
        cb = sb("cb", [128, NH])
        nA = sb("nA", [128, NH, NST])
        dsk = sb("dsk", [128, NH])
        bo = sb("bo", [128, 1])
        diagD = sb("diagD", [128, NH, 128])

        xT = sb("xT", [128, NSEQ, S + 1])
        eps = sb("eps", [128, 1])
        one = sb("one", [128, 1])
        held = sb("held", [128, 1])

        identb = sb("identb", [128, 128], BF16)
        maskf = sb("maskf", [128, 2, 128])
        maskb = sb("maskb", [128, 2, 4, 128], BF16)
        rot_c = sb("rot_c", [128, 2, 2, HD])
        rot_s = sb("rot_s", [128, 2, 2, HD])
        F = []
        for l in range(DEPTH):
            F.append(dict(
                wqkv=sb(f"wqkv{l}", [128, 3 * INNER]), wo=sb(f"wof{l}", [128, INNER // 128, D]),
                w1=sb(f"w1f{l}", [128, 2 * HID]), w2=sb(f"w2f{l}", [128, NC, D]),
                lg=sb(f"lg{l}", [128, 1]), lb=sb(f"lb{l}", [128, 1]), b1=sb(f"b1f{l}", [128, 2 * NC]),
                b2=sb(f"b2f{l}", [128, 1]), qk_scale=sb(f"qks{l}", [128, 2, HD]),
                tc=sb(f"tc{l}", [128, 2, 2, HD]), ts=sb(f"ts{l}", [128, 2, 2, HD])))

        mscope = ExitStack()

        def msb(name, shape, dt=F32):
            return mscope.enter_context(nc.sbuf_tensor(name, shape, dt))

        def mps(name, shape, dt=F32):
            return mscope.enter_context(nc.psum_tensor(name, shape, dt))

        xin = msb("xin", [128, XB, D])
        ub = msb("ub", [128, NH, 2, S + 3])
        uacc = msb("uacc", [128, NH, 2, S])
        u = msb("u", [128, NH, 2, S])
        xdt = msb("xdt", [RANK, T])
        bc_f = msb("bc_f", [3 * BC, T])
        bc_r = msb("bc_r", [3 * BC, T])
        bc_t = msb("bc_t", [3 * BC, T], BF16)
        third = msb("third", [3 * BC, 2])
        bc_s = msb("bc_s", [3 * BC, T], BF16)
        sp_m = msb("sp_m", [128, NH, T])
        sp_l = msb("sp_l", [128, NH, T])
        delta = msb("delta", [128, NH, 2, S])
        du = msb("du", [128, NH * T])
        gate = msb("gate", [128, NH, T])
        yg = msb("yg", [128, NH, T])
        NDA, NHB = 2, 4
        dA = [msb(f"dA{k}", [128, 2, NH, 2, S]) for k in range(NDA)]
        hb = [msb(f"hb{k}", [128, 2, NH, T]) for k in range(NHB)]
        hc = [msb(f"hc{k}", [128, 2, NH, T]) for k in range(2)]
        csb = msb("csb", [128, 2, 2, T])
        rb = msb("rb", [128, T])
        rc = msb("rc", [128, T])
        rsq = msb("rsq", [128, T])
        rstd = msb("rstd", [128, T])
        pB = mps("pB", [128, 2, T])
        pC = mps("pC", [128, 2, T])
        pY = mps("pY", [128, NH, T])
        pW = mps("pW", [128, 2, T])
        mscope.close()

        fscope = ExitStack()

        fsb = lambda name, shape: fscope.enter_context(nc.sbuf_tensor(name, shape, F32))

        def fps(scope, name, shape, dt=F32):
            return scope.enter_context(nc.psum_tensor(name, shape, dt))

        x0T = fsb("x0T", [128, NSEQ, S])
        hn = fsb("hn", [128, PAIRS, T])
        lin = fsb("lin", [128, T])
        lc = fsb("lc", [128, T])
        lsq = fsb("lsq", [128, T])
        lr = fsb("lr", [128, T])
        ascope = ExitStack()
        fsb = lambda name, shape: ascope.enter_context(nc.sbuf_tensor(name, shape, F32))
        hT = fsb("hT", [128, XB, 128])
        t1 = [fsb(f"t1_{k}", [128, 2, INNER]) for k in range(2)]
        t2 = [fsb(f"t2_{k}", [128, 2, INNER]) for k in range(2)]
        qk_sq = fsb("qk_sq", [128, 2, INNER])
        ss = fsb("ss", [128, 2 * HEADS])
        ssi = fsb("ssi", [128, 2 * HEADS])
        ssc = fsb("ssc", [128, 2, 2 * HEADS])
        lns = fsb("lns", [128, 2, 2 * HEADS])
        lsum = fsb("lsum", [128, 2 * HEADS])
        rn = [fsb(f"rn{k}", [128, 2 * HEADS]) for k in range(2)]
        qk = [fsb(f"qk{k}", [128, 2, INNER]) for k in range(2)]
        qkT = [fsb(f"qkT{k}", [128, 2, HP, 128]) for k in range(2)]
        V = [fsb(f"V{k}", [128, INNER]) for k in range(XB)]
        Vm = [fsb(f"Vm{k}", [128, INNER]) for k in range(XB)]
        mx = fsb("mx", [128, HEADS])
        sc8 = [fsb(f"sc8_{k}", [128, HEADS]) for k in range(2)]
        nb = [fsb(f"nb{k}", [128, HEADS]) for k in range(2)]
        psums = fsb("psums", [128, HEADS])
        rs = fsb("rs", [128, HEADS])
        P = [fsb(f"P{k}", [128, HEADS, 128]) for k in range(2)]
        PT = fsb("PT", [128, HEADS, 128])
        oT = fsb("oT", [128, HP, T])
        ascope.close()
        lscope = ExitStack()
        fsb = lambda name, shape: lscope.enter_context(nc.sbuf_tensor(name, shape, F32))
        gl = fsb("gl", [128, NC, T])
        mm_ = fsb("mm_", [128, NC, T])
        lin_b = [fsb(f"lin_b{k}", [128, T]) for k in range(2)]
        lc_b = [fsb(f"lc_b{k}", [128, T]) for k in range(2)]
        lsq_b = [fsb(f"lsq_b{k}", [128, T]) for k in range(2)]
        lr_b = [fsb(f"lr_b{k}", [128, T]) for k in range(2)]
        foT = [fsb(f"foT{k}", [128, T]) for k in range(2)]
        fout = [fsb(f"fout{k}", [128, XB, D]) for k in range(2)]
        lscope.close()
        fscope.close()
        s1 = ExitStack()
        pA = fps(s1, "pA", [128, 2, INNER])
        pT = fps(s1, "pT", [128, 2, INNER])
        pS = fps(s1, "pS", [128, 2, HP, 128])
        pV = fps(s1, "pV", [128, INNER])
        pE = fps(s1, "pE", [128, T])
        s1.close()
        pGU = fps(s1, "pGU", [128, NC, 2, T])

        def pG(w, c):
            return pGU[0:w, (0, 2, 1)[c], 0, :]

        def pU(w, c):
            return pGU[0:w, (0, 2, 1)[c], 1, :]

        fps(s1, "of_pV", [128, T])
        pO = fps(s1, "pO", [128, T])
        s1.close()
        pLm = fps(s1, "pLm", [128, 2, T])
        pLv = fps(s1, "pLv", [128, 2, T])
        pLt = fps(s1, "pLt", [128, 2, T])
        s1.close()

        ffn_loaded = sem("ffn_loaded")
        tabs = sem("tabs")
        x0_saved = sem("x0_saved")
        ATT_PER_LAYER = {n: TILES for n in """ht qk_ps v_ps rot sqd ssr ssl ssi ssd lnd lsd rnd addd qkd tps qk_ev mxs ptp pt_ev v_ev pvd o_ev""".split()}
        ATT_PER_LAYER |= {n: 2 * TILES for n in ("simd", "mxr", "mxd", "expd", "rsd", "pnorm")} | {"wod": PAIRS, "xud": PAIRS}
        LN_PER_STAGE = {n: PAIRS for n in "lin lmean lcent lsq lvar lrl lrstd lnorm".split()} | {"ltp": 0, "lev": 0}
        FF_PER_LAYER = {n: NC * PAIRS for n in "g u ge m o".split()} | {"x": PAIRS}
        ATT = {n: sem("att_" + n) for n in ATT_PER_LAYER}
        LNS = {n: sem("ln_" + n) for n in LN_PER_STAGE}
        FF = {n: sem("ff_" + n) for n in FF_PER_LAYER}
        b1_ps = sem("b1_ps")
        b1_done = sem("b1_done")

        def counted(per, k):
            return {n: k * v for n, v in per.items()}
        a_exp = sem("a_exp")
        b_ready = sem("b_ready")
        bc_f_done = sem("bc_f_done")
        bc_ps = sem("bc_ps")
        bc_split = sem("bc_split")
        tapped = sem("tapped")
        part = sem("part")
        c_ev = sem("c_ev")
        c_ready = sem("c_ready")
        cent = sem("cent")
        consts_p = sem("consts_p")
        consts_v = sem("consts_v")
        da_ready = sem("da_ready")
        dbu = sem("dbu")
        delta_done = sem("delta_done")
        dt_ps = sem("dt_ps")
        du_done = sem("du_done")
        gate_done = sem("gate_done")
        gate_e = sem("gate_e")
        gate_l = sem("gate_l")
        gate_ps = sem("gate_ps")
        hc_pool = sem("hc_pool")
        hc_dve = sem("hc_dve")
        mean_ps = sem("mean_ps")
        resid = sem("resid")
        rstd_done = sem("rstd_done")
        rstd_l = sem("rstd_l")
        scan = sem("scan")
        sig_e = sem("sig_e")
        sig_l = sem("sig_l")
        sp_a = sem("sp_a")
        sp_done = sem("sp_done")
        sp_e = sem("sp_e")
        sq = sem("sq")
        stored = [sem(f"stored{q}") for q in range(2)]
        u_b = sem("u_b")
        u_conv = sem("u_conv")
        u_ps = sem("u_ps")
        u_sig = sem("u_sig")
        var_ps = sem("var_ps")
        weights = sem("weights")
        first_loaded = sem("first_loaded")
        wo_ps = sem("wo_ps")
        x_done = sem("x_done")
        x_in = sem("x_in")
        x_t = sem("x_t")
        xdt_done = sem("xdt_done")
        xdt_ps = sem("xdt_ps")
        xt_ps = sem("xt_ps")
        y_init = sem("y_init")
        yg_done = sem("yg_done")
        ysum = sem("ysum")
        x_pairs = a["L0_attn_x"].rearrange("(i s) (b p) d -> i p (s b) d", s=2, p=128)
        first_list = [
            (xin[:], x_pairs[0]), (ident[:], a["c_ident"]), (w1[:], a["L0_attn_W1"]), (b1[:], a["L0_attn_b1"]),
            (cw[:], a["L0_attn_conv_w"].rearrange("(c p) k -> p c k", p=128)), (cb[:], a["L0_attn_conv_b"]),
        ]
        FIRST_LOADED = 16 * len(first_list)
        load_list = [
            (onehot_src[:], a["c_onehot"]), (third[:], a["c_third"]),
            (w2[:], a["L0_attn_W2"]),
            (wx[:], a["L0_attn_x_proj_w"].rearrange("(c p) n -> p c n", p=128)),
            (wdt[:], a["L0_attn_dt_proj_w"]),
            (wo[:], a["L0_attn_Wo"].rearrange("(c p) n -> p c n", p=128)),
            (nb2[:], a["L0_attn_b2"]),
            (bdt[:], a["L0_attn_dt_proj_b"]),
            (nA[:], a["L0_attn_A_log"].rearrange("(c p) k -> p c k", p=128)),
            (dsk[:], a["L0_attn_D_skip"]),
            (bo[:], a["L0_attn_bo"]),
        ]
        LOADED = 16 * len(load_list)
        ffn_list = [(maskf[:], a["c_mask"]), (rot_c[:], a["c_rot_c"]), (rot_s[:], a["c_rot_s"])]
        for l in range(DEPTH):
            f = F[l]
            ffn_list += [
                (f["wqkv"][:], a["L0_ffn_wqkv"][l]),
                (f["wo"][:], a["L0_ffn_wo"][l].rearrange("(c p) n -> p c n", p=128)),
                (f["w1"][:], a["L0_ffn_w1"][l]),
                (f["w2"][:, 0:NC - 1, :], a["L0_ffn_w2"][l, 0:128 * (NC - 1), :].rearrange("(c p) n -> p c n", p=128)),
                (f["w2"][0:CW[-1], NC - 1, :], a["L0_ffn_w2"][l, 128 * (NC - 1):HID, :]),
                (f["lg"][:], a["L0_ffn_ln_g"][l]), (f["lb"][:], a["L0_ffn_ln_b"][l]), (f["b2"][:], a["L0_ffn_b2"][l]),
                (f["b1"][:], a["L0_ffn_b1"][l]),
                (f["qk_scale"][:, 0, :], a["L0_ffn_q_scale"][l].partition_broadcast(128)),
                (f["qk_scale"][:, 1, :], a["L0_ffn_k_scale"][l].partition_broadcast(128)),
            ]
        FFN_LOADED = 16 * len(ffn_list)

        ON_DVE = ()
        ON_POOL = tuple(g for g in range(NG) if g not in ON_DVE)

        def wait_group(eng, on_pool, on_dve, i, g):
            if g < 0:
                i, g = i - 1, g + NG
            if below(i, 0):
                return
            mine, sem_ = (ON_DVE, on_dve) if g in ON_DVE else (ON_POOL, on_pool)
            eng.wait_ge(sem_, len(mine) * i + sum(x <= g for x in mine))

        def xs(i):
            return xT[:, bass.ds(2 * i, 2), 1:S + 1]

        def seqs(ap):
            return ap.rearrange("p (s t) -> p s t", s=2)

        block = ctx.enter_context(nc.Block())

        def pairs(eng, step):
            step(0, True, False)
            with eng.Fori(1, PAIRS - 1) as i:
                step(i, False, False)
            step(PAIRS - 1, False, True)

        def skewed(eng, stage):
            for n in range(3):
                stage(n, n % 2, n == 0, False)
            with eng.Fori(1, PAIRS // 2 - 1) as i:
                stage(2 * i + 1, 1, False, False)
                stage(2 * i + 2, 0, False, False)
            stage(PAIRS - 1, 1, False, True)

        @block.sync
        def _(sp):
            for dst, src in first_list:
                sp.dma_start(dst, src).then_inc(first_loaded, 16)
            for dst, src in load_list:
                sp.dma_start(dst, src).then_inc(weights, 16)
            for dst, src in ffn_list:
                sp.dma_start(dst, src).then_inc(ffn_loaded, 16)
            with sp.Fori(1, PAIRS) as i:
                sp.wait_ge(xt_ps, i)
                sp.dma_start(xin[:], x_pairs[i]).then_inc(x_in, 16)
            L, L0 = LNS, counted(LN_PER_STAGE, DEPTH)
            o_pairs = out.rearrange("(i s) (b p) d -> i p (s b) d", s=2, p=128)

            def store(n, q):
                sp.wait_ge(L["lev"], L0["lev"] + n + 1)
                sp.dma_start(o_pairs[n], fout[q][:]).then_inc(stored[q], 16)

            with sp.Fori(0, PAIRS // 2) as i:
                store(2 * i, 0)
                store(2 * i + 1, 1)
            for q in range(2):
                sp.wait_ge(stored[q], 16 * (PAIRS // 2))

        @block.tensor
        def _(pe):
            pe.wait_ge(first_loaded, FIRST_LOADED)
            pe.wait_ge(consts_p, 1)

            def transposes(n):
                if not below(n, 1):
                    pe.wait_ge(x_in, 16 * n)
                for b in range(XB):
                    mm = nc.tensor.transpose(pW[:, 0, 128 * b:128 * b + 128], xin[:, b, :], ident[:])
                mm.then_inc(xt_ps, 1)

            def u_rows(n):
                pe.wait_ge(x_t, n + 1)
                for h in range(NH):
                    mm = nc.tensor.matmul(pW[:, h, :], w1[:, 128 * h:128 * h + 128], xs(n), start=True, stop=True)
                mm.then_inc(u_ps, 1)

            def out_rows(n):
                pe.wait_ge(yg_done, n + 1)
                for h in range(NH):
                    mm = nc.tensor.matmul(pW[:, 0, :], wo[:, h, :], yg[:, h, :], start=(h == 0), stop=(h == NH - 1))
                mm.then_inc(wo_ps, 1)

            def bc_rows(n):
                pe.wait_ge(u_sig, n + 1)
                for h in range(NH):
                    mm = nc.tensor.matmul(pW[0:3 * BC, 0, :], wbc3[:, h, :, :].rearrange("p k n -> p (k n)"),
                                          u[:, h, :, :].rearrange("p s t -> p (s t)"), start=(h == 0), stop=(h == NH - 1))
                mm.then_inc(bc_ps, 1)

            def xdt_rows(n):
                pe.wait_ge(u_sig, n + 1)
                for h in range(NH):
                    mm = nc.tensor.matmul(pW[0:RANK, 1, :], wx[:, h, 0:RANK],
                                          u[:, h, :, :].rearrange("p s t -> p (s t)"), start=(h == 0), stop=(h == NH - 1))
                mm.then_inc(xdt_ps, 1)

            def dt_rows(n):
                pe.wait_ge(xdt_done, n + 1)
                for h in range(NH):
                    mm = nc.tensor.matmul(pW[:, h, :], wdt[:, 128 * h:128 * h + 128], xdt[:], start=True, stop=True)
                mm.then_inc(dt_ps, 1)

            def gate_rows(n):
                for h in range(NH):
                    mm = nc.tensor.matmul(pW[:, h, :], w2[:, 128 * h:128 * h + 128], xs(n), start=True, stop=True)
                mm.then_inc(gate_ps, 1)

            def b_rows(n, g, i0):
                if g == 0:
                    pe.wait_ge(bc_split, n + 1)
                if not below(i0 + g, 1):
                    pe.wait_ge(dbu, i0 + g)
                for k in range(2):
                    mm = nc.tensor.matmul(pB[:, k, :], onehot[:, 2 * g + k, :], bc_s[:], start=True, stop=True)
                mm.then_inc(b_ready, 1)
                wait_group(pe, c_ev, hc_dve, n, g - 1)
                for k in range(2):
                    mm = nc.tensor.matmul(pC[:, k, :], onehot[:, NST + 2 * g + k, :], bc_s[:], start=True, stop=True)
                mm.then_inc(c_ready, 1)

            def sum_states(i, g):
                wait_group(pe, hc_pool, hc_dve, i, g)
                for k in range(2):
                    for h in range(NH):
                        mm = nc.tensor.matmul(pY[:, h, :], ident[:], hc[g % 2][:, k, h, :], start=False,
                                              stop=(g == NG - 1 and k == 1), skip_group_check=True)
                mm.then_inc(ysum, 1)

            def variance_rows(n):
                pe.wait_ge(sq, n + 1)
                nc.tensor.matmul(pW[:, 1, :], ones_mean[:], rsq[:], start=True, stop=True).then_inc(var_ps, 1)

            def mean_rows(n):
                pe.wait_ge(resid, n + 1)
                nc.tensor.matmul(pW[:, 0, :], ones_mean[:], rb[:], start=True, stop=True).then_inc(mean_ps, 1)

            def step(i, first, last):
                for g in range(NG):
                    if g == 5 and not last:
                        pe.wait_ge(bc_f_done, i + 2)
                        dt_rows(i + 1)
                    if g < NG - 1:
                        b_rows(i, g + 1, NG * i)
                    if g == 0 and not last:
                        if first:
                            pe.wait_ge(sp_a, 1)
                        else:
                            pe.wait_ge(gate_e, i)
                        transposes(i + 1)
                    if g == 1 and not last:
                        u_rows(i + 1)
                    if g == 2 and not first:
                        if not last:
                            pe.wait_ge(u_b, i + 2)
                        else:
                            pe.wait_ge(gate_e, i)
                        out_rows(i - 1)
                    if g == 3:
                        if not first:
                            mean_rows(i - 1)
                    if g == 4 and not last:
                        xdt_rows(i + 1)
                        if not first:
                            pe.wait_ge(cent, i)
                        bc_rows(i + 1)
                    if g == 6:
                        if not last:
                            pe.wait_ge(sp_a, i + 2)
                        if not first:
                            variance_rows(i - 1)
                    if g == 7:
                        if not first:
                            pe.wait_ge(rstd_done, i)
                        gate_rows(i)
                        if not last:
                            b_rows(i + 1, 0, NG * (i + 1))
                    if g == 0 and not first:
                        sum_states(i - 1, NG - 1)
                    if g == 1:
                        if not first:
                            pe.wait_ge(yg_done, i)
                        else:
                            pe.wait_ge(b1_done, 1)
                        for h in range(NH):
                            mm = nc.tensor.matmul(pY[:, h, :], diagD[:, h, :], u[:, h, :, :].rearrange("p s t -> p (s t)"),
                                                  start=True, stop=False, skip_group_check=True)
                        mm.then_inc(y_init, 1)
                    if g > 0:
                        sum_states(i, g - 1)

            transposes(0)
            u_rows(0)
            pe.wait_ge(weights, LOADED)
            pe.wait_ge(consts_v, 1)
            pe.wait_ge(u_b, 1)
            xdt_rows(0)
            bc_rows(0)
            pe.wait_ge(bc_f_done, 1)
            dt_rows(0)
            pe.wait_ge(ffn_loaded, FFN_LOADED)
            for l in range(DEPTH):
                for c in range(2 * NC):
                    w = CW[c % NC]
                    c0 = 128 * (c % NC) + HID * (c // NC)
                    k = 2 * NC * l + c
                    mm = nc.tensor.matmul(pY[0:w, 0, k:k + 1], F[l]["w1"][:, c0:c0 + w], F[l]["lb"][:], start=True, stop=True)
            mm.then_inc(b1_ps, 1)
            b_rows(0, 0, 0)
            pairs(pe, step)
            sum_states(PAIRS - 1, NG - 1)
            pe.wait_ge(gate_e, PAIRS)
            out_rows(PAIRS - 1)
            mean_rows(PAIRS - 1)
            variance_rows(PAIRS - 1)
            pe.wait_ge(x_done, PAIRS)
            pe.wait_ge(ffn_loaded, FFN_LOADED)
            pe.wait_ge(tabs, 1)

            def up(l, i, c):
                f, Q, Q0 = F[l], FF, counted(FF_PER_LAYER, l)
                w = CW[c]
                rows = hn[:, bass.ds(i, 1), :].rearrange("p o t -> p (o t)")
                pe.wait_ge(LNS["lnorm"], PAIRS * l + i + 1)
                if not below(i, 1):
                    pe.wait_ge(Q["ge"], Q0["ge"] + NC * i + c - NC + 1)
                nc.tensor.matmul(pG(w, c), f["w1"][:, HID + 128 * c:HID + 128 * c + w], rows, start=True,
                                 stop=True).then_inc(Q["g"], 1)
                if not below(i, 1):
                    pe.wait_ge(Q["m"], Q0["m"] + NC * i + c - NC + 1)
                nc.tensor.matmul(pU(w, c), f["w1"][:, 128 * c:128 * c + w], rows, start=True,
                                 stop=True).then_inc(Q["u"], 1)

            def mean(l, n, vs):
                A, A0, L, L0 = ATT, counted(ATT_PER_LAYER, l), LNS, counted(LN_PER_STAGE, l)
                pe.wait_ge(L["lin"], L0["lin"] + n + 1)
                pe.wait_ge(A["v_ev"], A0["v_ev"] + vs)
                nc.tensor.matmul(pV[:], ones_mean[:], lin[:], start=True, stop=True).then_inc(L["lmean"], 1)

            def variance(l, n, vs):
                A, A0, L, L0 = ATT, counted(ATT_PER_LAYER, l), LNS, counted(LN_PER_STAGE, l)
                pe.wait_ge(L["lsq"], L0["lsq"] + n + 1)
                pe.wait_ge(A["v_ev"], A0["v_ev"] + vs)
                nc.tensor.matmul(pV[:], ones_mean[:], lsq[:], start=True, stop=True).then_inc(L["lvar"], 1)

            def attention(l):
                A, A0, f = ATT, counted(ATT_PER_LAYER, l), F[l]
                L, L0 = LNS, counted(LN_PER_STAGE, l)

                def qk_rows(t, j):
                    pe.wait_ge(A["ht"], A0["ht"] + t + 1)
                    if not below(t, 1):
                        pe.wait_ge(A["sqd"], A0["sqd"] + t)
                    for c in range(2):
                        mm = nc.tensor.matmul(pA[:, c, :], hT[:, j, :], f["wqkv"][:, INNER * c:INNER * (c + 1)],
                                              start=True, stop=True)
                    mm.then_inc(A["qk_ps"], 1)

                def v_rows(t, j):
                    if not below(t, 1):
                        pe.wait_ge(A["v_ev"], A0["v_ev"] + t)
                    nc.tensor.matmul(pV[:], hT[:, j, :], f["wqkv"][:, 2 * INNER:3 * INNER],
                                     start=True, stop=True).then_inc(A["v_ps"], 1)

                def turn_qk(t, j):
                    pe.wait_ge(A["qkd"], A0["qkd"] + t + 1)
                    if not below(t, 2):
                        pe.wait_ge(A["pt_ev"], A0["pt_ev"] + t - 1)
                    elif not below(t, 1):
                        pe.wait_ge(A["qk_ev"], A0["qk_ev"] + t)
                    for c in range(2):
                        for hp in range(HP):
                            mm = nc.tensor.transpose(pT[:, c, 128 * hp:128 * hp + 128],
                                                     qk[j % 2][:, c, 128 * hp:128 * hp + 128], ident[:])
                    mm.then_inc(A["tps"], 1)

                def sims(t, j, par):
                    if par == 0:
                        pe.wait_ge(A["qk_ev"], A0["qk_ev"] + t + 1)
                    pos = j % 2
                    cur, prev = qkT[j % 2], qkT[(j + 1) % 2]
                    if not below(t, 1):
                        pe.wait_ge(A["expd"], A0["expd"] + 2 * t - 1 + par)
                    nc.tensor.matmul(pS[:, par, :, :].rearrange("p h k -> p (h k)"), identb[:],
                                     maskb[:, pos, :, :].rearrange("p h k -> p (h k)"), start=True, stop=False,
                                     skip_group_check=True)
                    for hp in range(HP):
                        r = slice(64 * par, 64 * par + 64)
                        nc.tensor.matmul(pS[0:64, par, hp, 0:64], cur[r, 0, hp, 0:64], cur[r, 1, hp, 0:64],
                                         start=False, stop=True, skip_group_check=True)
                        if pos:
                            nc.tensor.matmul(pS[0:64, par, hp, 64:128], cur[r, 0, hp, 0:64], prev[r, 1, hp, 64:128],
                                             start=False, stop=True, skip_group_check=True)
                        mm = nc.tensor.matmul(pS[64:128, par, hp, :], cur[r, 0, hp, 64:128], cur[r, 1, hp, :],
                                              start=False, stop=True, skip_group_check=True)
                    mm.then_inc(A["simd"], 1)

                def turn_p(t, j):
                    for par in range(2):
                        pe.wait_ge(A["pnorm"], A0["pnorm"] + 2 * t + par + 1)
                        for hp in range(HP):
                            mm = nc.tensor.transpose(pT[:, par, 128 * hp:128 * hp + 128], P[j % 2][:, par * HP + hp, :], ident[:])
                    mm.then_inc(A["ptp"], 1)

                def mix(t, j):
                    pos = j % 2
                    pe.wait_ge(A["pt_ev"], A0["pt_ev"] + t + 1)
                    pe.wait_ge(A["v_ev"], A0["v_ev"] + t + 1)
                    if not below(t, 1):
                        pe.wait_ge(A["o_ev"], A0["o_ev"] + t)
                    for hp in range(HP):
                        for par in range(2):
                            hc_ = slice(HD * (2 * hp + par), HD * (2 * hp + par + 1))
                            o = pE[64 * par:64 * par + 64, 128 * hp:128 * hp + 128]
                            nc.tensor.matmul(o[:, 64:128], V[j][:, hc_], PT[:, par * HP + hp, 64:128], start=True, stop=True)
                            if pos:
                                mm = nc.tensor.matmul(o[:, 0:64], Vm[j][:, hc_], PT[:, par * HP + hp, 0:64], start=True, stop=True)
                            else:
                                mm = nc.tensor.matmul(o[:, 0:64], V[j][0:64, hc_], PT[0:64, par * HP + hp, 0:64], start=True, stop=True)
                    mm.then_inc(A["pvd"], 1)

                def project(i):
                    pe.wait_ge(A["o_ev"], A0["o_ev"] + XB * (i + 1))
                    for c in range(HP):
                        mm = nc.tensor.matmul(pE[:], f["wo"][:, c, :], oT[:, c, :], start=(c == 0), stop=(c == HP - 1))
                    mm.then_inc(A["wod"], 1)

                def step(i, first, last):
                    for j in range(XB):
                        t = XB * i + j
                        if last and j == XB - 1:
                            up(l, 0, 0)
                            pe.wait_ge(A["expd"], A0["expd"] + 2 * TILES)
                            up(l, 0, 1)
                        turn_p(t, j)
                        if j == 0 and not first:
                            project(i - 1)
                        if not last:
                            qk_rows(t + 4, j)
                        if not (last and j >= XB - 2):
                            turn_qk(t + 2, (j + 2) % XB)
                        if j == 1 and not first:
                            mean(l, i - 1, t + 3)
                        if j == 2 and not first:
                            variance(l, i - 1, TILES if last else t + 3)
                        if j == 0 and not first:
                            pe.wait_ge(A["xud"], A0["xud"] + i)
                        mix(t, j)
                        if not (last and j >= XB - 2):
                            sims(t + 2, (j + 2) % XB, 0)
                        if not first and not last:
                            if j == 1:
                                pe.wait_ge(L["lcent"], L0["lcent"] + i)
                            if j == 2:
                                pe.wait_ge(L["lrl"], L0["lrl"] + i)
                        if not (last and j >= XB - 3):
                            v_rows(t + 3, (j + 3) % XB)
                        if not (last and j >= XB - 2):
                            sims(t + 2, (j + 2) % XB, 1)

                qk_rows(0, 0)
                v_rows(0, 0)
                qk_rows(1, 1)
                turn_qk(0, 0)
                sims(0, 0, 0)
                sims(0, 0, 1)
                qk_rows(2, 2)
                v_rows(1, 1)
                turn_qk(1, 1)
                sims(1, 1, 0)
                v_rows(2, 2)
                sims(1, 1, 1)
                qk_rows(3, 3)
                pairs(pe, step)
                project(PAIRS - 1)
                up(l, 0, 2)
                mean(l, PAIRS - 1, TILES)

            def last_norm(k):
                L, L0 = LNS, counted(LN_PER_STAGE, k)

                def mean(n, q):
                    pe.wait_ge(L["lin"], L0["lin"] + n + 1)
                    if not below(n, 2):
                        pe.wait_ge(L["lcent"], L0["lcent"] + n - 1)
                    nc.tensor.matmul(pLm[:, q, :], ones_mean[:], lin_b[q][:], start=True, stop=True).then_inc(L["lmean"], 1)

                def variance(n, q):
                    pe.wait_ge(L["lsq"], L0["lsq"] + n + 1)
                    if not below(n, 2):
                        pe.wait_ge(L["lrl"], L0["lrl"] + n - 1)
                    nc.tensor.matmul(pLv[:, q, :], ones_mean[:], lsq_b[q][:], start=True, stop=True).then_inc(L["lvar"], 1)

                def turn(n, q):
                    pe.wait_ge(L["lnorm"], L0["lnorm"] + n + 1)
                    if not below(n, 2):
                        pe.wait_ge(L["lev"], L0["lev"] + n - 1)
                    for b in range(XB):
                        mm = nc.tensor.transpose(pLt[:, q, 128 * b:128 * b + 128], foT[q][:, 128 * b:128 * b + 128], ident[:])
                    mm.then_inc(L["ltp"], 1)

                def stage(n, q, first, last):
                    if not last:
                        mean(n + 1, 1 - q)
                    variance(n, q)
                    if not first:
                        turn(n - 1, 1 - q)

                mean(0, 0)
                skewed(pe, stage)
                turn(PAIRS - 1, 1)

            def feed(l):
                f, Q, Q0 = F[l], FF, counted(FF_PER_LAYER, l)
                def down(i, c):
                    w = CW[c]
                    pe.wait_ge(Q["m"], Q0["m"] + NC * i + c + 1)
                    if c == 0 and not below(i, 1):
                        pe.wait_ge(Q["x"], Q0["x"] + i)
                    nc.tensor.matmul(pO[:], f["w2"][0:w, c, :], mm_[0:w, c, :], start=(c == 0), stop=(c == NC - 1)).then_inc(Q["o"], 1)

                def step(i):
                    up(l, i, 0)
                    down(i - 1, NC - 1)
                    up(l, i, 1)
                    down(i, 0)
                    if below(i, 2):
                        variance(l, PAIRS - 1, TILES)
                    up(l, i, 2)
                    down(i, 1)

                down(0, 0)
                down(0, 1)
                step(1)
                with pe.Fori(2, PAIRS) as i:
                    step(i)
                down(PAIRS - 1, NC - 1)

            for l in range(DEPTH):
                attention(l)
                feed(l)
                pe.wait_ge(FF["x"], PAIRS * (l + 1))
            last_norm(DEPTH)

        @block.scalar
        def _(act):
            nc.scalar.preload_act_table_set("natural_log_exp_and_others")
            act.wait_ge(consts_p, 1)
            act.wait_ge(first_loaded, FIRST_LOADED)

            def x_copy(n):
                act.wait_ge(xt_ps, n + 1)
                nc.scalar.copy(xs(n), seqs(pW[:, 0, :])).then_inc(x_t, 1)

            def u_bias(n, first):
                act.wait_ge(u_ps, n + 1)
                if not first:
                    act.wait_ge(u_conv, n)
                for h in range(NH):
                    mm = nc.scalar.activation(ub[:, h, :, 3:S + 3], seqs(pW[:, h, :]), ACT.Identity, bias=b1[:, h:h + 1])
                mm.then_inc(u_b, 1)

            def newest_tap(n):
                act.wait_ge(u_b, n + 1)
                if not below(n, 1):
                    act.wait_ge(u_sig, n)
                for h in range(NH):
                    mm = nc.scalar.activation(uacc[:, h, :, :], ub[:, h, :, 3:S + 3], ACT.Identity, scale=cw[:, h, 3:4],
                                              bias=cb[:, h:h + 1])
                mm.then_inc(tapped, 1)

            def u_sigmoid(n, first):
                act.wait_ge(u_conv, n + 1)
                nc.scalar.activation(uacc[:], uacc[:], ACT.Exp, scale=-1.0).then_inc(sig_e, 1)
                act.wait_ge(sig_e, n + 1)
                nc.scalar.activation(uacc[:], uacc[:], ACT.Ln, bias=one[:]).then_inc(sig_l, 1)
                if not first:
                    act.wait_ge(y_init, n)
                    act.wait_ge(du_done, n)
                act.wait_ge(sig_l, n + 1)
                nc.scalar.activation(u[:], uacc[:], ACT.Exp, scale=-1.0).then_inc(u_sig, 1)

            def bc_copy(n, first):
                act.wait_ge(bc_ps, n + 1)
                if not first:
                    act.wait_ge(bc_split, n)
                nc.scalar.copy(bc_f[:], pW[0:3 * BC, 0, :]).then_inc(bc_f_done, 1)

            def xdt_copy(n):
                act.wait_ge(xdt_ps, n + 1)
                nc.scalar.copy(xdt[:], pW[0:RANK, 1, :]).then_inc(xdt_done, 1)

            def softplus(n, first):
                act.wait_ge(dt_ps, n + 1)
                if not first:
                    act.wait_ge(delta_done, n)
                for h in range(NH):
                    nc.scalar.activation(sp_m[:, h, :], pW[:, h, :], ACT.Relu, bias=bdt[:, h:h + 1])
                for h in range(NH):
                    mm = nc.scalar.activation(sp_l[:, h, :], pW[:, h, :], ACT.Abs, bias=bdt[:, h:h + 1])
                mm.then_inc(sp_a, 1)
                act.wait_ge(sp_a, n + 1)
                nc.scalar.activation(sp_l[:], sp_l[:], ACT.Exp, scale=-1.0).then_inc(sp_e, 1)
                act.wait_ge(sp_e, n + 1)
                nc.scalar.activation(sp_l[:], sp_l[:], ACT.Ln, bias=one[:]).then_inc(sp_done, 1)

            def gates(n, first):
                act.wait_ge(gate_ps, n + 1)
                if not first:
                    act.wait_ge(yg_done, n)
                for h in range(NH):
                    mm = nc.scalar.activation(gate[:, h, :], pW[:, h, :], ACT.Exp, scale=-1.0, bias=nb2[:, h:h + 1])
                mm.then_inc(gate_e, 1)
                act.wait_ge(gate_e, n + 1)
                nc.scalar.activation(gate[:], gate[:], ACT.Ln, bias=one[:]).then_inc(gate_l, 1)
                act.wait_ge(gate_l, n + 1)
                nc.scalar.activation(gate[:], gate[:], ACT.Exp, scale=-1.0).then_inc(gate_done, 1)

            def decay(n, g, k0):
                if g == 0:
                    act.wait_ge(delta_done, n + 1)
                if not below(k0 + g, NDA):
                    act.wait_ge(scan, k0 + g - NDA + 1)
                for k in range(2):
                    for h in range(NH):
                        mm = nc.scalar.activation(dA[g % NDA][:, k, h, :, 1:S], delta[:, h, :, 1:S], ACT.Exp,
                                                  scale=nA[:, h, 2 * g + k:2 * g + k + 1])
                mm.then_inc(da_ready, 1)

            def c_copy(n, g):
                act.wait_ge(c_ready, NG * n + g + 1)
                if g - 2 in ON_POOL or g < 2 and g - 2 + NG in ON_POOL:
                    wait_group(act, hc_pool, hc_dve, n, g - 2)
                nc.scalar.copy(csb[:, g % 2, :, :], pC[:]).then_inc(c_ev, 1)

            def square(n):
                act.wait_ge(cent, n + 1)
                if not below(n, 1):
                    act.wait_ge(var_ps, n)
                nc.scalar.activation(rsq[:], rc[:], ACT.Square).then_inc(sq, 1)

            def rsqrt(n):
                act.wait_ge(var_ps, n + 1)
                if not below(n, 1):
                    act.wait_ge(x_done, n)
                nc.scalar.activation(rstd[:], pW[:, 1, :], ACT.Ln, bias=eps[:]).then_inc(rstd_l, 1)
                act.wait_ge(rstd_l, n + 1)
                nc.scalar.activation(rstd[:], rstd[:], ACT.Exp, scale=-0.5).then_inc(rstd_done, 1)

            def step(i, first, last):
                for g in range(NG):
                    if g == 0 and not last:
                        x_copy(i + 1)
                    if g < NG - 1:
                        c_copy(i, g + 1)
                    if g == 1 and not last:
                        u_bias(i + 1, False)
                        newest_tap(i + 1)
                    if g == 3 and not last:
                        u_sigmoid(i + 1, False)
                    if g == 5 and not last:
                        softplus(i + 1, False)
                    if g + 2 < NG:
                        decay(i, g + 2, NG * i)
                    if g == 4 and not last:
                        xdt_copy(i + 1)
                        bc_copy(i + 1, False)
                    if g == 4 and not first:
                        square(i - 1)
                    if g == 6 and not first:
                        rsqrt(i - 1)
                    if g == 7:
                        if not last:
                            decay(i + 1, 0, NG * (i + 1))
                            if 0 in ON_POOL:
                                c_copy(i + 1, 0)
                        gates(i, first)
                        if not last:
                            decay(i + 1, 1, NG * (i + 1))

            x_copy(0)
            u_bias(0, True)
            newest_tap(0)
            act.wait_ge(weights, LOADED)
            nc.scalar.activation(nA[:], nA[:], ACT.Exp).then_inc(a_exp, 1)
            u_sigmoid(0, True)
            act.wait_ge(consts_v, 1)
            xdt_copy(0)
            bc_copy(0, True)
            softplus(0, True)
            decay(0, 0, 0)
            if 0 in ON_POOL:
                c_copy(0, 0)
            decay(0, 1, 0)
            pairs(act, step)
            square(PAIRS - 1)
            rsqrt(PAIRS - 1)

            act.wait_ge(x_done, PAIRS)
            act.wait_ge(ffn_loaded, FFN_LOADED)
            nc.scalar.copy(x0T[:], xT[:, :, 1:S + 1]).then_inc(x0_saved, 1)

            def norm_square(l, n):
                L, L0 = LNS, counted(LN_PER_STAGE, l)
                act.wait_ge(L["lcent"], L0["lcent"] + n + 1)
                nc.scalar.activation(lsq[:], lc[:], ACT.Square).then_inc(L["lsq"], 1)

            def norm_ln(l, n):
                L, L0 = LNS, counted(LN_PER_STAGE, l)
                act.wait_ge(L["lvar"], L0["lvar"] + n + 1)
                if not below(n, 1):
                    act.wait_ge(L["lnorm"], L0["lnorm"] + n)
                nc.scalar.activation(lr[:], pV[:], ACT.Ln, bias=eps[:]).then_inc(L["lrl"], 1)

            def norm_exp(l, n):
                L, L0 = LNS, counted(LN_PER_STAGE, l)
                act.wait_ge(L["lrl"], L0["lrl"] + n + 1)
                nc.scalar.activation(lr[:], lr[:], ACT.Exp, scale=-0.5).then_inc(L["lrstd"], 1)

            def attention(l):
                A, A0 = ATT, counted(ATT_PER_LAYER, l)
                L, L0 = LNS, counted(LN_PER_STAGE, l)

                def square(t):
                    act.wait_ge(A["rot"], A0["rot"] + t + 1)
                    if not below(t, 1):
                        act.wait_ge(A["ssr"], A0["ssr"] + t)
                    nc.scalar.activation(qk_sq[:], pA[:], ACT.Square).then_inc(A["sqd"], 1)

                def lengths_ln(t):
                    act.wait_ge(A["ssd"], A0["ssd"] + t + 1)
                    if not below(t, 1):
                        act.wait_ge(A["lsd"], A0["lsd"] + t)
                    nc.scalar.activation(lns[:], ssc[:], ACT.Ln).then_inc(A["lnd"], 1)

                def lengths_exp(t, j):
                    act.wait_ge(A["lsd"], A0["lsd"] + t + 1)
                    if not below(t, 2):
                        act.wait_ge(A["mxs"], A0["mxs"] + t - 1)
                        act.wait_ge(A["qkd"], A0["qkd"] + t - 1)
                    nc.scalar.activation(rn[j % 2][:], lsum[:], ACT.Exp, scale=-0.5).then_inc(A["rnd"], 1)

                def qk_copy(t, j):
                    act.wait_ge(A["tps"], A0["tps"] + t + 1)
                    nc.scalar.copy(qkT[j % 2][:].rearrange("p c h k -> p (c h k)"), pT[:].rearrange("p c n -> p (c n)")).then_inc(A["qk_ev"], 1)

                def p_copy(t):
                    act.wait_ge(A["ptp"], A0["ptp"] + t + 1)
                    nc.scalar.copy(PT[:].rearrange("p h k -> p (h k)"), pT[:].rearrange("p c n -> p (c n)")).then_inc(A["pt_ev"], 1)

                def exps(t, j, par):
                    act.wait_ge(A["mxd"], A0["mxd"] + 2 * t + par + 1)
                    if not below(t, 1):
                        act.wait_ge(A["rsd"], A0["rsd"] + 2 * t - 1 + par)
                    for hp in range(HP):
                        h = par * HP + hp
                        mm = nc.scalar.activation(P[j % 2][:, h, :], pS[:, par, hp, :], ACT.Exp, scale=sc8[j % 2][:, h:h + 1],
                                                  bias=nb[j % 2][:, h:h + 1], accum_out=psums[:, h:h + 1])
                    mm.then_inc(A["expd"], 1)

                def o_copy(t, j):
                    act.wait_ge(A["pvd"], A0["pvd"] + t + 1)
                    nc.scalar.copy(oT[:, :, 128 * j:128 * j + 128], pE[:].rearrange("p (h q) -> p h q", h=HP)).then_inc(A["o_ev"], 1)

                def step(i, first, last):
                    for j in range(XB):
                        t = XB * i + j
                        p_copy(t)
                        if not (last and j == XB - 1):
                            exps(t + 1, j + 1, 0)
                        if not (last and j >= XB - 2):
                            qk_copy(t + 2, j)
                        if not (last and j >= XB - 3):
                            lengths_ln(t + 3)
                        if j == 2 and not first:
                            norm_ln(l, i - 1)
                        if not (last and j == XB - 1):
                            exps(t + 1, j + 1, 1)
                        if not last:
                            square(t + 4)
                        o_copy(t, j)
                        if not (last and j >= XB - 3):
                            lengths_exp(t + 3, j + 3)
                        if j == 1 and not first:
                            norm_square(l, i - 1)
                        if j == 2 and not first:
                            norm_exp(l, i - 1)

                square(0)
                lengths_ln(0)
                lengths_exp(0, 0)
                square(1)
                qk_copy(0, 0)
                lengths_ln(1)
                exps(0, 0, 0)
                lengths_exp(1, 1)
                exps(0, 0, 1)
                qk_copy(1, 1)
                square(2)
                lengths_ln(2)
                lengths_exp(2, 2)
                square(3)
                pairs(act, step)

            def last_norm(k):
                L, L0 = LNS, counted(LN_PER_STAGE, k)

                def square(n, q):
                    act.wait_ge(L["lcent"], L0["lcent"] + n + 1)
                    if not below(n, 2):
                        act.wait_ge(L["lvar"], L0["lvar"] + n - 1)
                    nc.scalar.activation(lsq_b[q][:], lc_b[q][:], ACT.Square).then_inc(L["lsq"], 1)

                def rsqrt(n, q):
                    act.wait_ge(L["lvar"], L0["lvar"] + n + 1)
                    if not below(n, 2):
                        act.wait_ge(L["lnorm"], L0["lnorm"] + n - 1)
                    nc.scalar.activation(lr_b[q][:], pLv[:, q, :], ACT.Ln, bias=eps[:]).then_inc(L["lrl"], 1)
                    act.wait_ge(L["lrl"], L0["lrl"] + n + 1)
                    nc.scalar.activation(lr_b[q][:], lr_b[q][:], ACT.Exp, scale=-0.5).then_inc(L["lrstd"], 1)

                def rows_copy(n, q, reused):
                    act.wait_ge(L["ltp"], L0["ltp"] + n + 1)
                    if reused is not None:
                        act.wait_ge(stored[q], 16 * reused)
                    nc.scalar.copy(fout[q][:].rearrange("p b d -> p (b d)"), pLt[:, q, :]).then_inc(L["lev"], 1)

                square(0, 0)
                square(1, 1)
                rsqrt(0, 0)
                square(2, 0)
                rsqrt(1, 1)
                rows_copy(0, 0, None)
                square(3, 1)
                rsqrt(2, 0)
                rows_copy(1, 1, None)
                with act.Fori(1, PAIRS // 2 - 1) as i:
                    square(2 * i + 2, 0)
                    rsqrt(2 * i + 1, 1)
                    rows_copy(2 * i, 0, i)
                    square(2 * i + 3, 1)
                    rsqrt(2 * i + 2, 0)
                    rows_copy(2 * i + 1, 1, i)
                rsqrt(PAIRS - 1, 1)
                rows_copy(PAIRS - 2, 0, PAIRS // 2 - 1)
                rows_copy(PAIRS - 1, 1, PAIRS // 2 - 1)

            def feed(l):
                f, Q, Q0 = F[l], FF, counted(FF_PER_LAYER, l)
                act.wait_ge(b1_done, 1)

                def step(i, first):
                    for c in range(NC):
                        w = CW[c]
                        act.wait_ge(Q["g"], Q0["g"] + NC * i + c + 1)
                        if not first:
                            act.wait_ge(Q["m"], Q0["m"] + NC * i + c - NC + 1)
                        nc.scalar.activation(gl[0:w, c, :], pG(w, c), ACT.Gelu,
                                             bias=f["b1"][0:w, NC + c:NC + c + 1]).then_inc(Q["ge"], 1)

                nc.scalar.preload_act_table_set("gelu_and_others")
                step(0, True)
                norm_square(l, PAIRS - 1)
                step(1, False)
                nc.scalar.preload_act_table_set("natural_log_exp_and_others")
                norm_ln(l, PAIRS - 1)
                norm_exp(l, PAIRS - 1)
                nc.scalar.preload_act_table_set("gelu_and_others")
                with act.Fori(2, PAIRS) as i:
                    step(i, False)

            for l in range(DEPTH):
                if l:
                    nc.scalar.preload_act_table_set("natural_log_exp_and_others")
                attention(l)
                feed(l)
                act.wait_ge(FF["x"], PAIRS * (l + 1))
            nc.scalar.preload_act_table_set("natural_log_exp_and_others")
            last_norm(DEPTH)

        @block.vector
        def _(dve):
            def conv(n, first):
                for k in range(3):
                    dve.wait_ge(tapped, 3 * n + k + 1)
                    for h in range(NH):
                        mm = nc.vector.scalar_tensor_tensor(out=uacc[:, h, :, :], in0=ub[:, h, :, k:k + S],
                                                            scalar=cw[:, h, k:k + 1], in1=uacc[:, h, :, :],
                                                            op0=ALU.mult, op1=ALU.add)
                    mm.then_inc(tapped if k < 2 else u_conv, 1)

            def inject(n, g, k0):
                dve.wait_ge(b_ready, k0 + g + 1)
                if g == 0:
                    dve.wait_ge(du_done, n + 1)
                wait_group(dve, hc_pool, hc_dve, n, g - NHB)
                nc.vector.tensor_tensor(hb[g % NHB][:], du[:].rearrange("p (h t) -> p h t", h=NH).unsqueeze(1).to_broadcast([128, 2, NH, T]),
                                        pB[:].unsqueeze(2).to_broadcast([128, 2, NH, T]), ALU.mult).then_inc(dbu, 1)

            def recur(g, k0):
                dve.wait_ge(dbu, k0 + g + 1)
                dve.wait_ge(da_ready, k0 + g + 1)
                flat = hb[g % NHB][:].rearrange("p k h t -> p (k h t)")
                nc.vector.tensor_tensor_scan(flat, dA[g % NDA][:].rearrange("p k h s t -> p (k h s t)"), flat, 0.0,
                                             ALU.mult, ALU.add).then_inc(scan, 1)

            def product(n, g):
                dve.wait_ge(scan, NG * n + g + 1)
                dve.wait_ge(c_ready, NG * n + g + 1)
                if not below(NG * n + g, 2):
                    dve.wait_ge(ysum, NG * n + g - 1)
                nc.vector.tensor_tensor(hc[g % 2][:], hb[g % NHB][:], pC[:].unsqueeze(2).to_broadcast([128, 2, NH, T]),
                                        ALU.mult).then_inc(hc_dve, 1)

            def y_gate(n, k1):
                dve.wait_ge(ysum, k1)
                dve.wait_ge(gate_done, n + 1)
                if not below(n, 1):
                    dve.wait_ge(wo_ps, n)
                nc.vector.tensor_tensor(yg[:], pY[:], gate[:], ALU.mult).then_inc(yg_done, 1)

            def residual(n):
                dve.wait_ge(wo_ps, n + 1)
                nc.vector.scalar_tensor_tensor(out=seqs(rb[:]), in0=seqs(pW[:, 0, :]), scalar=bo[:, 0:1], in1=xs(n),
                                               op0=ALU.add, op1=ALU.add).then_inc(resid, 1)

            def center(n):
                dve.wait_ge(mean_ps, n + 1)
                nc.vector.tensor_tensor(rc[:], rb[:], pW[:, 0, :], ALU.subtract).then_inc(cent, 1)

            def normal(n):
                dve.wait_ge(rstd_done, n + 1)
                nc.vector.tensor_tensor(xs(n), seqs(rc[:]), seqs(rstd[:]), ALU.mult).then_inc(x_done, 1)

            def delta_add(n, k1):
                dve.wait_ge(sp_done, n + 1)
                if k1 is not None:
                    dve.wait_ge(da_ready, k1)
                nc.vector.tensor_tensor(delta[:].rearrange("p h s t -> p (h s t)"), sp_m[:].rearrange("p h t -> p (h t)"),
                                        sp_l[:].rearrange("p h t -> p (h t)"), ALU.add).then_inc(delta_done, 1)

            def du_mul(n):
                dve.wait_ge(delta_done, n + 1)
                nc.vector.tensor_tensor(du[:], delta[:].rearrange("p h s t -> p (h s t)"),
                                        u[:].rearrange("p h s t -> p (h s t)"), ALU.mult).then_inc(du_done, 1)

            def step(i, first, last):
                for g in range(NG):
                    inject(i, g, NG * i)
                    if g == NG - 1 and not last:
                        delta_add(i + 1, NG * i + NG)
                    recur(g, NG * i)
                    if g == NG - 1 and not last:
                        du_mul(i + 1)
                    if g in ON_DVE:
                        product(i, g)
                    if g == 2 and not last:
                        conv(i + 1, False)
                    if not first:
                        if g == 1:
                            y_gate(i - 1, NG * i)
                        if g == 2:
                            residual(i - 1)
                        if g == 3:
                            center(i - 1)
                        if g == 7:
                            normal(i - 1)

            dve.wait_ge(first_loaded, FIRST_LOADED)
            dve.wait_ge(consts_p, 1)
            conv(0, True)
            dve.wait_ge(weights, LOADED)
            nc.vector.tensor_copy(onehot[:], onehot_src[:].unsqueeze(2).to_broadcast([3 * BC, BC, 128]))
            for k in range(3):
                nc.vector.tensor_copy(wbc3[:, :, k, :], wx[:, :, RANK:RANK + BC])
            for h in range(NH):
                nc.vector.tensor_scalar(diagD[:, h, :], ident[:], dsk[:, h:h + 1], None, ALU.mult)
            nc.vector.tensor_scalar(nb2[:], nb2[:], -1.0, None, ALU.mult)
            dve.wait_ge(a_exp, 1)
            nc.vector.tensor_scalar(nA[:], nA[:], -1.0, None, ALU.mult).then_inc(consts_v, 1)
            dve.wait_ge(ffn_loaded, FFN_LOADED)
            nc.vector.tensor_copy(identb[:], ident[:])
            nc.vector.tensor_copy(maskb[:], maskf[:].unsqueeze(2).to_broadcast([128, 2, 4, 128]))
            for l in range(DEPTH):
                f = F[l]
                for pos in range(2):
                    nc.vector.tensor_tensor(f["tc"][:, pos], rot_c[:, pos], f["qk_scale"][:], ALU.mult)
                    for r in range(2):
                        mm = nc.vector.tensor_tensor(f["ts"][:, pos, :, 32 * r:32 * r + 32], rot_s[:, pos, :, 32 * r:32 * r + 32],
                                                     f["qk_scale"][:, :, 32 - 32 * r:64 - 32 * r], ALU.mult)
            mm.then_inc(tabs, 1)
            delta_add(0, None)
            du_mul(0)
            dve.wait_ge(b1_ps, 1)
            for l in range(DEPTH):
                b = F[l]["b1"]
                for c in (0, NC):
                    k, e = 2 * NC * l + c, c + NC - 1
                    nc.vector.tensor_tensor(b[:, c:e], b[:, c:e], pY[:, 0, k:k + NC - 1], ALU.add)
                    mm = nc.vector.tensor_tensor(b[0:CW[-1], e:e + 1], b[0:CW[-1], e:e + 1],
                                                 pY[0:CW[-1], 0, k + NC - 1:k + NC], ALU.add)
            mm.then_inc(b1_done, 1)
            pairs(dve, step)
            y_gate(PAIRS - 1, NG * PAIRS)
            residual(PAIRS - 1)
            center(PAIRS - 1)
            normal(PAIRS - 1)
            dve.wait_ge(x_done, PAIRS)
            dve.wait_ge(tabs, 1)

            def norm_in(l, n):
                L = LNS
                nc.vector.tensor_copy(seqs(lin[:])[0:64], xs(n)[0:64])
                nc.vector.tensor_copy(seqs(lin[:])[64:128], xT[64:128, bass.ds(2 * n, 2), 0:S]).then_inc(L["lin"], 1)

            def norm_center(l, n):
                L, L0 = LNS, counted(LN_PER_STAGE, l)
                dve.wait_ge(L["lmean"], L0["lmean"] + n + 1)
                nc.vector.tensor_tensor(lc[:], lin[:], pV[:], ALU.subtract).then_inc(L["lcent"], 1)

            def norm_out(l, n):
                L, L0 = LNS, counted(LN_PER_STAGE, l)
                dve.wait_ge(L["lrstd"], L0["lrstd"] + n + 1)
                nc.vector.scalar_tensor_tensor(out=hn[:, bass.ds(n, 1), :].rearrange("p o t -> p (o t)"), in0=lc[:],
                                               scalar=F[l]["lg"][:, 0:1], in1=lr[:], op0=ALU.mult, op1=ALU.mult
                                               ).then_inc(L["lnorm"], 1)

            def attention(l):
                A, A0, f = ATT, counted(ATT_PER_LAYER, l), F[l]
                L, L0 = LNS, counted(LN_PER_STAGE, l)

                def shift(n, j):
                    t, pos = XB * n + j, j % 2
                    if not below(t, XB):
                        dve.wait_ge(A["v_ps"], A0["v_ps"] + t - XB + 1)
                    sq_ = bass.ds(2 * n + j // 2, 1)
                    nc.vector.tensor_copy(hT[0:64, j, :], xT[0:64, sq_, 1 + 128 * pos:129 + 128 * pos].rearrange("p o t -> p (o t)"))
                    nc.vector.tensor_copy(hT[64:128, j, :], xT[64:128, sq_, 128 * pos:128 + 128 * pos].rearrange("p o t -> p (o t)")).then_inc(A["ht"], 1)

                def rotate(t, j):
                    pos = j % 2
                    dve.wait_ge(A["qk_ps"], A0["qk_ps"] + t + 1)
                    if not below(t, 2):
                        dve.wait_ge(A["addd"], A0["addd"] + t - 1)
                    v4 = lambda x: x[:].rearrange("p c (h d) -> p c h d", d=HD)
                    nc.vector.tensor_tensor(v4(t1[j % 2]), v4(pA), f["tc"][:, pos].unsqueeze(2).to_broadcast([128, 2, HEADS, HD]), ALU.mult)
                    for r in range(2):
                        o, n_ = 32 * r, 32 - 32 * r
                        mm = nc.vector.tensor_tensor(v4(t2[j % 2])[:, :, :, o:o + 32], v4(pA)[:, :, :, n_:n_ + 32],
                                                     f["ts"][:, pos, :, o:o + 32].unsqueeze(2).to_broadcast([128, 2, HEADS, 32]), ALU.mult)
                    mm.then_inc(A["rot"], 1)

                def lengths(t):
                    dve.wait_ge(A["sqd"], A0["sqd"] + t + 1)
                    nc.vector.tensor_reduce(ss[:], qk_sq[:].rearrange("p c (h d) -> p (c h) d", d=HD), AX.X, ALU.add).then_inc(A["ssr"], 1)
                    dve.wait_ge(A["ssr"], A0["ssr"] + t + 1)
                    if not below(t, 1):
                        dve.wait_ge(A["lnd"], A0["lnd"] + t)
                    nc.vector.tensor_scalar(ssc[:, 0, :], ss[:], 2.0 ** -60, 2.0 ** 60, ALU.max, ALU.min).then_inc(A["ssl"], 1)
                    dve.wait_ge(A["ssl"], A0["ssl"] + t + 1)
                    nc.vector.reciprocal(ssi[:], ssc[:, 0, :]).then_inc(A["ssi"], 1)
                    dve.wait_ge(A["ssi"], A0["ssi"] + t + 1)
                    nc.vector.scalar_tensor_tensor(out=ssc[:, 1, :], in0=ss[:], scalar=LEN_MIN, in1=ssi[:],
                                                   op0=ALU.max, op1=ALU.mult).then_inc(A["ssd"], 1)

                def log_sum(t):
                    dve.wait_ge(A["lnd"], A0["lnd"] + t + 1)
                    if not below(t, 1):
                        dve.wait_ge(A["rnd"], A0["rnd"] + t)
                    nc.vector.tensor_tensor(lsum[:], lns[:, 0, :], lns[:, 1, :], ALU.add).then_inc(A["lsd"], 1)

                def scales(t, j):
                    dve.wait_ge(A["rnd"], A0["rnd"] + t + 1)
                    nc.vector.tensor_scalar(sc8[j % 2][:].rearrange("p (c h) -> p c h", c=2),
                                            rn[j % 2][:, 0:HEADS].rearrange("p (h c) -> p c h", c=2), 8.0, None, ALU.mult).then_inc(A["mxs"], 1)

                def maxima(t, j, par):
                    dve.wait_ge(A["simd"], A0["simd"] + 2 * t + par + 1)
                    hs = slice(HP * par, HP * par + HP)
                    nc.vector.tensor_reduce(mx[:, hs], pS[:, par, :, :], AX.X, ALU.max).then_inc(A["mxr"], 1)
                    dve.wait_ge(A["mxr"], A0["mxr"] + 2 * t + par + 1)
                    dve.wait_ge(A["mxs"], A0["mxs"] + t + 1)
                    nc.vector.scalar_tensor_tensor(out=nb[j % 2][:, hs], in0=mx[:, hs], scalar=-1.0, in1=sc8[j % 2][:, hs],
                                                   op0=ALU.mult, op1=ALU.mult).then_inc(A["mxd"], 1)

                def v_copy(t, j):
                    dve.wait_ge(A["v_ps"], A0["v_ps"] + t + 1)
                    nc.vector.tensor_copy(V[j][:], pV[:])
                    if j % 2:
                        mm = nc.vector.tensor_copy(Vm[j][0:64, :], pV[0:64, :])
                    else:
                        mm = nc.vector.tensor_copy(Vm[j + 1][64:128, :], pV[64:128, :])
                    mm.then_inc(A["v_ev"], 1)

                def inverse(t, par):
                    dve.wait_ge(A["expd"], A0["expd"] + 2 * t + par + 1)
                    if not below(t, 1):
                        dve.wait_ge(A["pnorm"], A0["pnorm"] + 2 * t - 1 + par)
                    hs = slice(HP * par, HP * par + HP)
                    nc.vector.reciprocal(rs[:, hs], psums[:, hs]).then_inc(A["rsd"], 1)

                def add_x(n):
                    dve.wait_ge(A["wod"], A0["wod"] + n + 1)
                    nc.vector.tensor_tensor(xs(n), seqs(pE[:]), xs(n), ALU.add).then_inc(A["xud"], 1)

                def step(i, first, last):
                    for j in range(XB):
                        t = XB * i + j
                        if j == 1 and not first:
                            norm_in(l, i - 1)
                        if j == 3 and not first:
                            norm_out(l, i - 1)
                        if j == 0 and not last:
                            shift(i + 1, 0)
                        if not (last and j >= XB - 2):
                            v_copy(t + 2, (j + 2) % XB)
                        if not (last and j >= XB - 3):
                            lengths(t + 3)
                        if j == 0 and not first:
                            add_x(i - 1)
                        if not last:
                            rotate(t + 4, j)
                        if j == 1 and not first:
                            norm_center(l, i - 1)
                        if not (last and j == XB - 1):
                            inverse(t + 1, 0)
                        if not (last and j >= XB - 3):
                            log_sum(t + 3)
                        if not (last and j >= XB - 2):
                            scales(t + 2, j)
                        if not last and j < XB - 1:
                            shift(i + 1, j + 1)
                        if not (last and j >= XB - 2):
                            maxima(t + 2, j, 0)
                        if not (last and j == XB - 1):
                            inverse(t + 1, 1)
                        if not (last and j >= XB - 2):
                            maxima(t + 2, j, 1)

                for j in range(XB):
                    shift(0, j)
                rotate(0, 0)
                lengths(0)
                log_sum(0)
                rotate(1, 1)
                v_copy(0, 0)
                lengths(1)
                scales(0, 0)
                maxima(0, 0, 0)
                log_sum(1)
                maxima(0, 0, 1)
                rotate(2, 2)
                inverse(0, 0)
                scales(1, 1)
                v_copy(1, 1)
                lengths(2)
                inverse(0, 1)
                maxima(1, 1, 0)
                log_sum(2)
                maxima(1, 1, 1)
                rotate(3, 3)
                if l == 0:
                    dve.wait_ge(x0_saved, 1)
                pairs(dve, step)
                return lambda: add_x(PAIRS - 1)

            def last_norm(k):
                L, L0 = LNS, counted(LN_PER_STAGE, k)

                def add_in(n, q):
                    if not below(n, 2):
                        dve.wait_ge(L["lcent"], L0["lcent"] + n - 1)
                    nc.vector.tensor_tensor(seqs(lin_b[q][:]), xs(n), x0T[:, bass.ds(2 * n, 2), :], ALU.add).then_inc(L["lin"], 1)

                def center(n, q):
                    dve.wait_ge(L["lmean"], L0["lmean"] + n + 1)
                    if not below(n, 2):
                        dve.wait_ge(L["lnorm"], L0["lnorm"] + n - 1)
                        dve.wait_ge(L["lsq"], L0["lsq"] + n - 1)
                    nc.vector.tensor_tensor(lc_b[q][:], lin_b[q][:], pLm[:, q, :], ALU.subtract).then_inc(L["lcent"], 1)

                def normal(n, q):
                    dve.wait_ge(L["lrstd"], L0["lrstd"] + n + 1)
                    if not below(n, 2):
                        dve.wait_ge(L["ltp"], L0["ltp"] + n - 1)
                    nc.vector.tensor_tensor(foT[q][:], lc_b[q][:], lr_b[q][:], ALU.mult).then_inc(L["lnorm"], 1)

                add_in(0, 0)
                add_in(1, 1)
                center(0, 0)
                center(1, 1)
                add_in(2, 0)
                normal(0, 0)
                center(2, 0)
                add_in(3, 1)
                normal(1, 1)
                with dve.Fori(1, PAIRS // 2 - 1) as i:
                    center(2 * i + 1, 1)
                    add_in(2 * i + 2, 0)
                    normal(2 * i, 0)
                    center(2 * i + 2, 0)
                    add_in(2 * i + 3, 1)
                    normal(2 * i + 1, 1)
                center(PAIRS - 1, 1)
                normal(PAIRS - 2, 0)
                normal(PAIRS - 1, 1)

            def feed(l, attention_add):
                f, Q, Q0 = F[l], FF, counted(FF_PER_LAYER, l)
                def gated(i, c):
                    w = CW[c]
                    dve.wait_ge(Q["ge"], Q0["ge"] + NC * i + c + 1)
                    dve.wait_ge(Q["u"], Q0["u"] + NC * i + c + 1)
                    if not below(i, 1):
                        dve.wait_ge(Q["o"], Q0["o"] + NC * i + c - NC + 1)
                    nc.vector.scalar_tensor_tensor(out=mm_[0:w, c, :], in0=pU(w, c), scalar=f["b1"][0:w, c:c + 1],
                                                   in1=gl[0:w, c, :], op0=ALU.add, op1=ALU.mult).then_inc(Q["m"], 1)

                def add_x(n):
                    dve.wait_ge(Q["o"], Q0["o"] + NC * (n + 1))
                    nc.vector.scalar_tensor_tensor(out=xs(n), in0=seqs(pO[:]), scalar=f["b2"][:, 0:1], in1=xs(n),
                                                   op0=ALU.add, op1=ALU.add).then_inc(Q["x"], 1)

                def step(i, first):
                    gated(i, 0)
                    if not first:
                        add_x(i - 1)
                    gated(i, 1)
                    gated(i, 2)

                gated(0, 0)
                attention_add()
                dve.wait_ge(ATT["xud"], PAIRS * (l + 1))
                norm_in(l, PAIRS - 1)
                norm_center(l, PAIRS - 1)
                gated(0, 1)
                gated(0, 2)
                step(1, False)
                step(2, False)
                norm_out(l, PAIRS - 1)
                with dve.Fori(3, PAIRS) as i:
                    step(i, False)
                add_x(PAIRS - 1)

            for l in range(DEPTH):
                feed(l, attention(l))
                dve.wait_ge(FF["x"], PAIRS * (l + 1))
            last_norm(DEPTH)

        @block.gpsimd
        def _(pool):
            nc.gpsimd.memset(ones_mean[:], 1.0 / D)
            nc.gpsimd.memset(eps[:], EPS)
            nc.gpsimd.memset(one[:], 1.0)
            nc.gpsimd.memset(xT[:, :, 0:1], 0.0)
            nc.gpsimd.memset(ub[:, :, :, 0:3], 0.0)
            for k in range(NDA):
                mm = nc.gpsimd.memset(dA[k][:, :, :, :, 0:1].rearrange("p k h s t -> p (k h s) t"), 0.0)
            mm.then_inc(consts_p, 1)

            def hold():
                nc.gpsimd.tensor_tensor(held[:], one[:], one[:], ALU.mult)

            def split(n):
                pool.wait_ge(bc_f_done, n + 1)
                hold()
                nc.gpsimd.tensor_scalar(bc_t[:], bc_f[:], third[:, 0:1], 0.0, ALU.mult, ALU.add).then_inc(part, 1)
                pool.wait_ge(part, 3 * n + 1)
                nc.gpsimd.tensor_tensor(bc_r[:], bc_f[:], bc_t[:], ALU.subtract).then_inc(part, 1)
                pool.wait_ge(part, 3 * n + 2)
                hold()
                nc.gpsimd.tensor_scalar(bc_t[:], bc_r[:], third[:, 1:2], 0.0, ALU.mult, ALU.add).then_inc(part, 1)

            def split_end(n, k1):
                pool.wait_ge(part, 3 * n + 3)
                if k1 is not None:
                    pool.wait_ge(c_ready, k1)
                nc.gpsimd.tensor_tensor(bc_s[:], bc_r[:], bc_t[:], ALU.subtract).then_inc(bc_split, 1)

            def readout(n, g):
                k0 = NG * n
                wait_group(pool, c_ev, c_ev, n, g)
                pool.wait_ge(scan, k0 + g + 1)
                if not below(k0 + g, 2):
                    pool.wait_ge(ysum, k0 + g - 1)
                nc.gpsimd.tensor_tensor(hc[g % 2][:], hb[g % NHB][:], csb[:, g % 2, :, :].unsqueeze(2).to_broadcast([128, 2, NH, T]),
                                        ALU.mult).then_inc(hc_pool, 1)

            def step(i, first, last):
                for g in range(NG):
                    readout(i, g)
                    if g == NG - 3 and not last:
                        split(i + 1)
                    if g == NG - 2 and not last:
                        split_end(i + 1, NG * i + NG)

            pool.wait_ge(weights, LOADED)
            split(0)
            split_end(0, None)
            pairs(pool, step)
            pool.wait_ge(x_done, PAIRS)

            def attention(l):
                A, A0 = ATT, counted(ATT_PER_LAYER, l)

                def rotated(t, j):
                    pool.wait_ge(A["rot"], A0["rot"] + t + 1)
                    if not below(t, 2):
                        pool.wait_ge(A["tps"], A0["tps"] + t - 1)
                    nc.gpsimd.tensor_tensor(qk[j % 2][:], t1[j % 2][:], t2[j % 2][:], ALU.add).then_inc(A["addd"], 1)

                def unit_k(t, j):
                    pool.wait_ge(A["addd"], A0["addd"] + t + 1)
                    pool.wait_ge(A["rnd"], A0["rnd"] + t + 1)
                    kk = qk[j % 2][:, 1, :].rearrange("p (h d) -> p h d", d=HD)
                    nc.gpsimd.tensor_tensor(kk, kk, rn[j % 2][:, HEADS:2 * HEADS].unsqueeze(2).to_broadcast([128, HEADS, HD]),
                                            ALU.mult).then_inc(A["qkd"], 1)

                def normalise(t, j, par):
                    pool.wait_ge(A["rsd"], A0["rsd"] + 2 * t + par + 1)
                    hs = slice(HP * par, HP * par + HP)
                    nc.gpsimd.tensor_tensor(P[j % 2][:, hs], P[j % 2][:, hs], rs[:, hs].unsqueeze(2).to_broadcast([128, HP, 128]),
                                            ALU.mult).then_inc(A["pnorm"], 1)

                def step(i, first, last):
                    for j in range(XB):
                        t = XB * i + j
                        if not (last and j == XB - 1):
                            normalise(t + 1, j + 1, 0)
                            normalise(t + 1, j + 1, 1)
                        if not (last and j >= XB - 3):
                            unit_k(t + 3, j + 1)
                        if not last:
                            rotated(t + 4, j)

                for j in range(2):
                    rotated(j, j)
                    unit_k(j, j)
                rotated(2, 2)
                for par in range(2):
                    normalise(0, 0, par)
                unit_k(2, 2)
                rotated(3, 3)
                pairs(pool, step)

            for l in range(DEPTH):
                attention(l)


_INS = ['L0_attn_x', 'L0_attn_W1', 'L0_attn_b1', 'L0_attn_W2', 'L0_attn_b2', 'L0_attn_conv_w', 'L0_attn_conv_b',
        'L0_attn_A_log', 'L0_attn_x_proj_w', 'L0_attn_dt_proj_w', 'L0_attn_dt_proj_b', 'L0_attn_D_skip', 'L0_attn_Wo',
        'L0_attn_bo', 'L0_ffn_wqkv', 'L0_ffn_q_scale', 'L0_ffn_k_scale', 'L0_ffn_wo', 'L0_ffn_ln_g', 'L0_ffn_ln_b',
        'L0_ffn_w1', 'L0_ffn_b1', 'L0_ffn_w2', 'L0_ffn_b2']


_COLUMNS = {'L0_attn_b1', 'L0_attn_b2', 'L0_attn_dt_proj_b', 'L0_attn_conv_b', 'L0_attn_D_skip', 'L0_attn_bo'}

_LAYER_COLUMNS = {'L0_ffn_ln_g', 'L0_ffn_ln_b', 'L0_ffn_b2'}


def constants():
    bc, s, hd, window = 32, 256, 64, 64
    half = np.arange(0, hd, 2, dtype=np.float32)
    inv = (np.float32(1.0) / np.float32(10000.0) ** (half / np.float32(hd))).astype(np.float32)
    tok = np.arange(s, dtype=np.float32)
    freq = np.tile(tok[:, None] * inv[None, :], (1, 2))
    base = (half + np.float32(0.4 * hd)) / np.float32(1.4 * hd)
    power = (tok - s // 2) / np.float32(window // 2)
    scale = np.tile(base[None, :] ** power[:, None], (1, 2)).astype(np.float32)
    sign = np.where(np.arange(hd) < hd // 2, -1.0, 1.0).astype(np.float32)
    cos, sin = np.cos(freq), np.sin(freq) * sign
    rot_c = np.stack([cos * scale, cos / scale], 1).reshape(2, 128, 2, hd).transpose(1, 0, 2, 3)
    rot_s = np.stack([sin * scale, sin / scale], 1).reshape(2, 128, 2, hd).transpose(1, 0, 2, 3)
    r, c = np.arange(64)[:, None], np.arange(64)[None, :]
    own, before = np.where(c <= r, 0.0, -1e30), np.where(c >= r, 0.0, -1e30)
    none = np.full((64, 64), -1e30)
    mask = np.stack([np.block([[own, none], [before, own]]), np.block([[own, before], [before, own]])], 1)
    return {
        "c_ident": np.eye(128, dtype=np.float32),
        "c_third": np.repeat(np.array([[0, 0], [1, 0], [1, 1]], np.float32), bc, axis=0),
        "c_onehot": np.tile(np.eye(bc, dtype=np.float32), (3, 1)),
        "c_rot_c": np.ascontiguousarray(rot_c, np.float32), "c_rot_s": np.ascontiguousarray(rot_s, np.float32),
        "c_mask": np.ascontiguousarray(mask, np.float32),
    }


def kernel(**inputs):
    import concourse.bacc as bacc
    from concourse.bass_utils import run_bass_kernel_spmd

    nc = bacc.Bacc("TRN2", target_bir_lowering=False, num_devices=1)
    arrays, aps = {}, {}
    for name in _INS:
        value = np.asarray(inputs[name])
        if name in _COLUMNS:
            value = value.reshape(-1, 128).T
        if name in _LAYER_COLUMNS:
            value = value.reshape(value.shape[0], 128, 1)
        if name == 'L0_ffn_b1':
            hid = value.shape[1] // 2
            padded = np.zeros((value.shape[0], 2, 3 * 128), value.dtype)
            padded[:, :, :hid] = value.reshape(-1, 2, hid)
            value = padded.reshape(-1, 6, 128).transpose(0, 2, 1)
        arrays["in_" + name] = np.ascontiguousarray(value)
    for name, value in constants().items():
        arrays["in_" + name] = value
    for name, value in arrays.items():
        aps[name[3:]] = nc.dram_tensor(name, value.shape, mybir.dt.from_np(value.dtype), kind="ExternalInput").ap()
    shape = inputs["L0_attn_x"].shape
    out = nc.dram_tensor("out_0", shape, mybir.dt.float32, kind="ExternalOutput").ap()
    build(nc, aps, out)
    r = run_bass_kernel_spmd(nc, [arrays], core_ids=[0])
    return r.results[0]["out_0"]
```

```python
import numpy as np
import concourse.bass as bass
from concourse import mybir
from contextlib import ExitStack

F32 = mybir.dt.float32
BF16 = mybir.dt.bfloat16
ALU = mybir.AluOpType
ACT = mybir.ActivationFunctionType
AX = mybir.AxisListType


def below(v, k):
    return isinstance(v, int) and v < k


def build(nc, a, out):
    NSEQ, S, D = a["L0_attn_x"].shape
    CH = a["L0_attn_W1"].shape[1]
    NH = CH // 128
    NST = a["L0_attn_A_log"].shape[1]
    RANK = a["L0_attn_dt_proj_w"].shape[0]
    PAIRS = NSEQ // 2
    T = 2 * S
    NG = NST // 2
    XB = T // 128
    BC = 2 * NST
    EPS = 1e-5
    LEN_MIN = 1e-24
    DEPTH, HID = a["L0_ffn_w2"].shape[0:2]
    HD = a["L0_ffn_q_scale"].shape[1]
    INNER = a["L0_ffn_wo"].shape[1]
    HEADS = INNER // HD
    HP = HEADS // 2
    NC = -(-HID // 128)
    CW = [min(128, HID - 128 * c) for c in range(NC)]
    TILES = PAIRS * XB

    ctx = ExitStack()
    with ctx:
        def sb(name, shape, dt=F32):
            return ctx.enter_context(nc.sbuf_tensor(name, shape, dt))

        def ps(name, shape, dt=F32):
            return ctx.enter_context(nc.psum_tensor(name, shape, dt))

        def sem(name):
            return ctx.enter_context(nc.semaphore(name))

        ident = sb("ident", [128, 128])
        ones_mean = sb("ones_mean", [128, 128])
        onehot_src = sb("onehot_src", [3 * BC, BC])
        onehot = sb("onehot", [3 * BC, BC, 128], BF16)
        w1 = sb("w1", [128, CH])
        w2 = sb("w2", [128, CH])
        wx = sb("wx", [128, NH, RANK + BC])
        wbc3 = sb("wbc3", [128, NH, 3, BC])
        wdt = sb("wdt", [RANK, CH])
        wo = sb("wo", [128, NH, D])
        b1 = sb("b1", [128, NH])
        nb2 = sb("nb2", [128, NH])
        bdt = sb("bdt", [128, NH])
        cw = sb("cw", [128, NH, 4])
        cb = sb("cb", [128, NH])
        nA = sb("nA", [128, NH, NST])
        dsk = sb("dsk", [128, NH])
        bo = sb("bo", [128, 1])
        diagD = sb("diagD", [128, NH, 128])

        xT = sb("xT", [128, NSEQ, S + 1])
        eps = sb("eps", [128, 1])
        one = sb("one", [128, 1])
        held = sb("held", [128, 1])

        identb = sb("identb", [128, 128], BF16)
        maskf = sb("maskf", [128, 2, 128])
        maskb = sb("maskb", [128, 2, 4, 128], BF16)
        rot_c = sb("rot_c", [128, 2, 2, HD])
        rot_s = sb("rot_s", [128, 2, 2, HD])
        F = []
        for l in range(DEPTH):
            F.append(dict(
                wqkv=sb(f"wqkv{l}", [128, 3 * INNER]), wo=sb(f"wof{l}", [128, INNER // 128, D]),
                w1=sb(f"w1f{l}", [128, 2 * HID]), w2=sb(f"w2f{l}", [128, NC, D]),
                lg=sb(f"lg{l}", [128, 1]), lb=sb(f"lb{l}", [128, 1]), b1=sb(f"b1f{l}", [128, 2 * NC]),
                b2=sb(f"b2f{l}", [128, 1]), qk_scale=sb(f"qks{l}", [128, 2, HD]),
                tc=sb(f"tc{l}", [128, 2, 2, HD]), ts=sb(f"ts{l}", [128, 2, 2, HD])))

        mscope = ExitStack()

        def msb(name, shape, dt=F32):
            return mscope.enter_context(nc.sbuf_tensor(name, shape, dt))

        def mps(name, shape, dt=F32):
            return mscope.enter_context(nc.psum_tensor(name, shape, dt))

        xin = msb("xin", [128, XB, D])
        ub = msb("ub", [128, NH, 2, S + 3])
        uacc = msb("uacc", [128, NH, 2, S])
        u = msb("u", [128, NH, 2, S])
        xdt = msb("xdt", [RANK, T])
        bc_f = msb("bc_f", [3 * BC, T])
        bc_r = msb("bc_r", [3 * BC, T])
        bc_t = msb("bc_t", [3 * BC, T], BF16)
        third = msb("third", [3 * BC, 2])
        bc_s = msb("bc_s", [3 * BC, T], BF16)
        sp_m = msb("sp_m", [128, NH, T])
        sp_l = msb("sp_l", [128, NH, T])
        delta = msb("delta", [128, NH, 2, S])
        du = msb("du", [128, NH * T])
        gate = msb("gate", [128, NH, T])
        yg = msb("yg", [128, NH, T])
        NDA, NHB = 2, 4
        dA = [msb(f"dA{k}", [128, 2, NH, 2, S]) for k in range(NDA)]
        hb = [msb(f"hb{k}", [128, 2, NH, T]) for k in range(NHB)]
        hc = [msb(f"hc{k}", [128, 2, NH, T]) for k in range(2)]
        csb = msb("csb", [128, 2, 2, T])
        rb = msb("rb", [128, T])
        rc = msb("rc", [128, T])
        rsq = msb("rsq", [128, T])
        rstd = msb("rstd", [128, T])
        pB = mps("pB", [128, 2, T])
        pC = mps("pC", [128, 2, T])
        pY = mps("pY", [128, NH, T])
        pW = mps("pW", [128, 2, T])
        mscope.close()

        fscope = ExitStack()

        fsb = lambda name, shape: fscope.enter_context(nc.sbuf_tensor(name, shape, F32))

        def fps(scope, name, shape, dt=F32):
            return scope.enter_context(nc.psum_tensor(name, shape, dt))

        x0T = fsb("x0T", [128, NSEQ, S])
        hn = fsb("hn", [128, PAIRS, T])
        lin = fsb("lin", [128, T])
        lc = fsb("lc", [128, T])
        lsq = fsb("lsq", [128, T])
        lr = fsb("lr", [128, T])
        ascope = ExitStack()
        fsb = lambda name, shape: ascope.enter_context(nc.sbuf_tensor(name, shape, F32))
        hT = fsb("hT", [128, XB, 128])
        t1 = [fsb(f"t1_{k}", [128, 2, INNER]) for k in range(2)]
        t2 = [fsb(f"t2_{k}", [128, 2, INNER]) for k in range(2)]
        qk_sq = fsb("qk_sq", [128, 2, INNER])
        ss = fsb("ss", [128, 2 * HEADS])
        ssi = fsb("ssi", [128, 2 * HEADS])
        ssc = fsb("ssc", [128, 2, 2 * HEADS])
        lns = fsb("lns", [128, 2, 2 * HEADS])
        lsum = fsb("lsum", [128, 2 * HEADS])
        rn = [fsb(f"rn{k}", [128, 2 * HEADS]) for k in range(2)]
        qk = [fsb(f"qk{k}", [128, 2, INNER]) for k in range(2)]
        qkT = [fsb(f"qkT{k}", [128, 2, HP, 128]) for k in range(2)]
        V = [fsb(f"V{k}", [128, INNER]) for k in range(XB)]
        Vm = [fsb(f"Vm{k}", [128, INNER]) for k in range(XB)]
        mx = fsb("mx", [128, HEADS])
        sc8 = [fsb(f"sc8_{k}", [128, HEADS]) for k in range(2)]
        nb = [fsb(f"nb{k}", [128, HEADS]) for k in range(2)]
        psums = fsb("psums", [128, HEADS])
        rs = fsb("rs", [128, HEADS])
        P = [fsb(f"P{k}", [128, HEADS, 128]) for k in range(2)]
        PT = fsb("PT", [128, HEADS, 128])
        oT = fsb("oT", [128, HP, T])
        ascope.close()
        lscope = ExitStack()
        fsb = lambda name, shape: lscope.enter_context(nc.sbuf_tensor(name, shape, F32))
        gl = fsb("gl", [128, NC, T])
        hid = fsb("hid", [128, NC, T])
        lin_b = [fsb(f"lin_b{k}", [128, T]) for k in range(2)]
        lc_b = [fsb(f"lc_b{k}", [128, T]) for k in range(2)]
        lsq_b = [fsb(f"lsq_b{k}", [128, T]) for k in range(2)]
        lr_b = [fsb(f"lr_b{k}", [128, T]) for k in range(2)]
        foT = [fsb(f"foT{k}", [128, T]) for k in range(2)]
        fout = [fsb(f"fout{k}", [128, XB, D]) for k in range(2)]
        lscope.close()
        fscope.close()
        s1 = ExitStack()
        pA = fps(s1, "pA", [128, 2, INNER])
        pT = fps(s1, "pT", [128, 2, INNER])
        pS = fps(s1, "pS", [128, 2, HP, 128])
        pV = fps(s1, "pV", [128, INNER])
        pE = fps(s1, "pE", [128, T])
        s1.close()
        pGU = fps(s1, "pGU", [128, NC, 2, T])

        def pG(w, c):
            return pGU[0:w, (0, 2, 1)[c], 0, :]

        def pU(w, c):
            return pGU[0:w, (0, 2, 1)[c], 1, :]

        fps(s1, "of_pV", [128, T])
        pO = fps(s1, "pO", [128, T])
        s1.close()
        pLm = fps(s1, "pLm", [128, 2, T])
        pLv = fps(s1, "pLv", [128, 2, T])
        pLt = fps(s1, "pLt", [128, 2, T])
        s1.close()

        ffn_loaded = sem("ffn_loaded")
        tabs = sem("tabs")
        x0_saved = sem("x0_saved")
        ATT_PER_LAYER = {n: TILES for n in """
            h_shifted qk_made v_made rotation_parts squared squares_summed sum_clamped clamped_inverse
            length_factors factor_logs log_summed inverse_length qk_rotated k_unit qk_turned qkT_copied
            scale_ready p_turned pT_copied v_copied mixed o_copied""".split()}
        ATT_PER_LAYER |= {n: 2 * TILES for n in "scores maxima exp_bias exps sums_inverse p_normalised".split()}
        ATT_PER_LAYER |= {n: PAIRS for n in "projected x_updated".split()}
        LN_PER_STAGE = {n: PAIRS for n in "input mean centred squared variance log_variance rstd normalised".split()}
        LN_PER_STAGE |= {"turned": 0, "rows_copied": 0}
        FF_PER_LAYER = {n: NC * PAIRS for n in "gate_made other_made gelu hidden down_chunk".split()}
        FF_PER_LAYER |= {"x_updated": PAIRS}
        ATT = {n: sem("att_" + n) for n in ATT_PER_LAYER}
        LNS = {n: sem("ln_" + n) for n in LN_PER_STAGE}
        FF = {n: sem("ff_" + n) for n in FF_PER_LAYER}
        b1_ps = sem("b1_ps")
        b1_done = sem("b1_done")

        def counted(per, k):
            return {n: k * v for n, v in per.items()}
        a_exp = sem("a_exp")
        b_ready = sem("b_ready")
        bc_f_done = sem("bc_f_done")
        bc_ps = sem("bc_ps")
        bc_split = sem("bc_split")
        tapped = sem("tapped")
        part = sem("part")
        c_ev = sem("c_ev")
        c_ready = sem("c_ready")
        cent = sem("cent")
        consts_p = sem("consts_p")
        consts_v = sem("consts_v")
        da_ready = sem("da_ready")
        dbu = sem("dbu")
        delta_done = sem("delta_done")
        dt_ps = sem("dt_ps")
        du_done = sem("du_done")
        gate_done = sem("gate_done")
        gate_e = sem("gate_e")
        gate_l = sem("gate_l")
        gate_ps = sem("gate_ps")
        hc_done = sem("hc_done")
        mean_ps = sem("mean_ps")
        resid = sem("resid")
        rstd_done = sem("rstd_done")
        rstd_l = sem("rstd_l")
        scan = sem("scan")
        sig_e = sem("sig_e")
        sig_l = sem("sig_l")
        sp_a = sem("sp_a")
        sp_done = sem("sp_done")
        sp_e = sem("sp_e")
        sq = sem("sq")
        stored = [sem(f"stored{q}") for q in range(2)]
        u_b = sem("u_b")
        u_conv = sem("u_conv")
        u_ps = sem("u_ps")
        u_sig = sem("u_sig")
        var_ps = sem("var_ps")
        weights = sem("weights")
        first_loaded = sem("first_loaded")
        wo_ps = sem("wo_ps")
        x_done = sem("x_done")
        x_in = sem("x_in")
        x_t = sem("x_t")
        xdt_done = sem("xdt_done")
        xdt_ps = sem("xdt_ps")
        xt_ps = sem("xt_ps")
        y_init = sem("y_init")
        yg_done = sem("yg_done")
        ysum = sem("ysum")
        x_pairs = a["L0_attn_x"].rearrange("(i s) (b p) d -> i p (s b) d", s=2, p=128)
        first_list = [
            (xin[:], x_pairs[0]), (ident[:], a["c_ident"]), (w1[:], a["L0_attn_W1"]), (b1[:], a["L0_attn_b1"]),
            (cw[:], a["L0_attn_conv_w"].rearrange("(c p) k -> p c k", p=128)), (cb[:], a["L0_attn_conv_b"]),
        ]
        FIRST_LOADED = 16 * len(first_list)
        load_list = [
            (onehot_src[:], a["c_onehot"]), (third[:], a["c_third"]),
            (w2[:], a["L0_attn_W2"]),
            (wx[:], a["L0_attn_x_proj_w"].rearrange("(c p) n -> p c n", p=128)),
            (wdt[:], a["L0_attn_dt_proj_w"]),
            (wo[:], a["L0_attn_Wo"].rearrange("(c p) n -> p c n", p=128)),
            (nb2[:], a["L0_attn_b2"]),
            (bdt[:], a["L0_attn_dt_proj_b"]),
            (nA[:], a["L0_attn_A_log"].rearrange("(c p) k -> p c k", p=128)),
            (dsk[:], a["L0_attn_D_skip"]),
            (bo[:], a["L0_attn_bo"]),
        ]
        LOADED = 16 * len(load_list)
        ffn_list = [(maskf[:], a["c_mask"]), (rot_c[:], a["c_rot_c"]), (rot_s[:], a["c_rot_s"])]
        for l in range(DEPTH):
            f = F[l]
            ffn_list += [
                (f["wqkv"][:], a["L0_ffn_wqkv"][l]),
                (f["wo"][:], a["L0_ffn_wo"][l].rearrange("(c p) n -> p c n", p=128)),
                (f["w1"][:], a["L0_ffn_w1"][l]),
                (f["w2"][:, 0:NC - 1, :], a["L0_ffn_w2"][l, 0:128 * (NC - 1), :].rearrange("(c p) n -> p c n", p=128)),
                (f["w2"][0:CW[-1], NC - 1, :], a["L0_ffn_w2"][l, 128 * (NC - 1):HID, :]),
                (f["lg"][:], a["L0_ffn_ln_g"][l]), (f["lb"][:], a["L0_ffn_ln_b"][l]), (f["b2"][:], a["L0_ffn_b2"][l]),
                (f["b1"][:], a["L0_ffn_b1"][l]),
                (f["qk_scale"][:, 0, :], a["L0_ffn_q_scale"][l].partition_broadcast(128)),
                (f["qk_scale"][:, 1, :], a["L0_ffn_k_scale"][l].partition_broadcast(128)),
            ]
        FFN_LOADED = 16 * len(ffn_list)

        def wait_group(eng, sem_, i, g):
            if below(i, 1) and g < 0:
                return
            eng.wait_ge(sem_, NG * i + g + 1)

        def xs(i):
            return xT[:, bass.ds(2 * i, 2), 1:S + 1]

        def seqs(ap):
            return ap.rearrange("p (s t) -> p s t", s=2)

        block = ctx.enter_context(nc.Block())

        def pairs(eng, step):
            step(0, True, False)
            with eng.Fori(1, PAIRS - 1) as i:
                step(i, False, False)
            step(PAIRS - 1, False, True)

        def skewed(eng, stage):
            for n in range(3):
                stage(n, n % 2, n == 0, False)
            with eng.Fori(1, PAIRS // 2 - 1) as i:
                stage(2 * i + 1, 1, False, False)
                stage(2 * i + 2, 0, False, False)
            stage(PAIRS - 1, 1, False, True)

        @block.sync
        def _(sp):
            for dst, src in first_list:
                sp.dma_start(dst, src).then_inc(first_loaded, 16)
            for dst, src in load_list:
                sp.dma_start(dst, src).then_inc(weights, 16)
            for dst, src in ffn_list:
                sp.dma_start(dst, src).then_inc(ffn_loaded, 16)
            with sp.Fori(1, PAIRS) as i:
                sp.wait_ge(xt_ps, i)
                sp.dma_start(xin[:], x_pairs[i]).then_inc(x_in, 16)
            L, L0 = LNS, counted(LN_PER_STAGE, DEPTH)
            o_pairs = out.rearrange("(i s) (b p) d -> i p (s b) d", s=2, p=128)

            def store(n, q):
                sp.wait_ge(L["rows_copied"], L0["rows_copied"] + n + 1)
                sp.dma_start(o_pairs[n], fout[q][:]).then_inc(stored[q], 16)

            with sp.Fori(0, PAIRS // 2) as i:
                store(2 * i, 0)
                store(2 * i + 1, 1)
            for q in range(2):
                sp.wait_ge(stored[q], 16 * (PAIRS // 2))

        @block.tensor
        def _(pe):
            pe.wait_ge(first_loaded, FIRST_LOADED)
            pe.wait_ge(consts_p, 1)

            def transposes(n):
                if not below(n, 1):
                    pe.wait_ge(x_in, 16 * n)
                for b in range(XB):
                    mm = nc.tensor.transpose(pW[:, 0, 128 * b:128 * b + 128], xin[:, b, :], ident[:])
                mm.then_inc(xt_ps, 1)

            def u_rows(n):
                pe.wait_ge(x_t, n + 1)
                for h in range(NH):
                    mm = nc.tensor.matmul(pW[:, h, :], w1[:, 128 * h:128 * h + 128], xs(n), start=True, stop=True)
                mm.then_inc(u_ps, 1)

            def out_rows(n):
                pe.wait_ge(yg_done, n + 1)
                for h in range(NH):
                    mm = nc.tensor.matmul(pW[:, 0, :], wo[:, h, :], yg[:, h, :], start=(h == 0), stop=(h == NH - 1))
                mm.then_inc(wo_ps, 1)

            def bc_rows(n):
                pe.wait_ge(u_sig, n + 1)
                for h in range(NH):
                    mm = nc.tensor.matmul(pW[0:3 * BC, 0, :], wbc3[:, h, :, :].rearrange("p k n -> p (k n)"),
                                          u[:, h, :, :].rearrange("p s t -> p (s t)"), start=(h == 0), stop=(h == NH - 1))
                mm.then_inc(bc_ps, 1)

            def xdt_rows(n):
                pe.wait_ge(u_sig, n + 1)
                for h in range(NH):
                    mm = nc.tensor.matmul(pW[0:RANK, 1, :], wx[:, h, 0:RANK],
                                          u[:, h, :, :].rearrange("p s t -> p (s t)"), start=(h == 0), stop=(h == NH - 1))
                mm.then_inc(xdt_ps, 1)

            def dt_rows(n):
                pe.wait_ge(xdt_done, n + 1)
                for h in range(NH):
                    mm = nc.tensor.matmul(pW[:, h, :], wdt[:, 128 * h:128 * h + 128], xdt[:], start=True, stop=True)
                mm.then_inc(dt_ps, 1)

            def gate_rows(n):
                for h in range(NH):
                    mm = nc.tensor.matmul(pW[:, h, :], w2[:, 128 * h:128 * h + 128], xs(n), start=True, stop=True)
                mm.then_inc(gate_ps, 1)

            def b_rows(n, g, i0):
                if g == 0:
                    pe.wait_ge(bc_split, n + 1)
                if not below(i0 + g, 1):
                    pe.wait_ge(dbu, i0 + g)
                for k in range(2):
                    mm = nc.tensor.matmul(pB[:, k, :], onehot[:, 2 * g + k, :], bc_s[:], start=True, stop=True)
                mm.then_inc(b_ready, 1)
                wait_group(pe, c_ev, n, g - 1)
                for k in range(2):
                    mm = nc.tensor.matmul(pC[:, k, :], onehot[:, NST + 2 * g + k, :], bc_s[:], start=True, stop=True)
                mm.then_inc(c_ready, 1)

            def sum_states(i, g):
                wait_group(pe, hc_done, i, g)
                for k in range(2):
                    for h in range(NH):
                        mm = nc.tensor.matmul(pY[:, h, :], ident[:], hc[g % 2][:, k, h, :], start=False,
                                              stop=(g == NG - 1 and k == 1), skip_group_check=True)
                mm.then_inc(ysum, 1)

            def variance_rows(n):
                pe.wait_ge(sq, n + 1)
                nc.tensor.matmul(pW[:, 1, :], ones_mean[:], rsq[:], start=True, stop=True).then_inc(var_ps, 1)

            def mean_rows(n):
                pe.wait_ge(resid, n + 1)
                nc.tensor.matmul(pW[:, 0, :], ones_mean[:], rb[:], start=True, stop=True).then_inc(mean_ps, 1)

            def step(i, first, last):
                for g in range(NG):
                    if g < NG - 1:
                        b_rows(i, g + 1, NG * i)
                    if g == 5 and not last:
                        pe.wait_ge(bc_f_done, i + 2)
                        dt_rows(i + 1)
                    if g == 0 and not last:
                        if first:
                            pe.wait_ge(sp_a, 1)
                        else:
                            pe.wait_ge(gate_e, i)
                        transposes(i + 1)
                    if g == 1 and not last:
                        u_rows(i + 1)
                    if g == 2 and not first:
                        if not last:
                            pe.wait_ge(u_b, i + 2)
                        else:
                            pe.wait_ge(gate_e, i)
                        out_rows(i - 1)
                    if g == 3:
                        if not first:
                            mean_rows(i - 1)
                    if g == 4 and not last:
                        xdt_rows(i + 1)
                        if not first:
                            pe.wait_ge(cent, i)
                        bc_rows(i + 1)
                    if g == 6:
                        if not last:
                            pe.wait_ge(sp_a, i + 2)
                        if not first:
                            variance_rows(i - 1)
                    if g == 7:
                        if not first:
                            pe.wait_ge(rstd_done, i)
                        gate_rows(i)
                        if not last:
                            b_rows(i + 1, 0, NG * (i + 1))
                    if g == 0 and not first:
                        sum_states(i - 1, NG - 1)
                    if g == 1:
                        if not first:
                            pe.wait_ge(yg_done, i)
                        else:
                            pe.wait_ge(b1_done, 1)
                        for h in range(NH):
                            mm = nc.tensor.matmul(pY[:, h, :], diagD[:, h, :], u[:, h, :, :].rearrange("p s t -> p (s t)"),
                                                  start=True, stop=False, skip_group_check=True)
                        mm.then_inc(y_init, 1)
                    if g > 0:
                        sum_states(i, g - 1)

            transposes(0)
            u_rows(0)
            pe.wait_ge(weights, LOADED)
            pe.wait_ge(consts_v, 1)
            pe.wait_ge(u_b, 1)
            xdt_rows(0)
            bc_rows(0)
            pe.wait_ge(bc_f_done, 1)
            dt_rows(0)
            pe.wait_ge(ffn_loaded, FFN_LOADED)
            for l in range(DEPTH):
                for c in range(2 * NC):
                    w = CW[c % NC]
                    c0 = 128 * (c % NC) + HID * (c // NC)
                    k = 2 * NC * l + c
                    mm = nc.tensor.matmul(pY[0:w, 0, k:k + 1], F[l]["w1"][:, c0:c0 + w], F[l]["lb"][:], start=True, stop=True)
            mm.then_inc(b1_ps, 1)
            b_rows(0, 0, 0)
            pairs(pe, step)
            sum_states(PAIRS - 1, NG - 1)
            pe.wait_ge(gate_e, PAIRS)
            out_rows(PAIRS - 1)
            mean_rows(PAIRS - 1)
            variance_rows(PAIRS - 1)
            pe.wait_ge(x_done, PAIRS)
            pe.wait_ge(ffn_loaded, FFN_LOADED)
            pe.wait_ge(tabs, 1)

            def up(l, i, c):
                f, Q, Q0 = F[l], FF, counted(FF_PER_LAYER, l)
                w = CW[c]
                rows = hn[:, bass.ds(i, 1), :].rearrange("p o t -> p (o t)")
                pe.wait_ge(LNS["normalised"], PAIRS * l + i + 1)
                if not below(i, 1):
                    pe.wait_ge(Q["gelu"], Q0["gelu"] + NC * i + c - NC + 1)
                nc.tensor.matmul(pG(w, c), f["w1"][:, HID + 128 * c:HID + 128 * c + w], rows, start=True,
                                 stop=True).then_inc(Q["gate_made"], 1)
                if not below(i, 1):
                    pe.wait_ge(Q["hidden"], Q0["hidden"] + NC * i + c - NC + 1)
                nc.tensor.matmul(pU(w, c), f["w1"][:, 128 * c:128 * c + w], rows, start=True,
                                 stop=True).then_inc(Q["other_made"], 1)

            def mean(l, n, vs):
                A, A0, L, L0 = ATT, counted(ATT_PER_LAYER, l), LNS, counted(LN_PER_STAGE, l)
                pe.wait_ge(L["input"], L0["input"] + n + 1)
                pe.wait_ge(A["v_copied"], A0["v_copied"] + vs)
                nc.tensor.matmul(pV[:], ones_mean[:], lin[:], start=True, stop=True).then_inc(L["mean"], 1)

            def variance(l, n, vs):
                A, A0, L, L0 = ATT, counted(ATT_PER_LAYER, l), LNS, counted(LN_PER_STAGE, l)
                pe.wait_ge(L["squared"], L0["squared"] + n + 1)
                pe.wait_ge(A["v_copied"], A0["v_copied"] + vs)
                nc.tensor.matmul(pV[:], ones_mean[:], lsq[:], start=True, stop=True).then_inc(L["variance"], 1)

            def attention(l):
                A, A0, f = ATT, counted(ATT_PER_LAYER, l), F[l]
                L, L0 = LNS, counted(LN_PER_STAGE, l)

                def qk_rows(t, j):
                    pe.wait_ge(A["h_shifted"], A0["h_shifted"] + t + 1)
                    if not below(t, 1):
                        pe.wait_ge(A["squared"], A0["squared"] + t)
                    for c in range(2):
                        mm = nc.tensor.matmul(pA[:, c, :], hT[:, j, :], f["wqkv"][:, INNER * c:INNER * (c + 1)],
                                              start=True, stop=True)
                    mm.then_inc(A["qk_made"], 1)

                def v_rows(t, j):
                    if not below(t, 1):
                        pe.wait_ge(A["v_copied"], A0["v_copied"] + t)
                    nc.tensor.matmul(pV[:], hT[:, j, :], f["wqkv"][:, 2 * INNER:3 * INNER],
                                     start=True, stop=True).then_inc(A["v_made"], 1)

                def turn_qk(t, j):
                    pe.wait_ge(A["k_unit"], A0["k_unit"] + t + 1)
                    if not below(t, 2):
                        pe.wait_ge(A["pT_copied"], A0["pT_copied"] + t - 1)
                    elif not below(t, 1):
                        pe.wait_ge(A["qkT_copied"], A0["qkT_copied"] + t)
                    for c in range(2):
                        for hp in range(HP):
                            mm = nc.tensor.transpose(pT[:, c, 128 * hp:128 * hp + 128],
                                                     qk[j % 2][:, c, 128 * hp:128 * hp + 128], ident[:])
                    mm.then_inc(A["qk_turned"], 1)

                def sims(t, j, par):
                    if par == 0:
                        pe.wait_ge(A["qkT_copied"], A0["qkT_copied"] + t + 1)
                    pos = j % 2
                    cur, prev = qkT[j % 2], qkT[(j + 1) % 2]
                    if not below(t, 1):
                        pe.wait_ge(A["exps"], A0["exps"] + 2 * t - 1 + par)
                    nc.tensor.matmul(pS[:, par, :, :].rearrange("p h k -> p (h k)"), identb[:],
                                     maskb[:, pos, :, :].rearrange("p h k -> p (h k)"), start=True, stop=False,
                                     skip_group_check=True)
                    for hp in range(HP):
                        r = slice(64 * par, 64 * par + 64)
                        nc.tensor.matmul(pS[0:64, par, hp, 0:64], cur[r, 0, hp, 0:64], cur[r, 1, hp, 0:64],
                                         start=False, stop=True, skip_group_check=True)
                        if pos:
                            nc.tensor.matmul(pS[0:64, par, hp, 64:128], cur[r, 0, hp, 0:64], prev[r, 1, hp, 64:128],
                                             start=False, stop=True, skip_group_check=True)
                        mm = nc.tensor.matmul(pS[64:128, par, hp, :], cur[r, 0, hp, 64:128], cur[r, 1, hp, :],
                                              start=False, stop=True, skip_group_check=True)
                    mm.then_inc(A["scores"], 1)

                def turn_p(t, j):
                    for par in range(2):
                        pe.wait_ge(A["p_normalised"], A0["p_normalised"] + 2 * t + par + 1)
                        for hp in range(HP):
                            mm = nc.tensor.transpose(pT[:, par, 128 * hp:128 * hp + 128], P[j % 2][:, par * HP + hp, :], ident[:])
                    mm.then_inc(A["p_turned"], 1)

                def mix(t, j):
                    pos = j % 2
                    pe.wait_ge(A["pT_copied"], A0["pT_copied"] + t + 1)
                    pe.wait_ge(A["v_copied"], A0["v_copied"] + t + 1)
                    if not below(t, 1):
                        pe.wait_ge(A["o_copied"], A0["o_copied"] + t)
                    for hp in range(HP):
                        for par in range(2):
                            dims = slice(HD * (2 * hp + par), HD * (2 * hp + par + 1))
                            o = pE[64 * par:64 * par + 64, 128 * hp:128 * hp + 128]
                            nc.tensor.matmul(o[:, 64:128], V[j][:, dims], PT[:, par * HP + hp, 64:128], start=True, stop=True)
                            r = slice(0, 128 if pos else 64)
                            mm = nc.tensor.matmul(o[:, 0:64], (Vm if pos else V)[j][r, dims], PT[r, par * HP + hp, 0:64],
                                                  start=True, stop=True)
                    mm.then_inc(A["mixed"], 1)

                def project(i):
                    pe.wait_ge(A["o_copied"], A0["o_copied"] + XB * (i + 1))
                    for c in range(HP):
                        mm = nc.tensor.matmul(pE[:], f["wo"][:, c, :], oT[:, c, :], start=(c == 0), stop=(c == HP - 1))
                    mm.then_inc(A["projected"], 1)

                def step(i, first, last):
                    for j in range(XB):
                        t = XB * i + j
                        if last and j == XB - 1:
                            up(l, 0, 0)
                            pe.wait_ge(A["exps"], A0["exps"] + 2 * TILES)
                            up(l, 0, 1)
                        turn_p(t, j)
                        if j == 0 and not first:
                            project(i - 1)
                        if not last:
                            qk_rows(t + 4, j)
                        if not (last and j >= XB - 2):
                            turn_qk(t + 2, (j + 2) % XB)
                        if j == 1 and not first:
                            mean(l, i - 1, t + 3)
                        if j == 2 and not first:
                            variance(l, i - 1, TILES if last else t + 3)
                        if j == 0 and not first:
                            pe.wait_ge(A["x_updated"], A0["x_updated"] + i)
                        mix(t, j)
                        if not (last and j >= XB - 2):
                            sims(t + 2, (j + 2) % XB, 0)
                        if not first and not last:
                            if j == 1:
                                pe.wait_ge(L["centred"], L0["centred"] + i)
                            if j == 2:
                                pe.wait_ge(L["log_variance"], L0["log_variance"] + i)
                        if not (last and j >= XB - 3):
                            v_rows(t + 3, (j + 3) % XB)
                        if not (last and j >= XB - 2):
                            sims(t + 2, (j + 2) % XB, 1)

                qk_rows(0, 0)
                v_rows(0, 0)
                qk_rows(1, 1)
                turn_qk(0, 0)
                sims(0, 0, 0)
                sims(0, 0, 1)
                qk_rows(2, 2)
                v_rows(1, 1)
                turn_qk(1, 1)
                sims(1, 1, 0)
                v_rows(2, 2)
                sims(1, 1, 1)
                qk_rows(3, 3)
                pairs(pe, step)
                project(PAIRS - 1)
                up(l, 0, 2)
                mean(l, PAIRS - 1, TILES)

            def last_norm(k):
                L, L0 = LNS, counted(LN_PER_STAGE, k)

                def mean(n, q):
                    pe.wait_ge(L["input"], L0["input"] + n + 1)
                    if not below(n, 2):
                        pe.wait_ge(L["centred"], L0["centred"] + n - 1)
                    nc.tensor.matmul(pLm[:, q, :], ones_mean[:], lin_b[q][:], start=True, stop=True
                        ).then_inc(L["mean"], 1)

                def variance(n, q):
                    pe.wait_ge(L["squared"], L0["squared"] + n + 1)
                    if not below(n, 2):
                        pe.wait_ge(L["log_variance"], L0["log_variance"] + n - 1)
                    nc.tensor.matmul(pLv[:, q, :], ones_mean[:], lsq_b[q][:], start=True, stop=True
                        ).then_inc(L["variance"], 1)

                def turn(n, q):
                    pe.wait_ge(L["normalised"], L0["normalised"] + n + 1)
                    if not below(n, 2):
                        pe.wait_ge(L["rows_copied"], L0["rows_copied"] + n - 1)
                    for b in range(XB):
                        mm = nc.tensor.transpose(pLt[:, q, 128 * b:128 * b + 128], foT[q][:, 128 * b:128 * b + 128], ident[:])
                    mm.then_inc(L["turned"], 1)

                def stage(n, q, first, last):
                    if not last:
                        mean(n + 1, 1 - q)
                    variance(n, q)
                    if not first:
                        turn(n - 1, 1 - q)

                mean(0, 0)
                skewed(pe, stage)
                turn(PAIRS - 1, 1)

            def feed(l):
                f, Q, Q0 = F[l], FF, counted(FF_PER_LAYER, l)

                def down(i, c):
                    w = CW[c]
                    pe.wait_ge(Q["hidden"], Q0["hidden"] + NC * i + c + 1)
                    if c == 0 and not below(i, 1):
                        pe.wait_ge(Q["x_updated"], Q0["x_updated"] + i)
                    nc.tensor.matmul(pO[:], f["w2"][0:w, c, :], hid[0:w, c, :], start=(c == 0), stop=(c == NC - 1)
                        ).then_inc(Q["down_chunk"], 1)

                def step(i):
                    up(l, i, 0)
                    down(i - 1, NC - 1)
                    up(l, i, 1)
                    down(i, 0)
                    if below(i, 2):
                        variance(l, PAIRS - 1, TILES)
                    up(l, i, 2)
                    down(i, 1)

                down(0, 0)
                down(0, 1)
                step(1)
                with pe.Fori(2, PAIRS) as i:
                    step(i)
                down(PAIRS - 1, NC - 1)

            for l in range(DEPTH):
                attention(l)
                feed(l)
                pe.wait_ge(FF["x_updated"], PAIRS * (l + 1))
            last_norm(DEPTH)

        @block.scalar
        def _(act):
            nc.scalar.preload_act_table_set("natural_log_exp_and_others")
            act.wait_ge(consts_p, 1)
            act.wait_ge(first_loaded, FIRST_LOADED)

            def x_copy(n):
                act.wait_ge(xt_ps, n + 1)
                nc.scalar.copy(xs(n), seqs(pW[:, 0, :])).then_inc(x_t, 1)

            def u_bias(n, first):
                act.wait_ge(u_ps, n + 1)
                if not first:
                    act.wait_ge(u_conv, n)
                for h in range(NH):
                    mm = nc.scalar.activation(ub[:, h, :, 3:S + 3], seqs(pW[:, h, :]), ACT.Identity, bias=b1[:, h:h + 1])
                mm.then_inc(u_b, 1)

            def newest_tap(n):
                act.wait_ge(u_b, n + 1)
                if not below(n, 1):
                    act.wait_ge(u_sig, n)
                for h in range(NH):
                    mm = nc.scalar.activation(uacc[:, h, :, :], ub[:, h, :, 3:S + 3], ACT.Identity, scale=cw[:, h, 3:4],
                                              bias=cb[:, h:h + 1])
                mm.then_inc(tapped, 1)

            def u_sigmoid(n, first):
                act.wait_ge(u_conv, n + 1)
                nc.scalar.activation(uacc[:], uacc[:], ACT.Exp, scale=-1.0).then_inc(sig_e, 1)
                act.wait_ge(sig_e, n + 1)
                nc.scalar.activation(uacc[:], uacc[:], ACT.Ln, bias=one[:]).then_inc(sig_l, 1)
                if not first:
                    act.wait_ge(y_init, n)
                    act.wait_ge(du_done, n)
                act.wait_ge(sig_l, n + 1)
                nc.scalar.activation(u[:], uacc[:], ACT.Exp, scale=-1.0).then_inc(u_sig, 1)

            def bc_copy(n, first):
                act.wait_ge(bc_ps, n + 1)
                if not first:
                    act.wait_ge(bc_split, n)
                nc.scalar.copy(bc_f[:], pW[0:3 * BC, 0, :]).then_inc(bc_f_done, 1)

            def xdt_copy(n):
                act.wait_ge(xdt_ps, n + 1)
                nc.scalar.copy(xdt[:], pW[0:RANK, 1, :]).then_inc(xdt_done, 1)

            def softplus(n, first):
                act.wait_ge(dt_ps, n + 1)
                if not first:
                    act.wait_ge(delta_done, n)
                for h in range(NH):
                    nc.scalar.activation(sp_m[:, h, :], pW[:, h, :], ACT.Relu, bias=bdt[:, h:h + 1])
                for h in range(NH):
                    mm = nc.scalar.activation(sp_l[:, h, :], pW[:, h, :], ACT.Abs, bias=bdt[:, h:h + 1])
                mm.then_inc(sp_a, 1)
                act.wait_ge(sp_a, n + 1)
                nc.scalar.activation(sp_l[:], sp_l[:], ACT.Exp, scale=-1.0).then_inc(sp_e, 1)
                act.wait_ge(sp_e, n + 1)
                nc.scalar.activation(sp_l[:], sp_l[:], ACT.Ln, bias=one[:]).then_inc(sp_done, 1)

            def gates(n, first):
                act.wait_ge(gate_ps, n + 1)
                if not first:
                    act.wait_ge(yg_done, n)
                for h in range(NH):
                    mm = nc.scalar.activation(gate[:, h, :], pW[:, h, :], ACT.Exp, scale=-1.0, bias=nb2[:, h:h + 1])
                mm.then_inc(gate_e, 1)
                act.wait_ge(gate_e, n + 1)
                nc.scalar.activation(gate[:], gate[:], ACT.Ln, bias=one[:]).then_inc(gate_l, 1)
                act.wait_ge(gate_l, n + 1)
                nc.scalar.activation(gate[:], gate[:], ACT.Exp, scale=-1.0).then_inc(gate_done, 1)

            def decay(n, g, k0):
                if g == 0:
                    act.wait_ge(delta_done, n + 1)
                if not below(k0 + g, NDA):
                    act.wait_ge(scan, k0 + g - NDA + 1)
                for k in range(2):
                    for h in range(NH):
                        mm = nc.scalar.activation(dA[g % NDA][:, k, h, :, 1:S], delta[:, h, :, 1:S], ACT.Exp,
                                                  scale=nA[:, h, 2 * g + k:2 * g + k + 1])
                mm.then_inc(da_ready, 1)

            def c_copy(n, g):
                act.wait_ge(c_ready, NG * n + g + 1)
                wait_group(act, hc_done, n, g - 2)
                nc.scalar.copy(csb[:, g % 2, :, :], pC[:]).then_inc(c_ev, 1)

            def square(n):
                act.wait_ge(cent, n + 1)
                if not below(n, 1):
                    act.wait_ge(var_ps, n)
                nc.scalar.activation(rsq[:], rc[:], ACT.Square).then_inc(sq, 1)

            def rsqrt(n):
                act.wait_ge(var_ps, n + 1)
                if not below(n, 1):
                    act.wait_ge(x_done, n)
                nc.scalar.activation(rstd[:], pW[:, 1, :], ACT.Ln, bias=eps[:]).then_inc(rstd_l, 1)
                act.wait_ge(rstd_l, n + 1)
                nc.scalar.activation(rstd[:], rstd[:], ACT.Exp, scale=-0.5).then_inc(rstd_done, 1)

            def step(i, first, last):
                for g in range(NG):
                    if g == 0 and not last:
                        x_copy(i + 1)
                    if g < NG - 1:
                        c_copy(i, g + 1)
                    if g == 1 and not last:
                        u_bias(i + 1, False)
                        newest_tap(i + 1)
                    if g == 3 and not last:
                        u_sigmoid(i + 1, False)
                    if g + 2 < NG:
                        decay(i, g + 2, NG * i)
                    if g == 5 and not last:
                        softplus(i + 1, False)
                    if g == 4 and not last:
                        xdt_copy(i + 1)
                        bc_copy(i + 1, False)
                    if g == 4 and not first:
                        square(i - 1)
                    if g == 6 and not first:
                        rsqrt(i - 1)
                    if g == 7:
                        if not last:
                            decay(i + 1, 0, NG * (i + 1))
                            c_copy(i + 1, 0)
                        gates(i, first)
                        if not last:
                            decay(i + 1, 1, NG * (i + 1))

            x_copy(0)
            u_bias(0, True)
            newest_tap(0)
            act.wait_ge(weights, LOADED)
            nc.scalar.activation(nA[:], nA[:], ACT.Exp).then_inc(a_exp, 1)
            u_sigmoid(0, True)
            act.wait_ge(consts_v, 1)
            xdt_copy(0)
            bc_copy(0, True)
            softplus(0, True)
            decay(0, 0, 0)
            c_copy(0, 0)
            decay(0, 1, 0)
            pairs(act, step)
            square(PAIRS - 1)
            rsqrt(PAIRS - 1)

            act.wait_ge(x_done, PAIRS)
            act.wait_ge(ffn_loaded, FFN_LOADED)
            nc.scalar.copy(x0T[:], xT[:, :, 1:S + 1]).then_inc(x0_saved, 1)

            def norm_square(l, n):
                L, L0 = LNS, counted(LN_PER_STAGE, l)
                act.wait_ge(L["centred"], L0["centred"] + n + 1)
                nc.scalar.activation(lsq[:], lc[:], ACT.Square).then_inc(L["squared"], 1)

            def norm_ln(l, n):
                L, L0 = LNS, counted(LN_PER_STAGE, l)
                act.wait_ge(L["variance"], L0["variance"] + n + 1)
                if not below(n, 1):
                    act.wait_ge(L["normalised"], L0["normalised"] + n)
                nc.scalar.activation(lr[:], pV[:], ACT.Ln, bias=eps[:]).then_inc(L["log_variance"], 1)

            def norm_exp(l, n):
                L, L0 = LNS, counted(LN_PER_STAGE, l)
                act.wait_ge(L["log_variance"], L0["log_variance"] + n + 1)
                nc.scalar.activation(lr[:], lr[:], ACT.Exp, scale=-0.5).then_inc(L["rstd"], 1)

            def attention(l):
                A, A0 = ATT, counted(ATT_PER_LAYER, l)
                L, L0 = LNS, counted(LN_PER_STAGE, l)

                def square(t):
                    act.wait_ge(A["rotation_parts"], A0["rotation_parts"] + t + 1)
                    if not below(t, 1):
                        act.wait_ge(A["squares_summed"], A0["squares_summed"] + t)
                    nc.scalar.activation(qk_sq[:], pA[:], ACT.Square).then_inc(A["squared"], 1)

                def lengths_ln(t):
                    act.wait_ge(A["length_factors"], A0["length_factors"] + t + 1)
                    if not below(t, 1):
                        act.wait_ge(A["log_summed"], A0["log_summed"] + t)
                    nc.scalar.activation(lns[:], ssc[:], ACT.Ln).then_inc(A["factor_logs"], 1)

                def lengths_exp(t, j):
                    act.wait_ge(A["log_summed"], A0["log_summed"] + t + 1)
                    if not below(t, 2):
                        act.wait_ge(A["scale_ready"], A0["scale_ready"] + t - 1)
                        act.wait_ge(A["k_unit"], A0["k_unit"] + t - 1)
                    nc.scalar.activation(rn[j % 2][:], lsum[:], ACT.Exp, scale=-0.5).then_inc(A["inverse_length"], 1)

                def qk_copy(t, j):
                    act.wait_ge(A["qk_turned"], A0["qk_turned"] + t + 1)
                    nc.scalar.copy(qkT[j % 2][:].rearrange("p c h k -> p (c h k)"), pT[:].rearrange("p c n -> p (c n)")
                        ).then_inc(A["qkT_copied"], 1)

                def p_copy(t):
                    act.wait_ge(A["p_turned"], A0["p_turned"] + t + 1)
                    nc.scalar.copy(PT[:].rearrange("p h k -> p (h k)"), pT[:].rearrange("p c n -> p (c n)")
                        ).then_inc(A["pT_copied"], 1)

                def exps(t, j, par):
                    act.wait_ge(A["exp_bias"], A0["exp_bias"] + 2 * t + par + 1)
                    if not below(t, 1):
                        act.wait_ge(A["sums_inverse"], A0["sums_inverse"] + 2 * t - 1 + par)
                    for hp in range(HP):
                        h = par * HP + hp
                        mm = nc.scalar.activation(P[j % 2][:, h, :], pS[:, par, hp, :], ACT.Exp, scale=sc8[j % 2][:, h:h + 1],
                                                  bias=nb[j % 2][:, h:h + 1], accum_out=psums[:, h:h + 1])
                    mm.then_inc(A["exps"], 1)

                def o_copy(t, j):
                    act.wait_ge(A["mixed"], A0["mixed"] + t + 1)
                    nc.scalar.copy(oT[:, :, 128 * j:128 * j + 128], pE[:].rearrange("p (h q) -> p h q", h=HP)
                        ).then_inc(A["o_copied"], 1)

                def step(i, first, last):
                    for j in range(XB):
                        t = XB * i + j
                        p_copy(t)
                        if not (last and j == XB - 1):
                            exps(t + 1, j + 1, 0)
                        if not (last and j >= XB - 2):
                            qk_copy(t + 2, j)
                        if not (last and j >= XB - 3):
                            lengths_ln(t + 3)
                        if j == 2 and not first:
                            norm_ln(l, i - 1)
                        if not (last and j == XB - 1):
                            exps(t + 1, j + 1, 1)
                        if not last:
                            square(t + 4)
                        o_copy(t, j)
                        if not (last and j >= XB - 3):
                            lengths_exp(t + 3, j + 3)
                        if j == 1 and not first:
                            norm_square(l, i - 1)
                        if j == 2 and not first:
                            norm_exp(l, i - 1)

                square(0)
                lengths_ln(0)
                lengths_exp(0, 0)
                square(1)
                qk_copy(0, 0)
                lengths_ln(1)
                exps(0, 0, 0)
                lengths_exp(1, 1)
                exps(0, 0, 1)
                qk_copy(1, 1)
                square(2)
                lengths_ln(2)
                lengths_exp(2, 2)
                square(3)
                pairs(act, step)

            def last_norm(k):
                L, L0 = LNS, counted(LN_PER_STAGE, k)

                def square(n, q):
                    act.wait_ge(L["centred"], L0["centred"] + n + 1)
                    if not below(n, 2):
                        act.wait_ge(L["variance"], L0["variance"] + n - 1)
                    nc.scalar.activation(lsq_b[q][:], lc_b[q][:], ACT.Square).then_inc(L["squared"], 1)

                def rsqrt(n, q):
                    act.wait_ge(L["variance"], L0["variance"] + n + 1)
                    if not below(n, 2):
                        act.wait_ge(L["normalised"], L0["normalised"] + n - 1)
                    nc.scalar.activation(lr_b[q][:], pLv[:, q, :], ACT.Ln, bias=eps[:]).then_inc(L["log_variance"], 1)
                    act.wait_ge(L["log_variance"], L0["log_variance"] + n + 1)
                    nc.scalar.activation(lr_b[q][:], lr_b[q][:], ACT.Exp, scale=-0.5).then_inc(L["rstd"], 1)

                def rows_copy(n, q, reused):
                    act.wait_ge(L["turned"], L0["turned"] + n + 1)
                    if reused is not None:
                        act.wait_ge(stored[q], 16 * reused)
                    nc.scalar.copy(fout[q][:].rearrange("p b d -> p (b d)"), pLt[:, q, :]).then_inc(L["rows_copied"], 1)

                square(0, 0)
                square(1, 1)
                rsqrt(0, 0)
                square(2, 0)
                rsqrt(1, 1)
                rows_copy(0, 0, None)
                square(3, 1)
                rsqrt(2, 0)
                rows_copy(1, 1, None)
                with act.Fori(1, PAIRS // 2 - 1) as i:
                    square(2 * i + 2, 0)
                    rsqrt(2 * i + 1, 1)
                    rows_copy(2 * i, 0, i)
                    square(2 * i + 3, 1)
                    rsqrt(2 * i + 2, 0)
                    rows_copy(2 * i + 1, 1, i)
                rsqrt(PAIRS - 1, 1)
                rows_copy(PAIRS - 2, 0, PAIRS // 2 - 1)
                rows_copy(PAIRS - 1, 1, PAIRS // 2 - 1)

            def feed(l):
                f, Q, Q0 = F[l], FF, counted(FF_PER_LAYER, l)
                act.wait_ge(b1_done, 1)

                def step(i, first):
                    for c in range(NC):
                        w = CW[c]
                        act.wait_ge(Q["gate_made"], Q0["gate_made"] + NC * i + c + 1)
                        if not first:
                            act.wait_ge(Q["hidden"], Q0["hidden"] + NC * i + c - NC + 1)
                        nc.scalar.activation(gl[0:w, c, :], pG(w, c), ACT.Gelu,
                                             bias=f["b1"][0:w, NC + c:NC + c + 1]).then_inc(Q["gelu"], 1)

                nc.scalar.preload_act_table_set("gelu_and_others")
                step(0, True)
                norm_square(l, PAIRS - 1)
                step(1, False)
                nc.scalar.preload_act_table_set("natural_log_exp_and_others")
                norm_ln(l, PAIRS - 1)
                norm_exp(l, PAIRS - 1)
                nc.scalar.preload_act_table_set("gelu_and_others")
                with act.Fori(2, PAIRS) as i:
                    step(i, False)

            for l in range(DEPTH):
                attention(l)
                feed(l)
                nc.scalar.preload_act_table_set("natural_log_exp_and_others")
                act.wait_ge(FF["x_updated"], PAIRS * (l + 1))
            last_norm(DEPTH)

        @block.vector
        def _(dve):
            def conv(n, first):
                for k in range(3):
                    dve.wait_ge(tapped, 3 * n + k + 1)
                    for h in range(NH):
                        mm = nc.vector.scalar_tensor_tensor(out=uacc[:, h, :, :], in0=ub[:, h, :, k:k + S],
                                                            scalar=cw[:, h, k:k + 1], in1=uacc[:, h, :, :],
                                                            op0=ALU.mult, op1=ALU.add)
                    mm.then_inc(tapped if k < 2 else u_conv, 1)

            def inject(n, g, k0):
                dve.wait_ge(b_ready, k0 + g + 1)
                if g == 0:
                    dve.wait_ge(du_done, n + 1)
                wait_group(dve, hc_done, n, g - NHB)
                nc.vector.tensor_tensor(hb[g % NHB][:], du[:].rearrange("p (h t) -> p h t", h=NH).unsqueeze(1).to_broadcast([128, 2, NH, T]),
                                        pB[:].unsqueeze(2).to_broadcast([128, 2, NH, T]), ALU.mult).then_inc(dbu, 1)

            def recur(g, k0):
                dve.wait_ge(dbu, k0 + g + 1)
                dve.wait_ge(da_ready, k0 + g + 1)
                flat = hb[g % NHB][:].rearrange("p k h t -> p (k h t)")
                nc.vector.tensor_tensor_scan(flat, dA[g % NDA][:].rearrange("p k h s t -> p (k h s t)"), flat, 0.0,
                                             ALU.mult, ALU.add).then_inc(scan, 1)

            def y_gate(n, k1):
                dve.wait_ge(ysum, k1)
                dve.wait_ge(gate_done, n + 1)
                if not below(n, 1):
                    dve.wait_ge(wo_ps, n)
                nc.vector.tensor_tensor(yg[:], pY[:], gate[:], ALU.mult).then_inc(yg_done, 1)

            def residual(n):
                dve.wait_ge(wo_ps, n + 1)
                nc.vector.scalar_tensor_tensor(out=seqs(rb[:]), in0=seqs(pW[:, 0, :]), scalar=bo[:, 0:1], in1=xs(n),
                                               op0=ALU.add, op1=ALU.add).then_inc(resid, 1)

            def center(n):
                dve.wait_ge(mean_ps, n + 1)
                nc.vector.tensor_tensor(rc[:], rb[:], pW[:, 0, :], ALU.subtract).then_inc(cent, 1)

            def normal(n):
                dve.wait_ge(rstd_done, n + 1)
                nc.vector.tensor_tensor(xs(n), seqs(rc[:]), seqs(rstd[:]), ALU.mult).then_inc(x_done, 1)

            def delta_add(n, k1):
                dve.wait_ge(sp_done, n + 1)
                if k1 is not None:
                    dve.wait_ge(da_ready, k1)
                nc.vector.tensor_tensor(delta[:].rearrange("p h s t -> p (h s t)"), sp_m[:].rearrange("p h t -> p (h t)"),
                                        sp_l[:].rearrange("p h t -> p (h t)"), ALU.add).then_inc(delta_done, 1)

            def du_mul(n):
                dve.wait_ge(delta_done, n + 1)
                nc.vector.tensor_tensor(du[:], delta[:].rearrange("p h s t -> p (h s t)"),
                                        u[:].rearrange("p h s t -> p (h s t)"), ALU.mult).then_inc(du_done, 1)

            def step(i, first, last):
                for g in range(NG):
                    inject(i, g, NG * i)
                    if g == NG - 1 and not last:
                        delta_add(i + 1, NG * i + NG)
                    recur(g, NG * i)
                    if g == NG - 1 and not last:
                        du_mul(i + 1)
                    if g == 2 and not last:
                        conv(i + 1, False)
                    if not first:
                        if g == 1:
                            y_gate(i - 1, NG * i)
                        if g == 2:
                            residual(i - 1)
                        if g == 3:
                            center(i - 1)
                        if g == 7:
                            normal(i - 1)

            dve.wait_ge(first_loaded, FIRST_LOADED)
            dve.wait_ge(consts_p, 1)
            conv(0, True)
            dve.wait_ge(weights, LOADED)
            nc.vector.tensor_copy(onehot[:], onehot_src[:].unsqueeze(2).to_broadcast([3 * BC, BC, 128]))
            for k in range(3):
                nc.vector.tensor_copy(wbc3[:, :, k, :], wx[:, :, RANK:RANK + BC])
            for h in range(NH):
                nc.vector.tensor_scalar(diagD[:, h, :], ident[:], dsk[:, h:h + 1], None, ALU.mult)
            nc.vector.tensor_scalar(nb2[:], nb2[:], -1.0, None, ALU.mult)
            dve.wait_ge(a_exp, 1)
            nc.vector.tensor_scalar(nA[:], nA[:], -1.0, None, ALU.mult).then_inc(consts_v, 1)
            dve.wait_ge(ffn_loaded, FFN_LOADED)
            nc.vector.tensor_copy(identb[:], ident[:])
            nc.vector.tensor_copy(maskb[:], maskf[:].unsqueeze(2).to_broadcast([128, 2, 4, 128]))
            for l in range(DEPTH):
                f = F[l]
                for pos in range(2):
                    nc.vector.tensor_tensor(f["tc"][:, pos], rot_c[:, pos], f["qk_scale"][:], ALU.mult)
                    for r in range(2):
                        mm = nc.vector.tensor_tensor(f["ts"][:, pos, :, 32 * r:32 * r + 32], rot_s[:, pos, :, 32 * r:32 * r + 32],
                                                     f["qk_scale"][:, :, 32 - 32 * r:64 - 32 * r], ALU.mult)
            mm.then_inc(tabs, 1)
            delta_add(0, None)
            du_mul(0)
            dve.wait_ge(b1_ps, 1)
            for l in range(DEPTH):
                b = F[l]["b1"]
                for c in (0, NC):
                    k, e = 2 * NC * l + c, c + NC - 1
                    nc.vector.tensor_tensor(b[:, c:e], b[:, c:e], pY[:, 0, k:k + NC - 1], ALU.add)
                    mm = nc.vector.tensor_tensor(b[0:CW[-1], e:e + 1], b[0:CW[-1], e:e + 1],
                                                 pY[0:CW[-1], 0, k + NC - 1:k + NC], ALU.add)
            mm.then_inc(b1_done, 1)
            pairs(dve, step)
            y_gate(PAIRS - 1, NG * PAIRS)
            residual(PAIRS - 1)
            center(PAIRS - 1)
            normal(PAIRS - 1)
            dve.wait_ge(x_done, PAIRS)
            dve.wait_ge(tabs, 1)

            def norm_in(l, n):
                L = LNS
                nc.vector.tensor_copy(seqs(lin[:])[0:64], xs(n)[0:64])
                nc.vector.tensor_copy(seqs(lin[:])[64:128], xT[64:128, bass.ds(2 * n, 2), 0:S]).then_inc(L["input"], 1)

            def norm_center(l, n):
                L, L0 = LNS, counted(LN_PER_STAGE, l)
                dve.wait_ge(L["mean"], L0["mean"] + n + 1)
                nc.vector.tensor_tensor(lc[:], lin[:], pV[:], ALU.subtract).then_inc(L["centred"], 1)

            def norm_out(l, n):
                L, L0 = LNS, counted(LN_PER_STAGE, l)
                dve.wait_ge(L["rstd"], L0["rstd"] + n + 1)
                nc.vector.scalar_tensor_tensor(out=hn[:, bass.ds(n, 1), :].rearrange("p o t -> p (o t)"), in0=lc[:],
                                               scalar=F[l]["lg"][:, 0:1], in1=lr[:], op0=ALU.mult, op1=ALU.mult
                                               ).then_inc(L["normalised"], 1)

            def attention(l):
                A, A0, f = ATT, counted(ATT_PER_LAYER, l), F[l]
                L, L0 = LNS, counted(LN_PER_STAGE, l)

                def shift(n, j):
                    t, pos = XB * n + j, j % 2
                    if not below(t, XB):
                        dve.wait_ge(A["v_made"], A0["v_made"] + t - XB + 1)
                    seq = bass.ds(2 * n + j // 2, 1)
                    nc.vector.tensor_copy(hT[0:64, j, :], xT[0:64, seq, 1 + 128 * pos:129 + 128 * pos].rearrange("p o t -> p (o t)"))
                    nc.vector.tensor_copy(hT[64:128, j, :], xT[64:128, seq, 128 * pos:128 + 128 * pos].rearrange("p o t -> p (o t)")
                        ).then_inc(A["h_shifted"], 1)

                def rotate(t, j):
                    pos = j % 2
                    dve.wait_ge(A["qk_made"], A0["qk_made"] + t + 1)
                    if not below(t, 2):
                        dve.wait_ge(A["qk_rotated"], A0["qk_rotated"] + t - 1)
                    v4 = lambda x: x[:].rearrange("p c (h d) -> p c h d", d=HD)
                    nc.vector.tensor_tensor(v4(t1[j % 2]), v4(pA), f["tc"][:, pos].unsqueeze(2).to_broadcast([128, 2, HEADS, HD]), ALU.mult)
                    for r in range(2):
                        o, n_ = 32 * r, 32 - 32 * r
                        mm = nc.vector.tensor_tensor(v4(t2[j % 2])[:, :, :, o:o + 32], v4(pA)[:, :, :, n_:n_ + 32],
                                                     f["ts"][:, pos, :, o:o + 32].unsqueeze(2).to_broadcast([128, 2, HEADS, 32]), ALU.mult)
                    mm.then_inc(A["rotation_parts"], 1)

                def lengths(t):
                    dve.wait_ge(A["squared"], A0["squared"] + t + 1)
                    nc.vector.tensor_reduce(ss[:], qk_sq[:].rearrange("p c (h d) -> p (c h) d", d=HD), AX.X, ALU.add
                        ).then_inc(A["squares_summed"], 1)
                    dve.wait_ge(A["squares_summed"], A0["squares_summed"] + t + 1)
                    if not below(t, 1):
                        dve.wait_ge(A["factor_logs"], A0["factor_logs"] + t)
                    nc.vector.tensor_scalar(ssc[:, 0, :], ss[:], 2.0 ** -60, 2.0 ** 60, ALU.max, ALU.min
                        ).then_inc(A["sum_clamped"], 1)
                    dve.wait_ge(A["sum_clamped"], A0["sum_clamped"] + t + 1)
                    nc.vector.reciprocal(ssi[:], ssc[:, 0, :]).then_inc(A["clamped_inverse"], 1)
                    dve.wait_ge(A["clamped_inverse"], A0["clamped_inverse"] + t + 1)
                    nc.vector.scalar_tensor_tensor(out=ssc[:, 1, :], in0=ss[:], scalar=LEN_MIN, in1=ssi[:],
                                                   op0=ALU.max, op1=ALU.mult).then_inc(A["length_factors"], 1)

                def log_sum(t):
                    dve.wait_ge(A["factor_logs"], A0["factor_logs"] + t + 1)
                    if not below(t, 1):
                        dve.wait_ge(A["inverse_length"], A0["inverse_length"] + t)
                    nc.vector.tensor_tensor(lsum[:], lns[:, 0, :], lns[:, 1, :], ALU.add).then_inc(A["log_summed"], 1)

                def scales(t, j):
                    dve.wait_ge(A["inverse_length"], A0["inverse_length"] + t + 1)
                    nc.vector.tensor_scalar(sc8[j % 2][:].rearrange("p (c h) -> p c h", c=2),
                                            rn[j % 2][:, 0:HEADS].rearrange("p (h c) -> p c h", c=2), 8.0, None, ALU.mult
                                                ).then_inc(A["scale_ready"], 1)

                def maxima(t, j, par):
                    dve.wait_ge(A["scores"], A0["scores"] + 2 * t + par + 1)
                    hs = slice(HP * par, HP * par + HP)
                    nc.vector.tensor_reduce(mx[:, hs], pS[:, par, :, :], AX.X, ALU.max).then_inc(A["maxima"], 1)
                    dve.wait_ge(A["maxima"], A0["maxima"] + 2 * t + par + 1)
                    dve.wait_ge(A["scale_ready"], A0["scale_ready"] + t + 1)
                    nc.vector.scalar_tensor_tensor(out=nb[j % 2][:, hs], in0=mx[:, hs], scalar=-1.0, in1=sc8[j % 2][:, hs],
                                                   op0=ALU.mult, op1=ALU.mult).then_inc(A["exp_bias"], 1)

                def v_copy(t, j):
                    dve.wait_ge(A["v_made"], A0["v_made"] + t + 1)
                    nc.vector.tensor_copy(V[j][:], pV[:])
                    if j % 2:
                        mm = nc.vector.tensor_copy(Vm[j][0:64, :], pV[0:64, :])
                    else:
                        mm = nc.vector.tensor_copy(Vm[j + 1][64:128, :], pV[64:128, :])
                    mm.then_inc(A["v_copied"], 1)

                def inverse(t, par):
                    dve.wait_ge(A["exps"], A0["exps"] + 2 * t + par + 1)
                    if not below(t, 1):
                        dve.wait_ge(A["p_normalised"], A0["p_normalised"] + 2 * t - 1 + par)
                    hs = slice(HP * par, HP * par + HP)
                    nc.vector.reciprocal(rs[:, hs], psums[:, hs]).then_inc(A["sums_inverse"], 1)

                def add_x(n):
                    dve.wait_ge(A["projected"], A0["projected"] + n + 1)
                    nc.vector.tensor_tensor(xs(n), seqs(pE[:]), xs(n), ALU.add).then_inc(A["x_updated"], 1)

                def step(i, first, last):
                    for j in range(XB):
                        t = XB * i + j
                        if j == 1 and not first:
                            norm_in(l, i - 1)
                        if j == 3 and not first:
                            norm_out(l, i - 1)
                        if j == 0 and not last:
                            shift(i + 1, 0)
                        if not (last and j >= XB - 2):
                            v_copy(t + 2, (j + 2) % XB)
                        if not (last and j >= XB - 3):
                            lengths(t + 3)
                        if j == 0 and not first:
                            add_x(i - 1)
                        if not last:
                            rotate(t + 4, j)
                        if j == 1 and not first:
                            norm_center(l, i - 1)
                        if not (last and j == XB - 1):
                            inverse(t + 1, 0)
                        if not (last and j >= XB - 3):
                            log_sum(t + 3)
                        if not (last and j >= XB - 2):
                            scales(t + 2, j)
                        if not last and j < XB - 1:
                            shift(i + 1, j + 1)
                        if not (last and j >= XB - 2):
                            maxima(t + 2, j, 0)
                        if not (last and j == XB - 1):
                            inverse(t + 1, 1)
                        if not (last and j >= XB - 2):
                            maxima(t + 2, j, 1)

                for j in range(XB):
                    shift(0, j)
                rotate(0, 0)
                lengths(0)
                log_sum(0)
                rotate(1, 1)
                v_copy(0, 0)
                lengths(1)
                scales(0, 0)
                maxima(0, 0, 0)
                log_sum(1)
                maxima(0, 0, 1)
                rotate(2, 2)
                inverse(0, 0)
                scales(1, 1)
                v_copy(1, 1)
                lengths(2)
                inverse(0, 1)
                maxima(1, 1, 0)
                log_sum(2)
                maxima(1, 1, 1)
                rotate(3, 3)
                if l == 0:
                    dve.wait_ge(x0_saved, 1)
                pairs(dve, step)
                return lambda: add_x(PAIRS - 1)

            def last_norm(k):
                L, L0 = LNS, counted(LN_PER_STAGE, k)

                def add_in(n, q):
                    if not below(n, 2):
                        dve.wait_ge(L["centred"], L0["centred"] + n - 1)
                    nc.vector.tensor_tensor(seqs(lin_b[q][:]), xs(n), x0T[:, bass.ds(2 * n, 2), :], ALU.add
                        ).then_inc(L["input"], 1)

                def center(n, q):
                    dve.wait_ge(L["mean"], L0["mean"] + n + 1)
                    if not below(n, 2):
                        dve.wait_ge(L["normalised"], L0["normalised"] + n - 1)
                        dve.wait_ge(L["squared"], L0["squared"] + n - 1)
                    nc.vector.tensor_tensor(lc_b[q][:], lin_b[q][:], pLm[:, q, :], ALU.subtract
                        ).then_inc(L["centred"], 1)

                def normal(n, q):
                    dve.wait_ge(L["rstd"], L0["rstd"] + n + 1)
                    if not below(n, 2):
                        dve.wait_ge(L["turned"], L0["turned"] + n - 1)
                    nc.vector.tensor_tensor(foT[q][:], lc_b[q][:], lr_b[q][:], ALU.mult).then_inc(L["normalised"], 1)

                add_in(0, 0)
                add_in(1, 1)
                center(0, 0)
                center(1, 1)
                add_in(2, 0)
                normal(0, 0)
                center(2, 0)
                add_in(3, 1)
                normal(1, 1)
                with dve.Fori(1, PAIRS // 2 - 1) as i:
                    center(2 * i + 1, 1)
                    add_in(2 * i + 2, 0)
                    normal(2 * i, 0)
                    center(2 * i + 2, 0)
                    add_in(2 * i + 3, 1)
                    normal(2 * i + 1, 1)
                center(PAIRS - 1, 1)
                normal(PAIRS - 2, 0)
                normal(PAIRS - 1, 1)

            def feed(l, attention_add):
                f, Q, Q0 = F[l], FF, counted(FF_PER_LAYER, l)

                def gated(i, c):
                    w = CW[c]
                    dve.wait_ge(Q["gelu"], Q0["gelu"] + NC * i + c + 1)
                    dve.wait_ge(Q["other_made"], Q0["other_made"] + NC * i + c + 1)
                    if not below(i, 1):
                        dve.wait_ge(Q["down_chunk"], Q0["down_chunk"] + NC * i + c - NC + 1)
                    nc.vector.scalar_tensor_tensor(out=hid[0:w, c, :], in0=pU(w, c), scalar=f["b1"][0:w, c:c + 1],
                                                   in1=gl[0:w, c, :], op0=ALU.add, op1=ALU.mult
                                                       ).then_inc(Q["hidden"], 1)

                def add_x(n):
                    dve.wait_ge(Q["down_chunk"], Q0["down_chunk"] + NC * (n + 1))
                    nc.vector.scalar_tensor_tensor(out=xs(n), in0=seqs(pO[:]), scalar=f["b2"][:, 0:1], in1=xs(n),
                                                   op0=ALU.add, op1=ALU.add).then_inc(Q["x_updated"], 1)

                def step(i, first):
                    gated(i, 0)
                    if not first:
                        add_x(i - 1)
                    gated(i, 1)
                    gated(i, 2)

                gated(0, 0)
                attention_add()
                dve.wait_ge(ATT["x_updated"], PAIRS * (l + 1))
                norm_in(l, PAIRS - 1)
                norm_center(l, PAIRS - 1)
                gated(0, 1)
                gated(0, 2)
                step(1, False)
                step(2, False)
                norm_out(l, PAIRS - 1)
                with dve.Fori(3, PAIRS) as i:
                    step(i, False)
                add_x(PAIRS - 1)

            for l in range(DEPTH):
                feed(l, attention(l))
                dve.wait_ge(FF["x_updated"], PAIRS * (l + 1))
            last_norm(DEPTH)

        @block.gpsimd
        def _(pool):
            nc.gpsimd.memset(ones_mean[:], 1.0 / D)
            nc.gpsimd.memset(eps[:], EPS)
            nc.gpsimd.memset(one[:], 1.0)
            nc.gpsimd.memset(xT[:, :, 0:1], 0.0)
            nc.gpsimd.memset(ub[:, :, :, 0:3], 0.0)
            for k in range(NDA):
                mm = nc.gpsimd.memset(dA[k][:, :, :, :, 0:1].rearrange("p k h s t -> p (k h s) t"), 0.0)
            mm.then_inc(consts_p, 1)

            def hold():
                nc.gpsimd.tensor_tensor(held[:], one[:], one[:], ALU.mult)

            def split(n):
                pool.wait_ge(bc_f_done, n + 1)
                hold()
                nc.gpsimd.tensor_scalar(bc_t[:], bc_f[:], third[:, 0:1], 0.0, ALU.mult, ALU.add).then_inc(part, 1)
                pool.wait_ge(part, 3 * n + 1)
                nc.gpsimd.tensor_tensor(bc_r[:], bc_f[:], bc_t[:], ALU.subtract).then_inc(part, 1)
                pool.wait_ge(part, 3 * n + 2)
                hold()
                nc.gpsimd.tensor_scalar(bc_t[:], bc_r[:], third[:, 1:2], 0.0, ALU.mult, ALU.add).then_inc(part, 1)

            def split_end(n, k1):
                pool.wait_ge(part, 3 * n + 3)
                if k1 is not None:
                    pool.wait_ge(c_ready, k1)
                nc.gpsimd.tensor_tensor(bc_s[:], bc_r[:], bc_t[:], ALU.subtract).then_inc(bc_split, 1)

            def readout(n, g):
                k0 = NG * n
                wait_group(pool, c_ev, n, g)
                pool.wait_ge(scan, k0 + g + 1)
                if not below(k0 + g, 2):
                    pool.wait_ge(ysum, k0 + g - 1)
                nc.gpsimd.tensor_tensor(hc[g % 2][:], hb[g % NHB][:], csb[:, g % 2, :, :].unsqueeze(2).to_broadcast([128, 2, NH, T]),
                                        ALU.mult).then_inc(hc_done, 1)

            def step(i, first, last):
                for g in range(NG):
                    readout(i, g)
                    if g == NG - 3 and not last:
                        split(i + 1)
                    if g == NG - 2 and not last:
                        split_end(i + 1, NG * i + NG)

            pool.wait_ge(weights, LOADED)
            split(0)
            split_end(0, None)
            pairs(pool, step)
            pool.wait_ge(x_done, PAIRS)

            def attention(l):
                A, A0 = ATT, counted(ATT_PER_LAYER, l)

                def rotated(t, j):
                    pool.wait_ge(A["rotation_parts"], A0["rotation_parts"] + t + 1)
                    if not below(t, 2):
                        pool.wait_ge(A["qk_turned"], A0["qk_turned"] + t - 1)
                    nc.gpsimd.tensor_tensor(qk[j % 2][:], t1[j % 2][:], t2[j % 2][:], ALU.add
                        ).then_inc(A["qk_rotated"], 1)

                def unit_k(t, j):
                    pool.wait_ge(A["qk_rotated"], A0["qk_rotated"] + t + 1)
                    pool.wait_ge(A["inverse_length"], A0["inverse_length"] + t + 1)
                    kk = qk[j % 2][:, 1, :].rearrange("p (h d) -> p h d", d=HD)
                    nc.gpsimd.tensor_tensor(kk, kk, rn[j % 2][:, HEADS:2 * HEADS].unsqueeze(2).to_broadcast([128, HEADS, HD]),
                                            ALU.mult).then_inc(A["k_unit"], 1)

                def normalise(t, j, par):
                    pool.wait_ge(A["sums_inverse"], A0["sums_inverse"] + 2 * t + par + 1)
                    hs = slice(HP * par, HP * par + HP)
                    nc.gpsimd.tensor_tensor(P[j % 2][:, hs], P[j % 2][:, hs], rs[:, hs].unsqueeze(2).to_broadcast([128, HP, 128]),
                                            ALU.mult).then_inc(A["p_normalised"], 1)

                def step(i, first, last):
                    for j in range(XB):
                        t = XB * i + j
                        if not (last and j == XB - 1):
                            normalise(t + 1, j + 1, 0)
                            normalise(t + 1, j + 1, 1)
                        if not (last and j >= XB - 3):
                            unit_k(t + 3, j + 1)
                        if not last:
                            rotated(t + 4, j)

                for j in range(2):
                    rotated(j, j)
                    unit_k(j, j)
                rotated(2, 2)
                for par in range(2):
                    normalise(0, 0, par)
                unit_k(2, 2)
                rotated(3, 3)
                pairs(pool, step)

            for l in range(DEPTH):
                attention(l)


_INS = ['L0_attn_x', 'L0_attn_W1', 'L0_attn_b1', 'L0_attn_W2', 'L0_attn_b2', 'L0_attn_conv_w', 'L0_attn_conv_b',
        'L0_attn_A_log', 'L0_attn_x_proj_w', 'L0_attn_dt_proj_w', 'L0_attn_dt_proj_b', 'L0_attn_D_skip', 'L0_attn_Wo',
        'L0_attn_bo', 'L0_ffn_wqkv', 'L0_ffn_q_scale', 'L0_ffn_k_scale', 'L0_ffn_wo', 'L0_ffn_ln_g', 'L0_ffn_ln_b',
        'L0_ffn_w1', 'L0_ffn_b1', 'L0_ffn_w2', 'L0_ffn_b2']


_COLUMNS = {'L0_attn_b1', 'L0_attn_b2', 'L0_attn_dt_proj_b', 'L0_attn_conv_b', 'L0_attn_D_skip', 'L0_attn_bo'}

_LAYER_COLUMNS = {'L0_ffn_ln_g', 'L0_ffn_ln_b', 'L0_ffn_b2'}


def constants():
    bc, s, hd, window = 32, 256, 64, 64
    half = np.arange(0, hd, 2, dtype=np.float32)
    inv = (np.float32(1.0) / np.float32(10000.0) ** (half / np.float32(hd))).astype(np.float32)
    tok = np.arange(s, dtype=np.float32)
    freq = np.tile(tok[:, None] * inv[None, :], (1, 2))
    base = (half + np.float32(0.4 * hd)) / np.float32(1.4 * hd)
    power = (tok - s // 2) / np.float32(window // 2)
    scale = np.tile(base[None, :] ** power[:, None], (1, 2)).astype(np.float32)
    sign = np.where(np.arange(hd) < hd // 2, -1.0, 1.0).astype(np.float32)
    cos, sin = np.cos(freq), np.sin(freq) * sign
    rot_c = np.stack([cos * scale, cos / scale], 1).reshape(2, 128, 2, hd).transpose(1, 0, 2, 3)
    rot_s = np.stack([sin * scale, sin / scale], 1).reshape(2, 128, 2, hd).transpose(1, 0, 2, 3)
    r, c = np.arange(64)[:, None], np.arange(64)[None, :]
    own, before = np.where(c <= r, 0.0, -1e30), np.where(c >= r, 0.0, -1e30)
    none = np.full((64, 64), -1e30)
    mask = np.stack([np.block([[own, none], [before, own]]), np.block([[own, before], [before, own]])], 1)
    return {
        "c_ident": np.eye(128, dtype=np.float32),
        "c_third": np.repeat(np.array([[0, 0], [1, 0], [1, 1]], np.float32), bc, axis=0),
        "c_onehot": np.tile(np.eye(bc, dtype=np.float32), (3, 1)),
        "c_rot_c": np.ascontiguousarray(rot_c, np.float32), "c_rot_s": np.ascontiguousarray(rot_s, np.float32),
        "c_mask": np.ascontiguousarray(mask, np.float32),
    }


def kernel(**inputs):
    import concourse.bacc as bacc
    from concourse.bass_utils import run_bass_kernel_spmd

    nc = bacc.Bacc("TRN2", target_bir_lowering=False, num_devices=1)
    arrays, aps = {}, {}
    for name in _INS:
        value = np.asarray(inputs[name])
        if name in _COLUMNS:
            value = value.reshape(-1, 128).T
        if name in _LAYER_COLUMNS:
            value = value.reshape(value.shape[0], 128, 1)
        if name == 'L0_ffn_b1':
            hid = value.shape[1] // 2
            padded = np.zeros((value.shape[0], 2, 3 * 128), value.dtype)
            padded[:, :, :hid] = value.reshape(-1, 2, hid)
            value = padded.reshape(-1, 6, 128).transpose(0, 2, 1)
        arrays["in_" + name] = np.ascontiguousarray(value)
    for name, value in constants().items():
        arrays["in_" + name] = value
    for name, value in arrays.items():
        aps[name[3:]] = nc.dram_tensor(name, value.shape, mybir.dt.from_np(value.dtype), kind="ExternalInput").ap()
    shape = inputs["L0_attn_x"].shape
    out = nc.dram_tensor("out_0", shape, mybir.dt.float32, kind="ExternalOutput").ap()
    build(nc, aps, out)
    r = run_bass_kernel_spmd(nc, [arrays], core_ids=[0])
    return r.results[0]["out_0"]
```
